# Optimizing a Trainium2 kernel written in Bass

```python
import numpy as np
import jax
import jax.numpy as jnp

def _softmax(x, axis=-1):
    return jax.nn.softmax(x, axis=axis)

def _gelu(x):
    return jax.nn.gelu(x, approximate=True)

def _silu(x):
    return jax.nn.silu(x)

def _sigmoid(x):
    return jax.nn.sigmoid(x)

def _layernorm(x, axis=-1, eps=1e-05):
    m = jnp.mean(x, axis=axis, keepdims=True)
    v = jnp.var(x, axis=axis, keepdims=True)
    return (x - m) / jnp.sqrt(v + eps)

def _scatter_add(tgt, idx, src, axis=0):
    return tgt.at[idx].add(src)

def _segment_sum(src, seg, n):
    return jax.ops.segment_sum(src, seg, n)
kernel_name = 'mk_decoder_postln_d1_seqx_r8_0737e7'

def setup_inputs(seed: int=0):
    np.random.seed(seed)
    _w = jnp.asarray

    def _rec_inputs():
        import jax
        import jax.numpy as jnp
        _rk = jax.random.key(seed)
        x = 0.002226 + 0.9996 * jax.random.normal(jax.random.fold_in(_rk, 1), (128, 64, 128), jnp.float32)
        _lenS = 64 - jax.random.randint(jax.random.fold_in(_rk, 7), (128,), 0, max(1, 64 // 4) + 1, jnp.int32)
        _lenS2 = 64 - jax.random.randint(jax.random.fold_in(_rk, 8), (128,), 0, max(1, 64 // 4) + 1, jnp.int32)
        _ctx_1024P = jax.random.normal(jax.random.fold_in(_rk, 11), (128, 16, 128), jnp.float32)
        _ctx_1024c = jax.random.dirichlet(jax.random.fold_in(_rk, 511), 0.3 * jnp.ones((16,), jnp.float32), (128, 64))
        _ctx_1024t = jnp.einsum('bsk,bkd->bsd', _ctx_1024c, _ctx_1024P)
        _ctx_1024t = _ctx_1024t * jax.lax.rsqrt(jnp.mean(jnp.square(_ctx_1024t)) + 1e-12) * 0.953939
        ctx_1024 = -0.000125008 + 0.999885 * (_ctx_1024t + 0.3 * jax.random.normal(jax.random.fold_in(_rk, 611), (128, 64, 128), jnp.float32))
        _validS = jnp.arange(64)[None, :] < _lenS[:, None]
        _validS2 = jnp.arange(64)[None, :] < _lenS2[:, None]
        _causal = jnp.tril(jnp.ones((64, 64), dtype=bool))
        mask_BxS2_bf1 = jnp.ones((128, 64), dtype=bool)
        return (x, ctx_1024, mask_BxS2_bf1)
    x, ctx_1024, mask_BxS2_bf1 = _rec_inputs()

    def _L0_attn_setup():
        import jax, jax.numpy as jnp
        from jax import lax
        import numpy as np
        DIM = 128
        HEADS = 16
        B, N = (2, 256)

        def sn_dense(x, W, u, sigma_param):
            v = lax.stop_gradient(W @ u)
            v = lax.stop_gradient(v / jnp.linalg.norm(v, ord=2))
            u2 = lax.stop_gradient(W.T @ v)
            u2 = lax.stop_gradient(u2 / jnp.linalg.norm(u2, ord=2))
            sigma = jnp.einsum('c,cd,d->', v, W, u2)
            return x @ (sigma_param[0] / sigma * W)
        key = jax.random.key(seed)
        ks = jax.random.split(key, 5)
        std = 0.1
        batch = jax.random.normal(ks[0], (B, N, DIM), dtype=jnp.float32)
        W_qkv = jax.random.normal(ks[1], (DIM, 3 * DIM), dtype=jnp.float32) * std
        W_proj = jax.random.normal(ks[2], (DIM, DIM), dtype=jnp.float32) * std
        u_qkv = jax.random.normal(ks[3], (3 * DIM,), dtype=jnp.float32)
        u_qkv = u_qkv / jnp.linalg.norm(u_qkv)
        u_proj = jax.random.normal(ks[4], (DIM,), dtype=jnp.float32)
        u_proj = u_proj / jnp.linalg.norm(u_proj)
        sigma_qkv = jnp.ones((1,), dtype=jnp.float32)
        sigma_proj = jnp.ones((1,), dtype=jnp.float32)
        return {'batch': batch, 'W_qkv': W_qkv, 'u_qkv': u_qkv, 'sigma_qkv': sigma_qkv, 'W_proj': W_proj, 'u_proj': u_proj, 'sigma_proj': sigma_proj}
    _L0_attn_all = _L0_attn_setup()
    _L0_attn_in = {k: v for k, v in _L0_attn_all.items() if k in ('W_qkv', 'u_qkv', 'sigma_qkv', 'W_proj', 'u_proj', 'sigma_proj')}
    del _L0_attn_all

    def _L0_xattn_setup():
        import jax, jax.numpy as jnp
        import numpy as np
        DIM = 128
        HEADS = 16
        DIM_HEAD = 64
        INNER = HEADS * DIM_HEAD
        EPS = 1e-05

        def layer_norm(x, gamma, beta):
            mu = jnp.mean(x, axis=-1, keepdims=True)
            var = jnp.var(x, axis=-1, keepdims=True)
            return (x - mu) * jax.lax.rsqrt(var + EPS) * gamma + beta
        key = jax.random.key(seed)
        ks = jax.random.split(key, 8)
        b, n, m = (8, 512, 64)
        x = jax.random.normal(ks[0], (b, n, DIM), dtype=jnp.float32)
        latents = jax.random.normal(ks[1], (b, m, DIM), dtype=jnp.float32)
        mask = jnp.ones((b, n), dtype=bool)
        s = 0.02
        Wq = jax.random.normal(ks[2], (DIM, INNER), dtype=jnp.float32) * s
        Wkv = jax.random.normal(ks[3], (DIM, 2 * INNER), dtype=jnp.float32) * s
        Wout = jax.random.normal(ks[4], (INNER, DIM), dtype=jnp.float32) * s
        g_x = jnp.ones((DIM,), jnp.float32)
        b_x = jnp.zeros((DIM,), jnp.float32)
        g_l = jnp.ones((DIM,), jnp.float32)
        b_l = jnp.zeros((DIM,), jnp.float32)
        g_o = jnp.ones((DIM,), jnp.float32)
        b_o = jnp.zeros((DIM,), jnp.float32)
        return {'x': x, 'latents': latents, 'mask': mask, 'g_x': g_x, 'b_x': b_x, 'g_l': g_l, 'b_l': b_l, 'Wq': Wq, 'Wkv': Wkv, 'Wout': Wout, 'g_o': g_o, 'b_o': b_o}
    _L0_xattn_all = _L0_xattn_setup()
    _L0_xattn_in = {k: v for k, v in _L0_xattn_all.items() if k in ('g_x', 'b_x', 'g_l', 'b_l', 'Wq', 'Wkv', 'Wout', 'g_o', 'b_o')}
    del _L0_xattn_all

    def _L0_ffn_setup():
        import jax, jax.numpy as jnp
        import numpy as np
        from jax import lax
        B, N, DIM = (4, 256, 128)
        HEADS = 8
        NUM_EXPERTS = 2048
        NUM_KEYS = 128
        DIM_KEY = DIM // 2
        DIM_INNER = 2 * DIM
        PK_TOPK = 16
        TOPK = 1
        key = jax.random.key(seed)
        ks = jax.random.split(key, 10)
        s = lambda k, shape, std=0.02: jax.random.normal(k, shape, dtype=jnp.float32) * std
        return {'x': jax.random.normal(ks[0], (B, N, DIM), dtype=jnp.float32), 'Wq': s(ks[1], (DIM_KEY * HEADS * 2, DIM)), 'keys': s(ks[2], (HEADS, NUM_KEYS, 2, DIM_KEY)), 'W_in': s(ks[3], (DIM_INNER, DIM)), 'W_out': s(ks[4], (DIM, DIM_INNER)), 'in_a': s(ks[5], (NUM_EXPERTS, DIM)), 'in_b': s(ks[6], (NUM_EXPERTS, DIM_INNER)), 'out_a': s(ks[7], (NUM_EXPERTS, DIM_INNER)), 'out_b': s(ks[8], (NUM_EXPERTS, DIM))}
    _L0_ffn_all = _L0_ffn_setup()
    _L0_ffn_in = {k: v for k, v in _L0_ffn_all.items() if k in ('Wq', 'keys', 'W_in', 'W_out', 'in_a', 'in_b', 'out_a', 'out_b')}
    del _L0_ffn_all
    return {'x': x, 'ctx_1024': ctx_1024, 'mask_BxS2_bf1': mask_BxS2_bf1, 'L0_attn_W_qkv': _L0_attn_in['W_qkv'], 'L0_attn_u_qkv': _L0_attn_in['u_qkv'], 'L0_attn_sigma_qkv': _L0_attn_in['sigma_qkv'], 'L0_attn_W_proj': _L0_attn_in['W_proj'], 'L0_attn_u_proj': _L0_attn_in['u_proj'], 'L0_attn_sigma_proj': _L0_attn_in['sigma_proj'], 'L0_xattn_g_x': _L0_xattn_in['g_x'], 'L0_xattn_b_x': _L0_xattn_in['b_x'], 'L0_xattn_g_l': _L0_xattn_in['g_l'], 'L0_xattn_b_l': _L0_xattn_in['b_l'], 'L0_xattn_Wq': _L0_xattn_in['Wq'], 'L0_xattn_Wkv': _L0_xattn_in['Wkv'], 'L0_xattn_Wout': _L0_xattn_in['Wout'], 'L0_xattn_g_o': _L0_xattn_in['g_o'], 'L0_xattn_b_o': _L0_xattn_in['b_o'], 'L0_ffn_Wq': _L0_ffn_in['Wq'], 'L0_ffn_keys': _L0_ffn_in['keys'], 'L0_ffn_W_in': _L0_ffn_in['W_in'], 'L0_ffn_W_out': _L0_ffn_in['W_out'], 'L0_ffn_in_a': _L0_ffn_in['in_a'], 'L0_ffn_in_b': _L0_ffn_in['in_b'], 'L0_ffn_out_a': _L0_ffn_in['out_a'], 'L0_ffn_out_b': _L0_ffn_in['out_b']}

def reference(x, ctx_1024, mask_BxS2_bf1, L0_attn_W_qkv, L0_attn_u_qkv, L0_attn_sigma_qkv, L0_attn_W_proj, L0_attn_u_proj, L0_attn_sigma_proj, L0_xattn_g_x, L0_xattn_b_x, L0_xattn_g_l, L0_xattn_b_l, L0_xattn_Wq, L0_xattn_Wkv, L0_xattn_Wout, L0_xattn_g_o, L0_xattn_b_o, L0_ffn_Wq, L0_ffn_keys, L0_ffn_W_in, L0_ffn_W_out, L0_ffn_in_a, L0_ffn_in_b, L0_ffn_out_a, L0_ffn_out_b):
    import jax
    import jax.numpy as jnp

    def _L0_attn_ref(batch, W_qkv, u_qkv, sigma_qkv, W_proj, u_proj, sigma_proj):
        import jax, jax.numpy as jnp
        from jax import lax
        import numpy as np
        DIM = 128
        HEADS = 16
        B, N = (2, 256)

        def sn_dense(x, W, u, sigma_param):
            v = lax.stop_gradient(W @ u)
            v = lax.stop_gradient(v / jnp.linalg.norm(v, ord=2))
            u2 = lax.stop_gradient(W.T @ v)
            u2 = lax.stop_gradient(u2 / jnp.linalg.norm(u2, ord=2))
            sigma = jnp.einsum('c,cd,d->', v, W, u2)
            return x @ (sigma_param[0] / sigma * W)
        b, n, d = batch.shape
        h = HEADS
        hd = d // h
        qkv = sn_dense(batch, W_qkv, u_qkv, sigma_qkv)
        q, k, v = jnp.split(qkv, 3, axis=-1)
        split_heads = lambda t: t.reshape(b, n, h, hd).transpose(0, 2, 1, 3)
        q, k, v = (split_heads(q), split_heads(k), split_heads(v))
        scale = hd ** (-0.5)
        att = jnp.einsum('bhqd,bhkd->bhqk', q, k) * scale
        causal = jnp.tril(jnp.ones((n, n), dtype=jnp.float32))
        big_neg = jnp.finfo(att.dtype).min
        att = jnp.where(causal[None, None] == 0, big_neg, att)
        att = jax.nn.softmax(att, axis=-1)
        x = jnp.einsum('bhqk,bhkd->bhqd', att, v)
        x = x.transpose(0, 2, 1, 3).reshape(b, n, d)
        x = sn_dense(x, W_proj, u_proj, sigma_proj)
        return x

    def _L0_xattn_ref(x, latents, mask, g_x, b_x, g_l, b_l, Wq, Wkv, Wout, g_o, b_o):
        import jax, jax.numpy as jnp
        import numpy as np
        DIM = 128
        HEADS = 16
        DIM_HEAD = 64
        INNER = HEADS * DIM_HEAD
        EPS = 1e-05

        def layer_norm(x, gamma, beta):
            mu = jnp.mean(x, axis=-1, keepdims=True)
            var = jnp.var(x, axis=-1, keepdims=True)
            return (x - mu) * jax.lax.rsqrt(var + EPS) * gamma + beta
        scale = DIM_HEAD ** (-0.5)
        xn = layer_norm(x, g_x, b_x)
        ln = layer_norm(latents, g_l, b_l)
        b, m = (ln.shape[0], ln.shape[1])
        q = jnp.einsum('bnd,de->bne', ln, Wq)
        kv_in = jnp.concatenate([xn, ln], axis=1)
        kv = jnp.einsum('bnd,de->bne', kv_in, Wkv)
        k, v = jnp.split(kv, 2, axis=-1)

        def split_heads(t):
            return t.reshape(t.shape[0], t.shape[1], HEADS, DIM_HEAD).transpose(0, 2, 1, 3)
        q, k, v = (split_heads(q), split_heads(k), split_heads(v))
        q = q * scale
        sim = jnp.einsum('bhid,bhjd->bhij', q, k)
        full_mask = jnp.concatenate([mask, jnp.ones((b, m), dtype=bool)], axis=1)
        max_neg = -jnp.finfo(sim.dtype).max
        sim = jnp.where(full_mask[:, None, None, :], sim, max_neg)
        attn = jax.nn.softmax(sim, axis=-1)
        out = jnp.einsum('bhij,bhjd->bhid', attn, v)
        out = out.transpose(0, 2, 1, 3).reshape(b, m, INNER)
        out = jnp.einsum('bne,ed->bnd', out, Wout)
        return layer_norm(out, g_o, b_o)

    def _L0_ffn_ref(x, Wq, keys, W_in, W_out, in_a, in_b, out_a, out_b):
        import jax, jax.numpy as jnp
        import numpy as np
        from jax import lax
        B, N, DIM = (4, 256, 128)
        HEADS = 8
        NUM_EXPERTS = 2048
        NUM_KEYS = 128
        DIM_KEY = DIM // 2
        DIM_INNER = 2 * DIM
        PK_TOPK = 16
        TOPK = 1
        b, n, d = x.shape
        q = (x @ Wq.T).reshape(b, n, 2, HEADS, DIM_KEY).transpose(2, 0, 1, 3, 4)
        sim = jnp.einsum('pbnhd,hkpd->pbnhk', q, keys)
        sx, ix = lax.top_k(sim[0], PK_TOPK)
        sy, iy = lax.top_k(sim[1], PK_TOPK)
        all_scores = (sx[..., :, None] + sy[..., None, :]).reshape(b, n, HEADS, PK_TOPK * PK_TOPK)
        all_indices = (ix[..., :, None] * NUM_KEYS + iy[..., None, :]).reshape(b, n, HEADS, PK_TOPK * PK_TOPK)
        scores, pk = lax.top_k(all_scores, TOPK)
        indices = jnp.take_along_axis(all_indices, pk, axis=-1)
        A_in = in_a[indices]
        B_in = in_b[indices]
        A_out = out_a[indices]
        B_out = out_b[indices]
        gate = jax.nn.relu(scores)
        hidden = x @ W_in.T
        lin = jnp.einsum('bnd,bnhkd->bnhk', x, A_in) * gate
        hidden = hidden + jnp.einsum('bnhk,bnhkd->bnd', lin, B_in)
        hidden = jax.nn.gelu(hidden, approximate=False)
        out = hidden @ W_out.T
        lout = jnp.einsum('bnd,bnhkd->bnhk', hidden, A_out) * gate
        out = out + jnp.einsum('bnhk,bnhkd->bnd', lout, B_out)
        return out
    x = _layernorm(x + _L0_attn_ref(x, L0_attn_W_qkv, L0_attn_u_qkv, L0_attn_sigma_qkv, L0_attn_W_proj, L0_attn_u_proj, L0_attn_sigma_proj), axis=-1)
    x = _layernorm(x + _L0_xattn_ref(ctx_1024, x, mask_BxS2_bf1, L0_xattn_g_x, L0_xattn_b_x, L0_xattn_g_l, L0_xattn_b_l, L0_xattn_Wq, L0_xattn_Wkv, L0_xattn_Wout, L0_xattn_g_o, L0_xattn_b_o), axis=-1)
    x = _layernorm(x + _L0_ffn_ref(x, L0_ffn_Wq, L0_ffn_keys, L0_ffn_W_in, L0_ffn_W_out, L0_ffn_in_a, L0_ffn_in_b, L0_ffn_out_a, L0_ffn_out_b), axis=-1)
    return x

_drawn_inputs = setup_inputs


def setup_inputs(seed=0):
    import zlib

    import numpy as np

    out = dict(_drawn_inputs(seed))
    spreads = {'L0_xattn_g_x': (1.0, 0.2),
     'L0_xattn_b_x': (0.0, 0.1),
     'L0_xattn_g_l': (1.0, 0.2),
     'L0_xattn_b_l': (0.0, 0.1),
     'L0_xattn_g_o': (1.0, 0.2),
     'L0_xattn_b_o': (0.0, 0.1)}
    factors = {'L0_attn_u_qkv': 8.0,
     'L0_attn_u_proj': 8.0,
     'L0_ffn_Wq': 8.0,
     'L0_ffn_keys': 8.0,
     'L0_ffn_in_a': 8.0,
     'L0_ffn_in_b': 8.0,
     'L0_ffn_out_a': 8.0,
     'L0_ffn_out_b': 8.0,
     'L0_ffn_W_out': 4.455}
    for name, (base, spread) in spreads.items():
        noise = np.random.default_rng([zlib.crc32(name.encode()), seed]).standard_normal(out[name].shape)
        drawn = base * np.exp(spread * noise) if base else spread * noise
        out[name] = jnp.asarray(drawn.astype(out[name].dtype))
    for name, factor in factors.items():
        out[name] = (out[name] * factor).astype(out[name].dtype)
    return out
```

```python
from contextlib import ExitStack

import concourse.bass as bass
from concourse import mybir

ALU = mybir.AluOpType
ACT = mybir.ActivationFunctionType
AX_X = mybir.AxisListType.X
F32 = mybir.dt.float32
BF16 = mybir.dt.bfloat16
U32 = mybir.dt.uint32
U8 = mybir.dt.uint8

P = 128
BATCH, SEQ, DIM = 128, 64, 128
PAIRS = BATCH // 2
HEADS = 16
HD = DIM // HEADS
XH = 64
INNER = HEADS * XH
EPS = 1e-5
NEG = -1e30
FH = 8
KEYS = 128
EXPERTS = 2048
LAST = EXPERTS - 1
XROWS = EXPERTS // KEYS
FFN = 2 * DIM
TABLE = 2 * DIM + 2 * FFN
PEELED = 3
A_IN, B_IN, A_OUT, B_OUT = 0, DIM, DIM + FFN, DIM + 2 * FFN


class Pair:

    def __init__(self, base, off):
        self.base, self.off = base, off
        self.t = 2 * base + off
        self.slot = off % 2
        self.turn = base + off // 2

    def at(self, d):
        return Pair(self.base, self.off + d)

    def real(self):
        return not isinstance(self.t, int) or 0 <= self.t < PAIRS


def wait(eng, sem, value):
    if isinstance(value, int) and value <= 0:
        return
    eng.wait_ge(sem, value)


def wait_apart(eng, sem, value):
    if isinstance(value, int):
        return wait(eng, sem, value)
    eng.wait_ge(sem, value)
    eng.nop(nofuse=True)


def steps(eng, body, first, last, ahead=1):
    for s in range(first, PEELED):
        body(Pair(0, s))
    turns = (PAIRS - ahead - PEELED) // 2
    with eng.Fori(0, turns) as i:
        body(Pair(i, PEELED))
        body(Pair(i, PEELED + 1))
    for s in range(2 * turns + PEELED, last + 1):
        body(Pair(0, s))


def decoder_layer(nc, x, xT, ctx_in, mask, w_attn, u_attn, sig_qkv, sig_proj,
                  gains, wq_t, wk_t, wv_t, wout, ffn_wq, keys_t, w_in_t, w_out_t, table, out):
    with ExitStack() as stack:
        def sb(name, shape, dt=F32):
            return stack.enter_context(nc.sbuf_tensor(name, shape, dt))

        def sem(name):
            return stack.enter_context(nc.semaphore(name))

        bank = stack.enter_context(nc.psum_tensor("bank", [P, 8, 512], F32))

        ident = sb("ident", [P, P])
        identb = sb("identb", [P, P], BF16)
        ones_row = sb("ones_row", [1, P])
        onesb_row = sb("onesb_row", [1, P], BF16)
        causal = sb("causal", [P, 4, SEQ], BF16)
        head_of = sb("head_of", [P, 4])
        key_mask = sb("key_mask", [1, BATCH, 2, SEQ], BF16)
        mask_u8 = sb("mask_u8", [1, BATCH, SEQ], U8)
        eps_t = sb("eps_t", [P, 2])
        mhalf = sb("mhalf", [P, 2])
        rev_key = sb("rev_key", [P, KEYS])
        rev_row = sb("rev_row", [P, XROWS])
        gb = sb("gb", [P, 6, DIM])
        w_self = sb("w_self", [P, 4 * DIM])
        u_self = sb("u_self", [P, 4 * DIM])
        wu = sb("wu", [P, 4 * DIM])
        a_self = sb("a_self", [P, 2])
        row_self = sb("row_self", [1, 4 * DIM])
        row_sq = sb("row_sq", [1, 4 * DIM])
        norms = sb("norms", [1, 4])
        norms_p = sb("norms_p", [1, 4])
        powers = sb("powers", [1, 4])
        sigmas = sb("sigmas", [1, 2])
        c_row = sb("c_row", [1, 2])
        c_all = sb("c_all", [P, 2])
        fold_a = sb("fold_a", [P, HEADS, DIM])
        fold_b = sb("fold_b", [P, HEADS, DIM])
        fold_g = sb("fold_g", [P, HEADS, KEYS])
        hid_w = sb("hid_w", [P, FFN + 2])
        out_w = sb("out_w", [P, 2, DIM])
        last_row = sb("last_row", [P, TABLE])
        X = sb("X", [P, PAIRS, DIM])

        GX, BX, GL, BL, GO, BO = range(6)

        consts_ready = sem("consts_ready")
        const_step = sem("const_step")
        weights_in = sem("weights_in")
        fold_in = sem("fold_in")
        norm_a = sem("norm_a")
        norm_row = sem("norm_row")
        norm_copied = sem("norm_copied")
        norm_sq = sem("norm_sq")
        norm_pow = sem("norm_pow")
        norm_c = sem("norm_c")
        norm_cb = sem("norm_cb")
        self_ready = sem("self_ready")
        fold_done = sem("fold_done")
        fold_copied = sem("fold_copied")
        mask_ready = sem("mask_ready")

        with ExitStack() as prep, nc.Block() as block:
            factors = prep.enter_context(nc.sbuf_tensor("factors", [P, 6, 8, DIM], F32))
            rows_i = prep.enter_context(nc.sbuf_tensor("rows_i", [P, KEYS], mybir.dt.int32))

            @block.sync
            def _(sp):
                sp.dma_start(w_self[:, :], w_attn).then_inc(weights_in, 16)
                sp.dma_start(u_self[:, :], u_attn.partition_broadcast(P)).then_inc(weights_in, 16)
                sp.dma_start(sigmas[:, 0:1], sig_qkv.rearrange("(a n) -> a n", a=1)).then_inc(weights_in, 16)
                sp.dma_start(sigmas[:, 1:2], sig_proj.rearrange("(a n) -> a n", a=1)).then_inc(weights_in, 16)
                sp.dma_start(mask_u8[:, :, :], mask.rearrange("(a b) s -> a b s", a=1)).then_inc(weights_in, 16)
                for n, w in enumerate((wq_t, wk_t, wv_t, wout, ffn_wq, keys_t)):
                    sp.dma_start(factors[:, n, :, :], w.rearrange("(c p) d -> p c d", p=P)).then_inc(fold_in, 16)
                sp.dma_start(gb[:, :, :].rearrange("p a b -> p (a b)"), gains.partition_broadcast(P)).then_inc(weights_in, 16)
                sp.dma_start(hid_w[:, 0:FFN], w_in_t).then_inc(weights_in, 16)
                sp.dma_start(hid_w[:, FFN:FFN + 1], table[LAST, A_IN:A_IN + DIM].rearrange("(p a) -> p a", a=1)).then_inc(weights_in, 16)
                sp.dma_start(hid_w[:, FFN + 1:FFN + 2], table[LAST, A_IN:A_IN + DIM].rearrange("(p a) -> p a", a=1)).then_inc(weights_in, 16)
                sp.dma_start(out_w[:, :, :], w_out_t.rearrange("(c p) d -> p c d", p=P)).then_inc(weights_in, 16)
                sp.dma_start(last_row[:, :], table[LAST, :].partition_broadcast(P)).then_inc(weights_in, 16)
                sp.wait_ge(weights_in, 11 * 16)
                sp.wait_ge(fold_in, 6 * 16)

            @block.gpsimd
            def _(pool):
                made = 0

                def settle(instruction):
                    nonlocal made
                    made += 1
                    instruction.then_inc(const_step, 1)
                    pool.wait_ge(const_step, made)

                settle(nc.gpsimd.memset(ident[:, :], 0.0))
                settle(nc.gpsimd.affine_select(out=ident[:, :], in_=ident[:, :], compare_op=ALU.not_equal, fill=1.0,
                                               base=0, pattern=[[-1, P]], channel_multiplier=1))
                settle(nc.gpsimd.iota(rows_i[:, :], pattern=[[-1, KEYS]], base=KEYS, channel_multiplier=0))
                settle(nc.gpsimd.memset(powers[:, 0:2], 0.5))
                settle(nc.gpsimd.memset(powers[:, 2:4], -0.5))
                settle(nc.gpsimd.memset(eps_t[:, :], EPS))
                settle(nc.gpsimd.memset(mhalf[:, :], -0.5))
                settle(nc.gpsimd.memset(causal[:, :, :], 0.0))
                for b in range(2):
                    half = causal[SEQ * b:SEQ * b + SEQ, :, :]
                    settle(nc.gpsimd.affine_select(out=half, in_=half, compare_op=ALU.is_ge, fill=NEG, base=0,
                                                   pattern=[[0, 4], [-1, SEQ]], channel_multiplier=1))
                settle(nc.gpsimd.memset(head_of[:, :], 1.0))
                for j in range(4):
                    quad = head_of[32 * j:32 * j + 32, :]
                    settle(nc.gpsimd.affine_select(out=quad, in_=quad, compare_op=ALU.is_ge, fill=0.0, base=0,
                                                   pattern=[[-HD, 4]], channel_multiplier=1))
                    settle(nc.gpsimd.affine_select(out=quad, in_=quad, compare_op=ALU.is_ge, fill=0.0, base=HD - 1,
                                                   pattern=[[HD, 4]], channel_multiplier=-1))
                pool.wait_ge(norm_sq, 4)
                nc.gpsimd.tensor_tensor(norms_p[:, :], norms[:, :], powers[:, :], ALU.pow).then_inc(norm_pow, 1)

            @block.vector
            def _(dve):
                nc.vector.memset(ones_row[:, :], 1.0).then_inc(consts_ready, 1)
                nc.vector.memset(onesb_row[:, :], 1.0).then_inc(consts_ready, 1)
                nc.vector.memset(key_mask[:, :, :, :].rearrange("a b c s -> a (b c s)"), 0.0).then_inc(consts_ready, 1)
                dve.wait_ge(const_step, 2)
                nc.vector.tensor_copy(identb[:, :], ident[:, :]).then_inc(consts_ready, 1)
                dve.wait_ge(const_step, 3)
                nc.vector.tensor_copy(rev_key[:, :], rows_i[:, :]).then_inc(consts_ready, 1)
                nc.vector.tensor_scalar(rev_row[:, :], rows_i[:, 0:XROWS], float(XROWS - KEYS), None,
                                        ALU.add).then_inc(consts_ready, 1)
                dve.wait_ge(weights_in, 11 * 16)
                nc.vector.tensor_tensor(wu[:, :], w_self[:, :], u_self[:, :], ALU.mult).then_inc(norm_a, 1)
                dve.wait_ge(norm_a, 1)
                nc.vector.tensor_reduce(a_self[:, 0:1], wu[:, 0:3 * DIM], AX_X, ALU.add).then_inc(norm_a, 1)
                nc.vector.tensor_reduce(a_self[:, 1:2], wu[:, 3 * DIM:4 * DIM], AX_X, ALU.add).then_inc(norm_a, 1)
                dve.wait_ge(norm_row, 1)
                nc.vector.tensor_copy(row_self[:, :], bank[0:1, 0, :]).then_inc(norm_copied, 1)
                nc.vector.tensor_copy(norms[:, 0:2], bank[0:1, 1, 0:2]).then_inc(norm_sq, 1)
                dve.wait_ge(norm_copied, 1)
                nc.vector.tensor_tensor(row_sq[:, :], row_self[:, :], row_self[:, :], ALU.mult).then_inc(norm_sq, 1)
                dve.wait_ge(norm_sq, 2)
                nc.vector.tensor_reduce(norms[:, 2:3], row_sq[:, 0:3 * DIM], AX_X, ALU.add).then_inc(norm_sq, 1)
                nc.vector.tensor_reduce(norms[:, 3:4], row_sq[:, 3 * DIM:4 * DIM], AX_X, ALU.add).then_inc(norm_sq, 1)
                dve.wait_ge(norm_pow, 1)
                nc.vector.tensor_tensor(c_row[:, :], norms_p[:, 0:2], norms_p[:, 2:4], ALU.mult).then_inc(norm_c, 1)
                dve.wait_ge(norm_c, 1)
                nc.vector.tensor_tensor(c_row[:, :], c_row[:, :], sigmas[:, :], ALU.mult).then_inc(norm_c, 1)
                dve.wait_ge(norm_cb, 1)
                nc.vector.tensor_copy(c_all[:, :], bank[:, 1, 0:2]).then_inc(norm_c, 1)
                dve.wait_ge(norm_c, 3)
                nc.vector.tensor_scalar(w_self[:, 0:DIM], w_self[:, 0:DIM], c_all[:, 0:1], float(HD) ** -0.5,
                                        ALU.mult, ALU.mult).then_inc(self_ready, 1)
                nc.vector.tensor_scalar(w_self[:, DIM:3 * DIM], w_self[:, DIM:3 * DIM], c_all[:, 0:1], None,
                                        ALU.mult).then_inc(self_ready, 1)
                nc.vector.tensor_scalar(w_self[:, 3 * DIM:], w_self[:, 3 * DIM:], c_all[:, 1:2], None,
                                        ALU.mult).then_inc(self_ready, 1)
                dve.wait_ge(consts_ready, 3)
                for b in range(2):
                    kept = mask_u8[:, :, :].rearrange("a (t b) s -> a t b s", b=2)[:, :, b, :]
                    dst = key_mask[:, :, :, :].rearrange("a (t b) c s -> a t b c s", b=2)[:, :, b, 1 - b, :]
                    nc.vector.tensor_scalar(dst, kept, 1.0, -NEG, ALU.subtract, ALU.mult).then_inc(mask_ready, 1)
                for g in range(4):
                    dve.wait_ge(fold_done, 3 * g + 3)
                    for n, (dst, scale) in enumerate(((fold_a, XH ** -0.5), (fold_b, 1.0), (fold_g, 1.0))):
                        nc.vector.tensor_scalar(
                            dst[:, 4 * g:4 * g + 4, :].rearrange("p (c e) d -> p e c d", e=2),
                            bank[:, 2 + 2 * n:4 + 2 * n, 0:2 * DIM].rearrange("p e (c d) -> p e c d", c=2),
                            scale, None, ALU.mult).then_inc(fold_copied, 1)

            @block.tensor
            def _(pe):
                pe.wait_ge(norm_a, 3)
                nc.tensor.matmul(bank[0:1, 0, 0:3 * DIM], a_self[:, 0:1], w_self[:, 0:3 * DIM], start=True, stop=True)
                nc.tensor.matmul(bank[0:1, 0, 3 * DIM:4 * DIM], a_self[:, 1:2], w_self[:, 3 * DIM:4 * DIM],
                                 start=True, stop=True)
                for n in range(2):
                    last = nc.tensor.matmul(bank[0:1, 1, n:n + 1], a_self[:, n:n + 1], a_self[:, n:n + 1],
                                            start=True, stop=True)
                last.then_inc(norm_row, 1)
                pe.wait_ge(norm_c, 2)
                pe.wait_ge(norm_sq, 2)
                nc.tensor.matmul(bank[:, 1, 0:2], ones_row[:, :], c_row[:, :], start=True, stop=True).then_inc(norm_cb, 1)
                pe.wait_ge(fold_in, 6 * 16)
                for g in range(4):
                    wait(pe, fold_copied, 3 * g)
                    for n in range(3):
                        for k in range(4):
                            lo = XH * (k % 2)
                            c = 2 * g + k // 2
                            last = nc.tensor.matmul(bank[:, 2 + 2 * n + k % 2, (k // 2) * DIM:(k // 2 + 1) * DIM],
                                                    factors[lo:lo + XH, 2 * n, c, :],
                                                    factors[lo:lo + XH, 2 * n + 1, c, :], start=True, stop=True)
                        last.then_inc(fold_done, 1)

        self_attention(nc, bank, x, xT, X, w_self, ident, identb, causal, head_of, eps_t, mhalf)
        cross_attention(nc, bank, ctx_in, X, gb, fold_a, fold_b, ident, onesb_row, key_mask, eps_t, mhalf)
        expert_ffn(nc, bank, X, fold_g, hid_w, out_w, last_row, table, rev_key, rev_row, ident, eps_t, mhalf, out)


def self_attention(nc, bank, x, xT, X, w_self, ident, identb, causal, head_of, eps_t, mhalf):
    with ExitStack() as stack:
        def sb(name, shape, dt=F32):
            return stack.enter_context(nc.sbuf_tensor(name, shape, dt))

        def sem(name):
            return stack.enter_context(nc.semaphore(name))

        x_t = [sb(f"x_t{p}", [P, 2, 2, SEQ]) for p in range(2)]
        x_row = [sb(f"x_row{p}", [P, DIM]) for p in range(2)]
        q_t = sb("q_t", [P, 2 * SEQ])
        k_blocks = sb("k_blocks", [P, 2, 4, SEQ])
        v_blocks = [sb(f"v_blocks{p}", [P, 2, 8, 2, HD]) for p in range(2)]
        probs = [sb(f"probs{p}", [P, HEADS, SEQ]) for p in range(2)]
        probs_t = sb("probs_t", [P, 8, P])
        top = sb("top", [P, HEADS])
        total = sb("total", [P, HEADS])
        inv = sb("inv", [P, HEADS])
        heads_out = sb("heads_out", [P, DIM])
        heads_out_t = sb("heads_out_t", [P, DIM])
        resid = sb("resid", [P, DIM])
        stats = sb("stats", [P, 6])
        mv = sb("mv", [P, 2])
        var_eps = sb("var_eps", [P, 1])
        rstd = sb("rstd", [P, 1])

        loaded = [sem(f"a_loaded{p}") for p in range(2)]
        zeroed = sem("a_zeroed")
        qkv_done = sem("a_qkv_done")
        q_copied = sem("a_q_copied")
        v_spread = sem("a_v_spread")
        k_spread = sem("a_k_spread")
        scores_done = sem("a_scores_done")
        top_done = sem("a_top_done")
        shifted = sem("a_shifted")
        exp_done = sem("a_exp_done")
        total_done = sem("a_total_done")
        inv_done = sem("a_inv_done")
        turned = sem("a_turned")
        turned_copied = sem("a_turned_copied")
        pv_done = sem("a_pv_done")
        heads_scaled = sem("a_heads_scaled")
        out_turned = sem("a_out_turned")
        out_copied = sem("a_out_copied")
        projected = sem("a_projected")
        resid_done = sem("a_resid_done")
        stats_done = sem("a_stats_done")
        mv_done = sem("a_mv_done")
        eps_added = sem("a_eps_added")
        rstd_done = sem("a_rstd_done")
        normed = sem("a_normed")

        qkv_ps = bank[:, 0, :]
        scores_ps = bank[:, 1:5, 0:4 * SEQ]
        turned_ps = bank[:, 5:7, :]
        misc_ps = bank[:, 7, 0:DIM]
        block = stack.enter_context(nc.Block())

        @block.sync
        def _(sp):
            def load(n):
                t, p = n.t, n.slot
                wait(sp, qkv_done, t - 1)
                wait(sp, resid_done, t - 1)
                for c in range(2):
                    sp.dma_start(x_t[p][:, :, c, :], xT[:, bass.ds(t * P, P)].rearrange("d (b s) -> d b s", b=2)
                                 ).then_inc(loaded[p], 16)
                sp.dma_start(x_row[p][:, :], x[bass.ds(t * P, P), :]).then_inc(loaded[p], 16)
            steps(sp, load, 0, PAIRS - 1)

        @block.tensor
        def _(pe):
            def step(s):
                n = s
                if n.real():
                    pe.wait_ge(exp_done, n.t + 1)
                    wait(pe, turned_copied, n.t)
                    for c in range(8):
                        last = nc.tensor.transpose(turned_ps[:, c // 4, (c % 4) * P:(c % 4 + 1) * P],
                                                   probs[n.slot][:, 2 * c:2 * c + 2, :].rearrange("p h k -> p (h k)"),
                                                   ident[:, :])
                    last.then_inc(turned, 1)
                n = s.at(-1)
                if n.real():
                    pe.wait_ge(out_copied, n.t + 1)
                    nc.tensor.matmul(misc_ps, heads_out_t[:, :], w_self[:, 3 * DIM:4 * DIM],
                                     start=True, stop=True).then_inc(projected, 1)
                n = s.at(1)
                if n.real():
                    pe.wait_ge(loaded[n.slot], 48 * (n.turn + 1))
                    wait(pe, q_copied, n.t)
                    wait(pe, v_spread, 2 * n.t)
                    wait(pe, k_spread, n.t)
                    for c in range(2):
                        nc.tensor.matmul(qkv_ps[:, c * P:(c + 1) * P], w_self[:, c * DIM:(c + 1) * DIM],
                                         x_t[n.slot][:, :, 0, :], start=True, stop=True)
                    for b in range(2):
                        last = nc.tensor.matmul(qkv_ps[:, (2 + b) * P:(3 + b) * P],
                                                x_t[n.slot][:, b, :, :].rearrange("p c s -> p (c s)"),
                                                w_self[:, 2 * DIM:3 * DIM], start=True, stop=True)
                    last.then_inc(qkv_done, 1)
                n = s
                if n.real():
                    pe.wait_ge(turned_copied, n.t + 1)
                    pe.wait_ge(v_spread, 2 * (n.t + 1))
                    wait(pe, resid_done, n.t)
                    for b in range(2):
                        for c in range(8):
                            last = nc.tensor.matmul(misc_ps[SEQ * b:SEQ * b + SEQ, 2 * HD * c:2 * HD * (c + 1)],
                                                    probs_t[:, c, SEQ * b:SEQ * b + SEQ],
                                                    v_blocks[n.slot][:, b, c, :, :].rearrange("p e r -> p (e r)"),
                                                    start=True, stop=True)
                    last.then_inc(pv_done, 1)
                n = s.at(1)
                if n.real():
                    pe.wait_ge(q_copied, n.t + 1)
                    pe.wait_ge(k_spread, n.t + 1)
                    wait(pe, shifted, n.t)
                    for j in range(4):
                        nc.tensor.matmul(scores_ps[:, j, :], identb[:, :],
                                         causal[:, :, :].rearrange("p g k -> p (g k)"),
                                         start=True, stop=False, skip_group_check=True)
                    for b in range(2):
                        for j in range(4):
                            last = nc.tensor.matmul(scores_ps[SEQ * b:SEQ * b + SEQ, j, :],
                                                    q_t[32 * j:32 * j + 32, SEQ * b:SEQ * b + SEQ],
                                                    k_blocks[32 * j:32 * j + 32, b, :, :].rearrange("p g k -> p (g k)"),
                                                    start=False, stop=True, skip_group_check=True)
                    last.then_inc(scores_done, 1)
                n = s
                if n.real():
                    pe.wait_ge(heads_scaled, n.t + 1)
                    nc.tensor.transpose(misc_ps, heads_out[:, :], ident[:, :]).then_inc(out_turned, 1)
            steps(pe, step, -1, PAIRS)

        @block.scalar
        def _(act):
            def step(s):
                n = s.at(-1)
                if n.real():
                    act.wait_ge(out_turned, n.t + 1)
                    wait(act, projected, n.t)
                    nc.scalar.activation(heads_out_t[:, :], misc_ps, ACT.Copy).then_inc(out_copied, 1)
                n = s
                if n.real():
                    act.wait_ge(turned, n.t + 1)
                    wait(act, pv_done, n.t)
                    nc.scalar.activation(probs_t[:, :, :].rearrange("p c k -> p (c k)"),
                                         turned_ps.rearrange("p c k -> p (c k)"), ACT.Copy).then_inc(turned_copied, 1)
                n = s.at(1)
                if n.real():
                    act.wait_ge(qkv_done, n.t + 1)
                    wait(act, scores_done, n.t)
                    nc.scalar.activation(q_t[:, :], qkv_ps[:, 0:P], ACT.Copy).then_inc(q_copied, 1)
                    act.wait_ge(zeroed, 2)
                    wait(act, pv_done, n.t - 1)
                    for e in range(2):
                        rows = slice(SEQ * e, SEQ * e + SEQ)
                        nc.scalar.activation(v_blocks[n.slot][rows, :, :, e, :],
                                             qkv_ps[rows, 2 * P:4 * P].rearrange("p (b c e r) -> p b c e r",
                                                                                 b=2, c=8, e=2)[:, :, :, e, :],
                                             ACT.Copy).then_inc(v_spread, 1)
                    act.wait_ge(shifted, n.t + 1)
                    nc.scalar.activation(probs[n.slot][:, :, :], probs[n.slot][:, :, :], ACT.Exp).then_inc(exp_done, 1)
            steps(act, step, -1, PAIRS)

        @block.gpsimd
        def _(pool):
            for p in range(2):
                nc.gpsimd.memset(v_blocks[p][:, :, :, :, :].rearrange("p a b c d -> p (a b c d)"), 0.0
                                 ).then_inc(zeroed, 1)

            def step(n):
                pool.wait_ge(mv_done, n.t + 1)
                wait(pool, normed, n.t)
                nc.gpsimd.tensor_tensor(var_eps[:, :], mv[:, 1:2], eps_t[:, 0:1], ALU.add).then_inc(eps_added, 1)
                pool.wait_ge(eps_added, n.t + 1)
                nc.gpsimd.tensor_tensor(rstd[:, :], var_eps[:, :], mhalf[:, 0:1], ALU.pow).then_inc(rstd_done, 1)
            steps(pool, step, 0, PAIRS - 1)

        @block.vector
        def _(dve):
            def step(s):
                n = s.at(-1)
                if n.real():
                    dve.wait_ge(projected, n.t + 1)
                    wait(dve, normed, n.t)
                    nc.vector.tensor_tensor(resid[:, :], x_row[n.slot][:, :], misc_ps, ALU.add).then_inc(resid_done, 1)
                    dve.wait_ge(resid_done, n.t + 1)
                    nc.vector.bn_stats(stats[:, :], resid[:, :]).then_inc(stats_done, 1)
                    wait_apart(dve, stats_done, n.t + 1)
                    nc.vector.bn_aggr(mv[:, :], stats[:, :]).then_inc(mv_done, 1)
                n = s.at(1)
                if n.real():
                    dve.wait_ge(qkv_done, n.t + 1)
                    dve.wait_ge(v_spread, 2 * (n.t + 1))
                    wait(dve, scores_done, n.t)
                    nc.vector.tensor_tensor(
                        k_blocks[:, :, :, :],
                        qkv_ps[:, P:2 * P].rearrange("p (b g k) -> p b g k", b=2, g=1).broadcast_to([P, 2, 4, SEQ]),
                        head_of[:, :].rearrange("p (b g k) -> p b g k", b=1, k=1).broadcast_to([P, 2, 4, SEQ]),
                        ALU.mult).then_inc(k_spread, 1)
                n = s
                if n.real():
                    dve.wait_ge(exp_done, n.t + 1)
                    nc.vector.tensor_reduce(total[:, :], probs[n.slot][:, :, :], AX_X, ALU.add).then_inc(total_done, 1)
                    dve.wait_ge(total_done, n.t + 1)
                    nc.vector.reciprocal(inv[:, :], total[:, :]).then_inc(inv_done, 1)
                n = s.at(-1)
                if n.real():
                    dve.wait_ge(rstd_done, n.t + 1)
                    nc.vector.tensor_scalar(X[:, n.t, :], resid[:, :], mv[:, 0:1], rstd[:, 0:1],
                                            ALU.subtract, ALU.mult).then_inc(normed, 1)
                n = s
                if n.real():
                    dve.wait_ge(inv_done, n.t + 1)
                    dve.wait_ge(pv_done, n.t + 1)
                    wait(dve, out_turned, n.t)
                    nc.vector.tensor_tensor(
                        heads_out[:, :].rearrange("p (h r) -> p h r", h=HEADS),
                        misc_ps.rearrange("p (h r) -> p h r", h=HEADS),
                        inv[:, :].rearrange("p (h r) -> p h r", r=1).broadcast_to([P, HEADS, HD]),
                        ALU.mult).then_inc(heads_scaled, 1)
                n = s.at(1)
                if n.real():
                    dve.wait_ge(scores_done, n.t + 1)
                    heads = scores_ps.rearrange("p j (g k) -> p j g k", g=4)
                    nc.vector.tensor_reduce(top[:, :], heads, AX_X, ALU.max).then_inc(top_done, 1)
                    dve.wait_ge(top_done, n.t + 1)
                    wait(dve, turned, n.t - 1)
                    nc.vector.tensor_tensor(
                        probs[n.slot][:, :, :].rearrange("p (j g) k -> p j g k", g=4), heads,
                        top[:, :].rearrange("p (j g k) -> p j g k", g=4, k=1).broadcast_to([P, 4, 4, SEQ]),
                        ALU.subtract).then_inc(shifted, 1)
            steps(dve, step, -1, PAIRS)
            dve.wait_ge(normed, PAIRS)


def cross_attention(nc, bank, ctx_in, X, gb, fold_a, fold_b, ident, onesb_row, key_mask, eps_t, mhalf):
    GX, BX, GL, BL, GO, BO = range(6)
    UNITS = 4
    with ExitStack() as stack:
        def sb(name, shape, dt=F32):
            return stack.enter_context(nc.sbuf_tensor(name, shape, dt))

        def sem(name):
            return stack.enter_context(nc.semaphore(name))

        c_row = [sb(f"b_ctx{p}", [P, DIM]) for p in range(2)]
        stats = sb("b_stats", [P, 2, 6])
        mv = sb("b_mv", [P, 2, 2])
        var_eps = sb("b_var_eps", [P, 2])
        rstd = sb("b_rstd", [P, 2])
        gained = sb("b_gained", [P, 2, DIM])
        kv = [sb(f"b_kv{p}", [P, 2, DIM]) for p in range(2)]
        kv_t = [sb(f"b_kv_t{p}", [P, 2, P]) for p in range(2)]
        q_t = [sb(f"b_q_t{p}", [P, 2, HEADS, SEQ]) for p in range(2)]
        ntop = [sb(f"b_ntop{p}", [P, 4]) for p in range(2)]
        total = [sb(f"b_total{p}", [P, 4]) for p in range(2)]
        inv = [sb(f"b_inv{p}", [P, 4]) for p in range(2)]
        probs = [sb(f"b_probs{p}", [P, 4, P]) for p in range(2)]
        probs_t = [sb(f"b_probs_t{p}", [P, 512]) for p in range(2)]
        z_t = [sb(f"b_z_t{p}", [P, HEADS, 2, SEQ]) for p in range(2)]
        o_stats = sb("b_o_stats", [P, 2, 6])
        o_mv = sb("b_o_mv", [P, 2, 2])
        o_eps = sb("b_o_eps", [P, 2])
        o_rstd = sb("b_o_rstd", [P, 2])
        o_row = sb("b_o_row", [P, DIM])
        resid = sb("b_resid", [P, DIM])

        loaded = [sem(f"b_loaded{p}") for p in range(2)]
        stats_done = sem("b_stats_done")
        mv_done = sem("b_mv_done")
        eps_added = sem("b_eps_added")
        rstd_done = sem("b_rstd_done")
        gained_done = sem("b_gained_done")
        kv_done = sem("b_kv_done")
        kv_turned = sem("b_kv_turned")
        kv_copied = sem("b_kv_copied")
        q_done = sem("b_q_done")
        q_copied = sem("b_q_copied")
        scores_done = sem("b_scores_done")
        top_done = sem("b_top_done")
        exp_done = sem("b_exp_done")
        inv_done = sem("b_inv_done")
        scaled = sem("b_scaled")
        turned = sem("b_turned")
        turned_copied = sem("b_turned_copied")
        z_done = sem("b_z_done")
        z_copied = sem("b_z_copied")
        y_done = sem("b_y_done")
        o_chain = sem("b_o_chain")
        y_read = sem("b_y_read")
        o_mv_done = sem("b_o_mv_done")
        o_eps_added = sem("b_o_eps_added")
        o_rstd_done = sem("b_o_rstd_done")
        normed = sem("b_normed")

        scores_ps = [bank[:, 0, :], bank[:, 1, :]]
        turned_ps = bank[:, 2, :]
        z_ps = bank[:, 3, :]
        q_ps = bank[:, 4, :]
        y_ps = bank[:, 5, 0:DIM]
        O_CHAIN = 4
        block = stack.enter_context(nc.Block())

        @block.sync
        def _(sp):
            def load(n):
                t, p = n.t, n.slot
                wait(sp, gained_done, 2 * (t - 1))
                wait(sp, stats_done, 2 * (t - 1))
                for b in range(2):
                    sp.dma_start(c_row[p][SEQ * (1 - b):SEQ * (2 - b), :],
                                 ctx_in[bass.ds(t * P + SEQ * b, SEQ), :]).then_inc(loaded[p], 16)
            steps(sp, load, 0, PAIRS - 1)

        @block.tensor
        def _(pe):
            def keys_turn(n):
                if not n.real():
                    return
                pe.wait_ge(kv_done, 4 * (n.t + 1))
                wait(pe, q_copied, 4 * n.t)
                for b in range(2):
                    last = nc.tensor.transpose(q_ps[:, b * P:(b + 1) * P], kv[n.slot][:, b, :], ident[:, :])
                last.then_inc(kv_turned, 1)

            def queries(n, c):
                if not n.real():
                    return
                pe.wait_ge(kv_copied, n.t + 1)
                wait(pe, q_copied, 4 * n.t + c)
                x_tokens = kv_t[n.slot][:, :, :].rearrange("p b (e q) -> p (b e) q", e=2)[:, 0:4:3, :]
                for h in range(4):
                    last = nc.tensor.matmul(q_ps[:, h * P:(h + 1) * P], fold_a[:, 4 * c + h, :], x_tokens,
                                            start=True, stop=True)
                last.then_inc(q_done, 1)

            def scores(n, u):
                if not n.real():
                    return
                b, half = u // 2, u % 2
                wait_apart(pe, q_copied, 4 * n.t + 2 * half + 2)
                wait_apart(pe, exp_done, 4 * (4 * n.t + u - 1))
                ps = scores_ps[u % 2]
                nc.tensor.matmul(ps.rearrange("p (i k) -> p i k", i=4), onesb_row[:, :],
                                 key_mask[:, 2 * n.t + b, :, :].rearrange("a (i c) s -> a i (c s)", i=1)
                                 .broadcast_to([1, 4, P]), start=True, stop=False, skip_group_check=True)
                for i in range(4):
                    h = 8 * half + 2 * i
                    last = nc.tensor.matmul(ps[:, i * P:(i + 1) * P],
                                            q_t[n.slot][:, b, h:h + 2, :].rearrange("p h q -> p (h q)"),
                                            kv_t[n.slot][:, b, :], start=False, stop=True, skip_group_check=True)
                last.then_inc(scores_done, 1)

            def turn(n, u):
                if not n.real():
                    return
                pe.wait_ge(scaled, 4 * n.t + u + 1)
                wait(pe, turned_copied, 4 * n.t + u)
                for i in range(4):
                    last = nc.tensor.transpose(turned_ps[:, i * P:(i + 1) * P], probs[u % 2][:, i, :], ident[:, :])
                last.then_inc(turned, 1)

            def values(n, u):
                if not n.real():
                    return
                pe.wait_ge(turned_copied, 4 * n.t + u + 1)
                wait(pe, z_copied, 4 * n.t + u)
                nc.tensor.matmul(z_ps, kv[n.slot][:, u // 2, :], probs_t[u % 2][:, :],
                                 start=True, stop=True).then_inc(z_done, 1)

            def output(n):
                if not n.real():
                    return
                pe.wait_ge(z_copied, 4 * (n.t + 1))
                wait(pe, y_read, n.t)
                for h in range(HEADS):
                    last = nc.tensor.matmul(y_ps, z_t[n.slot][:, h, :, :].rearrange("p b q -> p (b q)"),
                                            fold_b[:, h, :], start=(h == 0), stop=(h == HEADS - 1))
                last.then_inc(y_done, 1)

            def step(s):
                scores(s, 1)
                turn(s, 0)
                keys_turn(s.at(1))
                values(s, 0)
                scores(s, 2)
                turn(s, 1)
                output(s.at(-1))
                queries(s.at(1), 0)
                values(s, 1)
                scores(s, 3)
                turn(s, 2)
                queries(s.at(1), 1)
                values(s, 2)
                scores(s.at(1), 0)
                turn(s, 3)
                queries(s.at(1), 2)
                values(s, 3)
                queries(s.at(1), 3)
            steps(pe, step, -1, PAIRS)

        @block.scalar
        def _(act):
            def kv_copy(n):
                if not n.real():
                    return
                act.wait_ge(kv_turned, n.t + 1)
                wait(act, scores_done, 4 * (n.t - 1))
                nc.scalar.activation(kv_t[n.slot][:, :, :].rearrange("p b k -> p (b k)"), q_ps[:, 0:2 * P],
                                     ACT.Copy).then_inc(kv_copied, 1)

            def q_copy(n, c):
                if not n.real():
                    return
                act.wait_ge(q_done, 4 * n.t + c + 1)
                wait(act, scores_done, 4 * (n.t - 1))
                nc.scalar.activation(q_t[n.slot][:, :, 4 * c:4 * c + 4, :].rearrange("p b h q -> p h b q"),
                                     q_ps.rearrange("p (h b q) -> p h b q", h=4, b=2), ACT.Copy).then_inc(q_copied, 1)

            def exps(n, u):
                if not n.real():
                    return
                act.wait_ge(top_done, 4 * n.t + u + 1)
                wait(act, turned, 4 * n.t + u - 1)
                wait(act, inv_done, 4 * n.t + u - 1)
                for i in range(4):
                    nc.scalar.activation(probs[u % 2][:, i, :], scores_ps[u % 2][:, i * P:(i + 1) * P], ACT.Exp,
                                         bias=ntop[u % 2][:, i:i + 1],
                                         accum_out=total[u % 2][:, i:i + 1]).then_inc(exp_done, 1)

            def step(s):
                exps(s, 1)
                kv_copy(s.at(1))
                exps(s, 2)
                q_copy(s.at(1), 0)
                exps(s, 3)
                q_copy(s.at(1), 1)
                exps(s.at(1), 0)
                q_copy(s.at(1), 2)
                q_copy(s.at(1), 3)
            steps(act, step, -1, PAIRS)

        @block.gpsimd
        def _(pool):
            def input_rstd(n):
                if not n.real():
                    return
                pool.wait_ge(mv_done, 2 * (n.t + 1))
                wait(pool, kv_done, 4 * n.t)
                nc.gpsimd.tensor_tensor(var_eps[:, :], mv[:, :, 1], eps_t[:, :], ALU.add).then_inc(eps_added, 1)
                pool.wait_ge(eps_added, n.t + 1)
                nc.gpsimd.tensor_tensor(rstd[:, :], var_eps[:, :], mhalf[:, :], ALU.pow).then_inc(rstd_done, 1)

            def output_rstd(n, k):
                if not n.real():
                    return
                pool.wait_ge(o_mv_done, 2 * n.t + k + 1)
                nc.gpsimd.tensor_tensor(o_eps[:, k:k + 1], o_mv[:, k, 1:2], eps_t[:, 0:1],
                                        ALU.add).then_inc(o_eps_added, 1)
                pool.wait_ge(o_eps_added, 2 * n.t + k + 1)
                nc.gpsimd.tensor_tensor(o_rstd[:, k:k + 1], o_eps[:, k:k + 1], mhalf[:, 0:1],
                                        ALU.pow).then_inc(o_rstd_done, 1)

            def scale(n, u):
                if not n.real():
                    return
                pool.wait_ge(exp_done, 4 * (4 * n.t + u + 1))
                pool.wait_ge(inv_done, 4 * n.t + u + 1)
                nc.gpsimd.tensor_tensor(
                    probs[u % 2][:, :, :], probs[u % 2][:, :, :],
                    inv[u % 2][:, :].rearrange("p (i k) -> p i k", k=1).broadcast_to([P, 4, P]),
                    ALU.mult).then_inc(scaled, 1)

            def step(s):
                scale(s, 1)
                output_rstd(s.at(-1), 0)
                scale(s, 2)
                output_rstd(s.at(-1), 1)
                input_rstd(s.at(2))
                scale(s, 3)
                scale(s.at(1), 0)
            input_rstd(Pair(0, 0))
            steps(pool, step, -1, PAIRS, ahead=2)

        @block.vector
        def _(dve):
            def input_stats(n):
                if not n.real():
                    return
                dve.wait_ge(loaded[n.slot], 32 * (n.turn + 1))
                nc.vector.bn_stats(stats[:, 0, :], X[:, n.t, :]).then_inc(stats_done, 1)
                nc.vector.bn_stats(stats[:, 1, :], c_row[n.slot][:, :]).then_inc(stats_done, 1)
                wait_apart(dve, stats_done, 2 * n.t + 2)
                wait_apart(dve, rstd_done, n.t)
                for k in range(2):
                    nc.vector.bn_aggr(mv[:, k, :], stats[:, k, :]).then_inc(mv_done, 1)

            def input_norm(n):
                if not n.real():
                    return
                dve.wait_ge(mv_done, 2 * (n.t + 1))
                wait(dve, kv_done, 4 * n.t)
                for k, (src, g) in enumerate(((X[:, n.t, :], GL), (c_row[n.slot][:, :], GX))):
                    nc.vector.scalar_tensor_tensor(gained[:, k, :], src, mv[:, k, 0:1], gb[:, g, :],
                                                   ALU.subtract, ALU.mult).then_inc(gained_done, 1)
                dve.wait_ge(gained_done, 2 * (n.t + 1))
                dve.wait_ge(rstd_done, n.t + 1)
                wait(dve, z_done, 4 * (n.t - 1))
                wait(dve, kv_turned, n.t - 1)
                for k, bias in ((0, BL), (1, BX)):
                    for e in range(2):
                        rows = slice(SEQ * e, SEQ * e + SEQ)
                        nc.vector.scalar_tensor_tensor(kv[n.slot][rows, e ^ k, :], gained[rows, k, :],
                                                       rstd[rows, k:k + 1], gb[rows, bias, :],
                                                       ALU.mult, ALU.add).then_inc(kv_done, 1)

            def tops(n, u):
                if not n.real():
                    return
                dve.wait_ge(scores_done, 4 * n.t + u + 1)
                wait(dve, exp_done, 4 * (4 * n.t + u - 1))
                nc.vector.tensor_reduce(ntop[u % 2][:, :], scores_ps[u % 2].rearrange("p (i k) -> p i k", i=4),
                                        AX_X, ALU.max, negate=True).then_inc(top_done, 1)

            def invert(n, u):
                if not n.real():
                    return
                dve.wait_ge(exp_done, 4 * (4 * n.t + u + 1))
                wait(dve, scaled, 4 * n.t + u - 1)
                nc.vector.reciprocal(inv[u % 2][:, :], total[u % 2][:, :]).then_inc(inv_done, 1)

            def turn_copy(n, u):
                if not n.real():
                    return
                dve.wait_ge(turned, 4 * n.t + u + 1)
                wait(dve, z_done, 4 * n.t + u - 1)
                nc.vector.tensor_copy(probs_t[u % 2][:, :], turned_ps).then_inc(turned_copied, 1)

            def z_copy(n, u):
                if not n.real():
                    return
                b, half = u // 2, u % 2
                dve.wait_ge(z_done, 4 * n.t + u + 1)
                wait(dve, y_done, n.t - 1)
                nc.vector.tensor_copy(z_t[n.slot][:, 8 * half:8 * half + 8, b, :],
                                      z_ps.rearrange("p (h q) -> p h q", h=8)).then_inc(z_copied, 1)

            def out_stats(n):
                if not n.real():
                    return
                dve.wait_ge(y_done, n.t + 1)
                nc.vector.bn_stats(o_stats[:, 0, :], y_ps).then_inc(o_chain, 1)
                wait_apart(dve, o_chain, O_CHAIN * n.t + 1)
                nc.vector.bn_aggr(o_mv[:, 0, :], o_stats[:, 0, :]).then_inc(o_mv_done, 1)
                dve.wait_ge(o_mv_done, 2 * n.t + 1)
                nc.vector.scalar_tensor_tensor(o_row[:, :], y_ps, o_mv[:, 0, 0:1], gb[:, GO, :],
                                               ALU.subtract, ALU.mult).then_inc(y_read, 1)

            def out_resid(n):
                if not n.real():
                    return
                dve.wait_ge(o_rstd_done, 2 * n.t + 1)
                dve.wait_ge(y_read, n.t + 1)
                nc.vector.scalar_tensor_tensor(resid[:, :], o_row[:, :], o_rstd[:, 0:1], gb[:, BO, :],
                                               ALU.mult, ALU.add).then_inc(o_chain, 1)
                dve.wait_ge(o_chain, O_CHAIN * n.t + 2)
                nc.vector.tensor_tensor(resid[:, :], resid[:, :], X[:, n.t, :], ALU.add).then_inc(o_chain, 1)
                dve.wait_ge(o_chain, O_CHAIN * n.t + 3)
                nc.vector.bn_stats(o_stats[:, 1, :], resid[:, :]).then_inc(o_chain, 1)
                wait_apart(dve, o_chain, O_CHAIN * n.t + 4)
                nc.vector.bn_aggr(o_mv[:, 1, :], o_stats[:, 1, :]).then_inc(o_mv_done, 1)

            def out_norm(n):
                if not n.real():
                    return
                dve.wait_ge(o_rstd_done, 2 * n.t + 2)
                nc.vector.tensor_scalar(X[:, n.t, :], resid[:, :], o_mv[:, 1, 0:1], o_rstd[:, 1:2],
                                        ALU.subtract, ALU.mult).then_inc(normed, 1)

            def step(s):
                tops(s, 1)
                turn_copy(s, 0)
                input_stats(s.at(2))
                z_copy(s, 0)
                tops(s, 2)
                invert(s, 1)
                turn_copy(s, 1)
                out_stats(s.at(-1))
                z_copy(s, 1)
                tops(s, 3)
                invert(s, 2)
                out_resid(s.at(-1))
                turn_copy(s, 2)
                z_copy(s, 2)
                tops(s.at(1), 0)
                invert(s, 3)
                out_norm(s.at(-1))
                turn_copy(s, 3)
                input_norm(s.at(2))
                z_copy(s, 3)
                invert(s.at(1), 0)
            input_stats(Pair(0, 0))
            input_norm(Pair(0, 0))
            steps(dve, step, -1, PAIRS, ahead=2)
            dve.wait_ge(normed, PAIRS)


def expert_ffn(nc, bank, X, fold_g, hid_w, out_w, last_row, table, rev_key, rev_row, ident, eps_t, mhalf, out):
    SLOTS = FH + 1
    with ExitStack() as stack:
        def sb(name, shape, dt=F32):
            return stack.enter_context(nc.sbuf_tensor(name, shape, dt))

        def sem(name):
            return stack.enter_context(nc.semaphore(name))

        x_t = sb("c_x_t", [P, P])
        best = sb("c_best", [P, 2 * FH])
        row_hit = sb("c_row_hit", [P, FH, XROWS])
        row_code = sb("c_row_code", [P, FH])
        row_base = sb("c_row_base", [P, FH])
        key_hit = sb("c_key_hit", [P, FH, KEYS])
        key_code = sb("c_key_code", [P, FH])
        index_f = sb("c_index_f", [P, FH])
        index = [sb(f"c_index{p}", [P, FH], U32) for p in range(2)]
        gate_sum = sb("c_gate_sum", [P, FH])
        gate_all = sb("c_gate_all", [P, FH])
        gate_out = sb("c_gate_out", [P, FH])
        gate = [sb(f"c_gate{p}", [P, SLOTS]) for p in range(2)]
        rows = [sb(f"c_rows{p}", [P, FH, TABLE]) for p in range(2)]
        lin = sb("c_lin", [P, SLOTS])
        lin_g = sb("c_lin_g", [P, SLOTS])
        prod = sb("c_prod", [P, FFN])
        hidden = sb("c_hidden", [P, FFN])
        act_h = sb("c_act_h", [P, FFN])
        act_t = sb("c_act_t", [P, 2, P])
        lout = sb("c_lout", [P, SLOTS])
        lout_g = sb("c_lout_g", [P, SLOTS])
        resid = sb("c_resid", [P, DIM])
        stats = sb("c_stats", [P, 6])
        mv = sb("c_mv", [P, 2])
        var_eps = sb("c_var_eps", [P, 1])
        rstd = sb("c_rstd", [P, 1])
        result = [sb(f"c_result{p}", [P, DIM]) for p in range(2)]

        x_staged = sem("c_x_staged")
        x_turned = sem("c_x_turned")
        x_copied = sem("c_x_copied")
        sims_done = sem("c_sims_done")
        best_done = sem("c_best_done")
        route = sem("c_route")
        sims_read = sem("c_sims_read")
        index_done = sem("c_index_done")
        gate_done = sem("c_gate_done")
        rows_zeroed = sem("c_rows_zeroed")
        gathered = [sem(f"c_gathered{p}") for p in range(2)]
        hid_done = sem("c_hid_done")
        lin_done = sem("c_lin_done")
        lin_g_done = sem("c_lin_g_done")
        hidden_step = sem("c_hidden_step")
        gelu_done = sem("c_gelu_done")
        act_turned = sem("c_act_turned")
        act_copied = sem("c_act_copied")
        out_done = sem("c_out_done")
        lout_done = sem("c_lout_done")
        lout_g_done = sem("c_lout_g_done")
        resid_step = sem("c_resid_step")
        stats_done = sem("c_stats_done")
        mv_done = sem("c_mv_done")
        eps_added = sem("c_eps_added")
        rstd_done = sem("c_rstd_done")
        result_done = sem("c_result_done")
        stored = [sem(f"c_stored{p}") for p in range(2)]

        sims_ps = bank[:, 0:4, :]
        hid_ps = bank[:, 4, 0:FFN + 2]
        x_turn_ps = bank[:, 5, 0:P]
        act_turn_ps = bank[:, 6, 0:2 * P]
        out_ps = bank[:, 7, 0:DIM]
        ROUTE = 7
        RESID = SLOTS + 1
        x_now = [sb(f"c_x_now{p}", [P, DIM]) for p in range(2)]
        block = stack.enter_context(nc.Block())

        @block.sync
        def _(sp):
            def store(n):
                sp.wait_ge(result_done, n.t + 1)
                sp.dma_start(out[bass.ds(n.t * P, P), :], result[n.slot][:, :]).then_inc(stored[n.slot], 16)
            steps(sp, store, 0, PAIRS - 1)
            for p in range(2):
                sp.wait_ge(stored[p], 16 * (PAIRS // 2))

        @block.tensor
        def _(pe):
            def route_products(n):
                if not n.real():
                    return
                pe.wait_ge(x_staged, n.t + 1)
                wait(pe, x_copied, n.t)
                nc.tensor.transpose(x_turn_ps, x_now[n.slot][:, :], ident[:, :]).then_inc(x_turned, 1)
                pe.wait_ge(x_copied, n.t + 1)
                wait(pe, sims_read, 9 * n.t)
                for c in range(4):
                    last = nc.tensor.matmul(sims_ps[:, c, :], x_t[:, :],
                                            fold_g[:, 4 * c:4 * c + 4, :].rearrange("p h k -> p (h k)"),
                                            start=True, stop=True)
                last.then_inc(sims_done, 1)
                wait(pe, hidden_step, SLOTS * n.t)
                wait(pe, lin_done, SLOTS * n.t)
                nc.tensor.matmul(hid_ps, x_t[:, :], hid_w[:, :], start=True, stop=True).then_inc(hid_done, 1)

            def output_product(n):
                if not n.real():
                    return
                pe.wait_ge(gelu_done, n.t + 1)
                wait(pe, act_copied, n.t)
                for c in range(2):
                    last = nc.tensor.transpose(act_turn_ps[:, c * P:(c + 1) * P], act_h[:, c * P:(c + 1) * P], ident[:, :])
                last.then_inc(act_turned, 1)
                pe.wait_ge(act_copied, n.t + 1)
                wait(pe, resid_step, RESID * (n.t - 1) + 1 if not isinstance(n.t, int) or n.t else 0)
                for c in range(2):
                    last = nc.tensor.matmul(out_ps, act_t[:, c, :], out_w[:, c, :], start=(c == 0), stop=(c == 1))
                last.then_inc(out_done, 1)

            def step(s):
                route_products(s.at(1))
                output_product(s)
            steps(pe, step, -1, PAIRS)

        @block.scalar
        def _(act):
            def step(s):
                n = s.at(1)
                if n.real():
                    act.wait_ge(x_turned, n.t + 1)
                    wait(act, hid_done, n.t)
                    nc.scalar.activation(x_t[:, :], x_turn_ps, ACT.Copy).then_inc(x_copied, 1)
                n = s
                if n.real():
                    act.wait_ge(hidden_step, SLOTS * (n.t + 1))
                    wait(act, lout_done, SLOTS * n.t)
                    wait(act, act_turned, n.t)
                    nc.scalar.activation(act_h[:, :], hidden[:, :], ACT.Gelu).then_inc(gelu_done, 1)
                    act.wait_ge(act_turned, n.t + 1)
                    wait(act, out_done, n.t)
                    nc.scalar.activation(act_t[:, :, :].rearrange("p c k -> p (c k)"), act_turn_ps,
                                         ACT.Copy).then_inc(act_copied, 1)
            steps(act, step, -1, PAIRS)

        @block.gpsimd
        def _(pool):
            for p in range(2):
                nc.gpsimd.memset(rows[p][:, :, :].rearrange("p h c -> p (h c)"), 0.0).then_inc(rows_zeroed, 1)
            pool.wait_ge(rows_zeroed, 2)
            in_table = nc.gpsimd.to_reg(LAST - 1)

            def gather(n):
                if not n.real():
                    return
                wait_apart(pool, index_done, n.t + 1)
                wait_apart(pool, resid_step, RESID * (n.t - 1))
                for h in range(FH):
                    nc.gpsimd.indirect_dma_start(
                        out=rows[n.slot][:, h, :], out_offset=None, in_=table,
                        in_offset=bass.IndirectOffsetOnAxis(ap=index[n.slot][:, h:h + 1], axis=0),
                        bounds_check=in_table, oob_is_err=False).then_inc(gathered[n.slot], 16)

            def out_rstd(n):
                if not n.real():
                    return
                pool.wait_ge(mv_done, n.t + 1)
                wait(pool, result_done, n.t)
                nc.gpsimd.tensor_tensor(var_eps[:, :], mv[:, 1:2], eps_t[:, 0:1], ALU.add).then_inc(eps_added, 1)
                pool.wait_ge(eps_added, n.t + 1)
                nc.gpsimd.tensor_tensor(rstd[:, :], var_eps[:, :], mhalf[:, 0:1], ALU.pow).then_inc(rstd_done, 1)

            def step(s):
                gather(s.at(1))
                out_rstd(s)
            steps(pool, step, -1, PAIRS)

        @block.vector
        def _(dve):
            def stage_x(n):
                if not n.real():
                    return
                wait(dve, x_turned, n.t - 1)
                wait(dve, resid_step, RESID * (n.t - 2) + 1 if not isinstance(n.t, int) or n.t > 1 else 0)
                nc.vector.tensor_copy(x_now[n.slot][:, :], X[:, n.t, :]).then_inc(x_staged, 1)

            def routing(n):
                if not n.real():
                    return
                k = ROUTE * n.t
                sims = sims_ps.rearrange("p c (h k) -> p (c h) k", k=KEYS)
                dve.wait_ge(sims_done, n.t + 1)
                nc.vector.tensor_reduce(best[:, :], sims, AX_X, ALU.max).then_inc(best_done, 1)
                dve.wait_ge(best_done, n.t + 1)
                nc.vector.tensor_tensor(row_hit[:, :, :], sims[:, 0:FH, 0:XROWS],
                                        best[:, 0:FH].rearrange("p (h k) -> p h k", k=1).broadcast_to([P, FH, XROWS]),
                                        ALU.is_equal).then_inc(sims_read, 1)
                for h in range(FH):
                    nc.vector.scalar_tensor_tensor(key_hit[:, h, :], sims[:, FH + h, :], best[:, FH + h:FH + h + 1],
                                                   rev_key[:, :], ALU.is_equal, ALU.mult).then_inc(sims_read, 1)
                dve.wait_ge(sims_read, 9 * n.t + 1)
                nc.vector.tensor_tensor(row_hit[:, :, :], row_hit[:, :, :],
                                        rev_row[:, :].rearrange("p (h k) -> p h k", h=1).broadcast_to([P, FH, XROWS]),
                                        ALU.mult).then_inc(route, 1)
                dve.wait_ge(sims_read, 9 * n.t + 9)
                nc.vector.tensor_reduce(key_code[:, :], key_hit[:, :, :], AX_X, ALU.max).then_inc(route, 1)
                dve.wait_ge(route, k + 1)
                nc.vector.tensor_reduce(row_code[:, :], row_hit[:, :, :], AX_X, ALU.max).then_inc(route, 1)
                nc.vector.tensor_tensor(gate_sum[:, :], best[:, 0:FH], best[:, FH:2 * FH], ALU.add).then_inc(route, 1)
                dve.wait_ge(route, k + 3)
                nc.vector.tensor_scalar(row_base[:, :], row_code[:, :], -float(KEYS), float((XROWS + 1) * KEYS),
                                        ALU.mult, ALU.add).then_inc(route, 1)
                dve.wait_ge(route, k + 5)
                nc.vector.tensor_tensor(index_f[:, :], row_base[:, :], key_code[:, :], ALU.subtract).then_inc(route, 1)
                nc.vector.tensor_scalar(gate_all[:, :], gate_sum[:, :], 0.0, None, ALU.max).then_inc(route, 1)
                dve.wait_ge(route, k + 7)
                wait(dve, gathered[n.slot], 16 * FH * n.turn)
                nc.vector.tensor_copy(index[n.slot][:, :], index_f[:, :]).then_inc(index_done, 1)
                wait(dve, lout_g_done, n.t - 1)
                nc.vector.scalar_tensor_tensor(gate[n.slot][:, 0:FH], index_f[:, :], float(LAST) - 0.5, gate_all[:, :],
                                               ALU.is_le, ALU.mult).then_inc(gate_done, 1)
                dve.wait_ge(gate_done, 3 * n.t + 1)
                nc.vector.tensor_tensor(gate_out[:, :], gate_all[:, :], gate[n.slot][:, 0:FH],
                                        ALU.subtract).then_inc(gate_done, 1)
                dve.wait_ge(gate_done, 3 * n.t + 2)
                nc.vector.tensor_reduce(gate[n.slot][:, FH:SLOTS], gate_out[:, :], AX_X, ALU.add).then_inc(gate_done, 1)

            def expert_in(n):
                if not n.real():
                    return
                r = rows[n.slot]
                dve.wait_ge(hid_done, n.t + 1)
                dve.wait_ge(gathered[n.slot], 16 * FH * (n.turn + 1))
                nc.vector.tensor_copy(lin[:, FH:SLOTS], hid_ps[:, FFN:FFN + 1]).then_inc(lin_done, 1)
                for h in range(FH):
                    if h:
                        dve.wait_ge(lin_done, SLOTS * n.t + 1 + h)
                    nc.vector.tensor_tensor_reduce(prod[:, 0:DIM], x_now[n.slot][:, :], r[:, h, A_IN:A_IN + DIM], 1.0, 0.0,
                                                   ALU.mult, ALU.add, lin[:, h:h + 1]).then_inc(lin_done, 1)
                dve.wait_ge(lin_done, SLOTS * (n.t + 1))
                dve.wait_ge(gate_done, 3 * (n.t + 1))
                nc.vector.tensor_tensor(lin_g[:, :], lin[:, :], gate[n.slot][:, :], ALU.mult).then_inc(lin_g_done, 1)
                dve.wait_ge(lin_g_done, n.t + 1)
                wait(dve, gelu_done, n.t)
                for h in range(SLOTS):
                    weights = r[:, h, B_IN:B_IN + FFN] if h < FH else last_row[:, B_IN:B_IN + FFN]
                    if h:
                        dve.wait_ge(hidden_step, SLOTS * n.t + h)
                    nc.vector.scalar_tensor_tensor(hidden[:, :], weights, lin_g[:, h:h + 1],
                                                   hidden[:, :] if h else hid_ps[:, 0:FFN],
                                                   ALU.mult, ALU.add).then_inc(hidden_step, 1)

            def expert_out(n):
                if not n.real():
                    return
                r = rows[n.slot]
                dve.wait_ge(gelu_done, n.t + 1)
                for h in range(SLOTS):
                    weights = r[:, h, A_OUT:A_OUT + FFN] if h < FH else last_row[:, A_OUT:A_OUT + FFN]
                    if h:
                        dve.wait_ge(lout_done, SLOTS * n.t + h)
                    nc.vector.tensor_tensor_reduce(prod[:, :], act_h[:, :], weights, 1.0, 0.0,
                                                   ALU.mult, ALU.add, lout[:, h:h + 1]).then_inc(lout_done, 1)
                dve.wait_ge(lout_done, SLOTS * (n.t + 1))
                nc.vector.tensor_tensor(lout_g[:, :], lout[:, :], gate[n.slot][:, :], ALU.mult).then_inc(lout_g_done, 1)
                dve.wait_ge(out_done, n.t + 1)
                wait(dve, result_done, n.t)
                nc.vector.tensor_tensor(resid[:, :], x_now[n.slot][:, :], out_ps, ALU.add).then_inc(resid_step, 1)
                dve.wait_ge(lout_g_done, n.t + 1)
                for h in range(SLOTS):
                    weights = r[:, h, B_OUT:B_OUT + DIM] if h < FH else last_row[:, B_OUT:B_OUT + DIM]
                    dve.wait_ge(resid_step, RESID * n.t + 1 + h)
                    nc.vector.scalar_tensor_tensor(resid[:, :], weights, lout_g[:, h:h + 1], resid[:, :],
                                                   ALU.mult, ALU.add).then_inc(resid_step, 1)
                dve.wait_ge(resid_step, RESID * (n.t + 1))
                nc.vector.bn_stats(stats[:, :], resid[:, :]).then_inc(stats_done, 1)
                wait_apart(dve, stats_done, n.t + 1)
                nc.vector.bn_aggr(mv[:, :], stats[:, :]).then_inc(mv_done, 1)
                dve.wait_ge(rstd_done, n.t + 1)
                wait(dve, stored[n.slot], 16 * n.turn)
                nc.vector.tensor_scalar(result[n.slot][:, :], resid[:, :], mv[:, 0:1], rstd[:, 0:1],
                                        ALU.subtract, ALU.mult).then_inc(result_done, 1)

            def step(s):
                stage_x(s.at(1))
                expert_in(s)
                routing(s.at(1))
                expert_out(s)
            steps(dve, step, -1, PAIRS)


def kernel(**inputs):
    import numpy as np
    import concourse.bacc as bacc
    from concourse.bass_utils import run_bass_kernel_spmd

    a = {k: np.asarray(v) for k, v in inputs.items()}

    def cat(*names, axis=-1):
        return np.concatenate([a[n] for n in names], axis=axis)

    def turned(m):
        return np.ascontiguousarray(m.T)

    wkv = a["L0_xattn_Wkv"]
    host = {
        "x": a["x"].reshape(BATCH * SEQ, DIM),
        "xT": turned(a["x"].reshape(BATCH * SEQ, DIM)),
        "ctx": a["ctx_1024"].reshape(BATCH * SEQ, DIM),
        "mask": a["mask_BxS2_bf1"].view(np.uint8),
        "w_attn": cat("L0_attn_W_qkv", "L0_attn_W_proj"),
        "u_attn": cat("L0_attn_u_qkv", "L0_attn_u_proj"),
        "sig_qkv": a["L0_attn_sigma_qkv"],
        "sig_proj": a["L0_attn_sigma_proj"],
        "gains": cat("L0_xattn_g_x", "L0_xattn_b_x", "L0_xattn_g_l", "L0_xattn_b_l", "L0_xattn_g_o", "L0_xattn_b_o"),
        "wq_t": turned(a["L0_xattn_Wq"]),
        "wk_t": turned(wkv[:, :INNER]),
        "wv_t": turned(wkv[:, INNER:]),
        "wout": a["L0_xattn_Wout"],
        "ffn_wq": a["L0_ffn_Wq"],
        "keys_t": a["L0_ffn_keys"].transpose(2, 0, 3, 1).reshape(2 * FH * XH, KEYS),
        "w_in_t": turned(a["L0_ffn_W_in"]),
        "w_out_t": turned(a["L0_ffn_W_out"]),
        "table": cat("L0_ffn_in_a", "L0_ffn_in_b", "L0_ffn_out_a", "L0_ffn_out_b"),
    }
    nc = bacc.Bacc("TRN2", target_bir_lowering=False, num_devices=1)
    arrays, args = {}, []
    for name, value in host.items():
        value = np.ascontiguousarray(value)
        arrays[f"in_{name}"] = value
        args.append(nc.dram_tensor(f"in_{name}", value.shape, mybir.dt.from_np(value.dtype), kind="ExternalInput").ap())
    out = nc.dram_tensor("result", (BATCH * SEQ, DIM), F32, kind="ExternalOutput").ap()
    decoder_layer(nc, *args, out)
    r = run_bass_kernel_spmd(nc, [arrays], core_ids=[0])
    return r.results[0]["result"].reshape(BATCH, SEQ, DIM)
```

```python
from contextlib import ExitStack

import concourse.bass as bass
from concourse import mybir

ALU = mybir.AluOpType
ACT = mybir.ActivationFunctionType
AX_X = mybir.AxisListType.X
F32 = mybir.dt.float32
BF16 = mybir.dt.bfloat16
U32 = mybir.dt.uint32
U8 = mybir.dt.uint8

P = 128
BATCH, SEQ, DIM = 128, 64, 128
PAIRS = BATCH // 2
HEADS = 16
HD = DIM // HEADS
XH = 64
INNER = HEADS * XH
EPS = 1e-5
NEG = -1e30
FH = 8
KEYS = 128
EXPERTS = 2048
LAST = EXPERTS - 1
XROWS = EXPERTS // KEYS
FFN = 2 * DIM
TABLE = 2 * DIM + 2 * FFN
A_IN, B_IN, A_OUT, B_OUT = 0, DIM, DIM + FFN, DIM + 2 * FFN


class Pair:

    def __init__(self, base, off):
        self.base, self.off = base, off
        self.t = 2 * base + off
        self.slot = off % 2
        self.turn = base + off // 2

    def at(self, d):
        return Pair(self.base, self.off + d)

    def real(self):
        return not isinstance(self.t, int) or 0 <= self.t < PAIRS


def wait(eng, sem, value):
    if isinstance(value, int) and value <= 0:
        return
    eng.wait_ge(sem, value)


def wait_apart(eng, sem, value):
    if isinstance(value, int):
        return wait(eng, sem, value)
    eng.wait_ge(sem, value)
    eng.nop(nofuse=True)


def steps(eng, body, first, last, ahead, behind):
    peeled = behind + 3
    for s in range(first, peeled):
        body(Pair(0, s))
    turns = (PAIRS - ahead - peeled) // 2
    with eng.Fori(0, turns) as i:
        body(Pair(i, peeled))
        body(Pair(i, peeled + 1))
    for s in range(2 * turns + peeled, last + 1):
        body(Pair(0, s))


def decoder_layer(nc, x, xT, ctx_in, mask, w_attn, u_attn, sig_qkv, sig_proj,
                  gains, wq_t, wk_t, wv_t, wout, ffn_wq, keys_t, w_in_t, w_out_t, table, out):
    with ExitStack() as stack:
        def sb(name, shape, dt=F32):
            return stack.enter_context(nc.sbuf_tensor(name, shape, dt))

        def sem(name):
            return stack.enter_context(nc.semaphore(name))

        bank = stack.enter_context(nc.psum_tensor("bank", [P, 8, 512], F32))

        ident = sb("ident", [P, P])
        identb = sb("identb", [P, P], BF16)
        ones_row = sb("ones_row", [1, P])
        onesb_row = sb("onesb_row", [1, P], BF16)
        causal = sb("causal", [P, 4, SEQ], BF16)
        head_of = sb("head_of", [P, 4])
        key_mask = sb("key_mask", [1, BATCH, SEQ], BF16)
        kv_gb = sb("kv_gb", [P, 2, 2, DIM])
        eps_t = sb("eps_t", [P, 2])
        mhalf = sb("mhalf", [P, 2])
        rev_row = sb("rev_row", [P, XROWS])
        gb = sb("gb", [P, 6, DIM])
        w_self = sb("w_self", [P, 4 * DIM])
        fold_a = sb("fold_a", [P, HEADS, DIM])
        fold_b = sb("fold_b", [P, HEADS, DIM])
        fold_g = sb("fold_g", [P, HEADS, KEYS])
        hid_w = sb("hid_w", [P, FFN + 2])
        out_w = sb("out_w", [P, 2, DIM])
        last_row = sb("last_row", [P, TABLE])
        X = sb("X", [P, PAIRS, DIM])

        GX, BX, GL, BL, GO, BO = range(6)

        consts_ready = sem("consts_ready")
        const_step = sem("const_step")
        weights_in = sem("weights_in")
        fold_in = sem("fold_in")
        norm_a = sem("norm_a")
        norm_row = sem("norm_row")
        norm_copied = sem("norm_copied")
        norm_sq = sem("norm_sq")
        norm_pow = sem("norm_pow")
        norm_c = sem("norm_c")
        norm_cb = sem("norm_cb")
        self_ready = sem("self_ready")
        fold_done = sem("fold_done")
        fold_copied = sem("fold_copied")
        mask_ready = sem("mask_ready")

        with ExitStack() as prep:
            def prep_sb(name, shape, dt=F32):
                return prep.enter_context(nc.sbuf_tensor(name, shape, dt))

            factors = prep_sb("factors", [P, 6, 8, DIM])
            rows_i = prep_sb("rows_i", [P, KEYS], mybir.dt.int32)
            mask_u8 = prep_sb("mask_u8", [1, BATCH, SEQ], U8)
            u_self = prep_sb("u_self", [P, 4 * DIM])
            wu = prep_sb("wu", [P, 4 * DIM])
            a_self = prep_sb("a_self", [P, 2])
            row_self = prep_sb("row_self", [1, 4 * DIM])
            row_sq = prep_sb("row_sq", [1, 4 * DIM])
            norms = prep_sb("norms", [1, 4])
            norms_p = prep_sb("norms_p", [1, 4])
            powers = prep_sb("powers", [1, 4])
            sigmas = prep_sb("sigmas", [1, 2])
            c_row = prep_sb("c_row", [1, 2])
            c_all = prep_sb("c_all", [P, 2])

            block = prep.enter_context(nc.Block())

            @block.sync
            def _(sp):
                sp.dma_start(w_self[:, :], w_attn).then_inc(weights_in, 16)
                sp.dma_start(u_self[:, :], u_attn.partition_broadcast(P)).then_inc(weights_in, 16)
                sp.dma_start(sigmas[:, 0:1], sig_qkv.rearrange("(a n) -> a n", a=1)).then_inc(weights_in, 16)
                sp.dma_start(sigmas[:, 1:2], sig_proj.rearrange("(a n) -> a n", a=1)).then_inc(weights_in, 16)
                sp.dma_start(mask_u8[:, :, :], mask.rearrange("(a b) s -> a b s", a=1)).then_inc(weights_in, 16)
                for n, w in enumerate((wq_t, wk_t, wv_t, wout, ffn_wq, keys_t)):
                    sp.dma_start(factors[:, n, :, :], w.rearrange("(c p) d -> p c d", p=P)).then_inc(fold_in, 16)
                sp.dma_start(gb[:, :, :].rearrange("p a b -> p (a b)"), gains.partition_broadcast(P)).then_inc(weights_in, 16)
                sp.dma_start(hid_w[:, 0:FFN], w_in_t).then_inc(weights_in, 16)
                sp.dma_start(hid_w[:, FFN:FFN + 1], table[LAST, A_IN:A_IN + DIM].rearrange("(p a) -> p a", a=1)).then_inc(weights_in, 16)
                sp.dma_start(hid_w[:, FFN + 1:FFN + 2], table[LAST, A_IN:A_IN + DIM].rearrange("(p a) -> p a", a=1)).then_inc(weights_in, 16)
                sp.dma_start(out_w[:, :, :], w_out_t.rearrange("(c p) d -> p c d", p=P)).then_inc(weights_in, 16)
                sp.dma_start(last_row[:, :], table[LAST, :].partition_broadcast(P)).then_inc(weights_in, 16)
                sp.wait_ge(weights_in, 11 * 16)
                sp.wait_ge(fold_in, 6 * 16)

            @block.gpsimd
            def _(pool):
                made = 0

                def settle(instruction):
                    nonlocal made
                    made += 1
                    instruction.then_inc(const_step, 1)
                    pool.wait_ge(const_step, made)

                settle(nc.gpsimd.memset(ident[:, :], 0.0))
                settle(nc.gpsimd.affine_select(out=ident[:, :], in_=ident[:, :], compare_op=ALU.not_equal, fill=1.0,
                                               base=0, pattern=[[-1, P]], channel_multiplier=1))
                settle(nc.gpsimd.iota(rows_i[:, :], pattern=[[-1, KEYS]], base=KEYS, channel_multiplier=0))
                settle(nc.gpsimd.memset(powers[:, 0:2], 0.5))
                settle(nc.gpsimd.memset(powers[:, 2:4], -0.5))
                settle(nc.gpsimd.memset(eps_t[:, :], EPS))
                settle(nc.gpsimd.memset(mhalf[:, :], -0.5))
                settle(nc.gpsimd.memset(causal[:, :, :], 0.0))
                for b in range(2):
                    half = causal[SEQ * b:SEQ * b + SEQ, :, :]
                    settle(nc.gpsimd.affine_select(out=half, in_=half, compare_op=ALU.is_ge, fill=NEG, base=0,
                                                   pattern=[[0, 4], [-1, SEQ]], channel_multiplier=1))
                settle(nc.gpsimd.memset(head_of[:, :], 1.0))
                for j in range(4):
                    quad = head_of[32 * j:32 * j + 32, :]
                    settle(nc.gpsimd.affine_select(out=quad, in_=quad, compare_op=ALU.is_ge, fill=0.0, base=0,
                                                   pattern=[[-HD, 4]], channel_multiplier=1))
                    settle(nc.gpsimd.affine_select(out=quad, in_=quad, compare_op=ALU.is_ge, fill=0.0, base=HD - 1,
                                                   pattern=[[HD, 4]], channel_multiplier=-1))
                pool.wait_ge(norm_sq, 4)
                nc.gpsimd.tensor_tensor(norms_p[:, :], norms[:, :], powers[:, :], ALU.pow).then_inc(norm_pow, 1)

            @block.vector
            def _(dve):
                nc.vector.memset(ones_row[:, :], 1.0).then_inc(consts_ready, 1)
                nc.vector.memset(onesb_row[:, :], 1.0).then_inc(consts_ready, 1)
                dve.wait_ge(const_step, 2)
                nc.vector.tensor_copy(identb[:, :], ident[:, :]).then_inc(consts_ready, 1)
                dve.wait_ge(const_step, 3)
                nc.vector.tensor_scalar(rev_row[:, :], rows_i[:, 0:XROWS], float(XROWS - KEYS), None,
                                        ALU.add).then_inc(consts_ready, 1)
                dve.wait_ge(weights_in, 11 * 16)
                nc.vector.tensor_tensor(wu[:, :], w_self[:, :], u_self[:, :], ALU.mult).then_inc(norm_a, 1)
                dve.wait_ge(norm_a, 1)
                nc.vector.tensor_reduce(a_self[:, 0:1], wu[:, 0:3 * DIM], AX_X, ALU.add).then_inc(norm_a, 1)
                nc.vector.tensor_reduce(a_self[:, 1:2], wu[:, 3 * DIM:4 * DIM], AX_X, ALU.add).then_inc(norm_a, 1)
                dve.wait_ge(norm_row, 1)
                nc.vector.tensor_copy(row_self[:, :], bank[0:1, 0, :]).then_inc(norm_copied, 1)
                nc.vector.tensor_copy(norms[:, 0:2], bank[0:1, 1, 0:2]).then_inc(norm_sq, 1)
                dve.wait_ge(norm_copied, 1)
                nc.vector.tensor_tensor(row_sq[:, :], row_self[:, :], row_self[:, :], ALU.mult).then_inc(norm_sq, 1)
                dve.wait_ge(norm_sq, 2)
                nc.vector.tensor_reduce(norms[:, 2:3], row_sq[:, 0:3 * DIM], AX_X, ALU.add).then_inc(norm_sq, 1)
                nc.vector.tensor_reduce(norms[:, 3:4], row_sq[:, 3 * DIM:4 * DIM], AX_X, ALU.add).then_inc(norm_sq, 1)
                dve.wait_ge(norm_pow, 1)
                nc.vector.tensor_tensor(c_row[:, :], norms_p[:, 0:2], norms_p[:, 2:4], ALU.mult).then_inc(norm_c, 1)
                dve.wait_ge(norm_c, 1)
                nc.vector.tensor_tensor(c_row[:, :], c_row[:, :], sigmas[:, :], ALU.mult).then_inc(norm_c, 1)
                dve.wait_ge(norm_cb, 1)
                nc.vector.tensor_copy(c_all[:, :], bank[:, 1, 0:2]).then_inc(norm_c, 1)
                dve.wait_ge(norm_c, 3)
                nc.vector.tensor_scalar(w_self[:, 0:DIM], w_self[:, 0:DIM], c_all[:, 0:1], float(HD) ** -0.5,
                                        ALU.mult, ALU.mult).then_inc(self_ready, 1)
                nc.vector.tensor_scalar(w_self[:, DIM:3 * DIM], w_self[:, DIM:3 * DIM], c_all[:, 0:1], None,
                                        ALU.mult).then_inc(self_ready, 1)
                nc.vector.tensor_scalar(w_self[:, 3 * DIM:], w_self[:, 3 * DIM:], c_all[:, 1:2], None,
                                        ALU.mult).then_inc(self_ready, 1)
                nc.vector.tensor_scalar(key_mask[:, :, :], mask_u8[:, :, :], 1.0, -NEG, ALU.subtract,
                                        ALU.mult).then_inc(mask_ready, 1)
                for n, (of_x, of_ctx) in enumerate(((GL, GX), (BL, BX))):
                    for b in range(2):
                        for half in range(2):
                            rows = slice(SEQ * half, SEQ * half + SEQ)
                            which = of_x if half == b else of_ctx
                            nc.vector.tensor_copy(kv_gb[rows, n, b, :], gb[rows, which, :]).then_inc(mask_ready, 1)
                for g in range(4):
                    dve.wait_ge(fold_done, 3 * g + 3)
                    for n, (dst, scale) in enumerate(((fold_a, XH ** -0.5), (fold_b, 1.0), (fold_g, 1.0))):
                        nc.vector.tensor_scalar(
                            dst[:, 4 * g:4 * g + 4, :].rearrange("p (c e) d -> p e c d", e=2),
                            bank[:, 2 + 2 * n:4 + 2 * n, 0:2 * DIM].rearrange("p e (c d) -> p e c d", c=2),
                            scale, None, ALU.mult).then_inc(fold_copied, 1)

            @block.tensor
            def _(pe):
                pe.wait_ge(norm_a, 3)
                nc.tensor.matmul(bank[0:1, 0, 0:3 * DIM], a_self[:, 0:1], w_self[:, 0:3 * DIM], start=True, stop=True)
                nc.tensor.matmul(bank[0:1, 0, 3 * DIM:4 * DIM], a_self[:, 1:2], w_self[:, 3 * DIM:4 * DIM],
                                 start=True, stop=True)
                for n in range(2):
                    last = nc.tensor.matmul(bank[0:1, 1, n:n + 1], a_self[:, n:n + 1], a_self[:, n:n + 1],
                                            start=True, stop=True)
                last.then_inc(norm_row, 1)
                pe.wait_ge(norm_c, 2)
                pe.wait_ge(norm_sq, 2)
                nc.tensor.matmul(bank[:, 1, 0:2], ones_row[:, :], c_row[:, :], start=True, stop=True).then_inc(norm_cb, 1)
                pe.wait_ge(fold_in, 6 * 16)
                for g in range(4):
                    wait(pe, fold_copied, 3 * g)
                    for n in range(3):
                        for k in range(4):
                            lo = XH * (k % 2)
                            c = 2 * g + k // 2
                            last = nc.tensor.matmul(bank[:, 2 + 2 * n + k % 2, (k // 2) * DIM:(k // 2 + 1) * DIM],
                                                    factors[lo:lo + XH, 2 * n, c, :],
                                                    factors[lo:lo + XH, 2 * n + 1, c, :], start=True, stop=True)
                        last.then_inc(fold_done, 1)

        self_attention(nc, bank, x, xT, X, w_self, ident, identb, causal, head_of, eps_t, mhalf)
        cross_attention_and_experts(nc, bank, ctx_in, X, gb, kv_gb, fold_a, fold_b, ident, ones_row, onesb_row,
                                    key_mask, eps_t,
                                    mhalf, fold_g, hid_w, out_w, last_row, table, rev_row, out)


def self_attention(nc, bank, x, xT, X, w_self, ident, identb, causal, head_of, eps_t, mhalf):
    VW = 2 * HD + 2
    with ExitStack() as stack:
        def sb(name, shape, dt=F32):
            return stack.enter_context(nc.sbuf_tensor(name, shape, dt))

        def sem(name):
            return stack.enter_context(nc.semaphore(name))

        x_t = [sb(f"x_t{p}", [P, 2, 2, SEQ]) for p in range(2)]
        x_row = [sb(f"x_row{p}", [P, DIM]) for p in range(2)]
        q_t = sb("q_t", [P, 2 * SEQ])
        k_blocks = sb("k_blocks", [P, 2, 4, SEQ])
        v_blocks = [sb(f"v_blocks{p}", [P, 2, 8, VW]) for p in range(2)]
        probs = [sb(f"probs{p}", [P, HEADS, SEQ]) for p in range(2)]
        probs_t = sb("probs_t", [P, 8, P])
        top = sb("top", [P, HEADS])
        inv = sb("inv", [P, 8, 2])
        heads_out = sb("heads_out", [P, DIM])
        heads_out_t = sb("heads_out_t", [P, DIM])
        resid = sb("resid", [P, DIM])
        stats = sb("stats", [P, 6])
        mv = sb("mv", [P, 2])
        var_eps = sb("var_eps", [P, 1])
        rstd = sb("rstd", [P, 1])

        t_loaded = [sem(f"a_t_loaded{p}") for p in range(2)]
        row_loaded = [sem(f"a_row_loaded{p}") for p in range(2)]
        zeroed = sem("a_zeroed")
        qkv_done = sem("a_qkv_done")
        q_copied = sem("a_q_copied")
        v_spread = sem("a_v_spread")
        k_spread = sem("a_k_spread")
        scores_done = sem("a_scores_done")
        top_done = sem("a_top_done")
        shifted = sem("a_shifted")
        exp_done = sem("a_exp_done")
        inv_done = sem("a_inv_done")
        turned = sem("a_turned")
        turned_copied = sem("a_turned_copied")
        pv_done = sem("a_pv_done")
        heads_scaled = sem("a_heads_scaled")
        out_turned = sem("a_out_turned")
        out_copied = sem("a_out_copied")
        projected = sem("a_projected")
        resid_done = sem("a_resid_done")
        stats_done = sem("a_stats_done")
        mv_done = sem("a_mv_done")
        eps_added = sem("a_eps_added")
        rstd_done = sem("a_rstd_done")
        normed = sem("a_normed")

        qkv_ps = bank[:, 0, :]
        scores_ps = bank[:, 1:5, 0:4 * SEQ]
        turned_ps = bank[:, 5:7, :]
        pv_ps = bank[:, 7, 0:8 * VW].rearrange("p (c w) -> p c w", c=8)
        misc_ps = bank[:, 7, 0:DIM]
        LOOP = {"ahead": 2, "behind": 1}
        block = stack.enter_context(nc.Block())

        @block.sync
        def _(sp):
            def load(n):
                if n.real():
                    wait(sp, v_spread, 2 * (n.t - 1))
                    for c in range(2):
                        sp.dma_start(x_t[n.slot][:, :, c, :],
                                     xT[:, bass.ds(n.t * P, P)].rearrange("d (b s) -> d b s", b=2)
                                     ).then_inc(t_loaded[n.slot], 16)
                n = n.at(-1)
                if n.real():
                    wait(sp, resid_done, n.t - 1)
                    sp.dma_start(x_row[n.slot][:, :], x[bass.ds(n.t * P, P), :]).then_inc(row_loaded[n.slot], 16)
            steps(sp, load, 0, PAIRS, **LOOP)

        @block.tensor
        def _(pe):
            def step(s):
                n = s.at(1)
                if n.real():
                    pe.wait_ge(q_copied, n.t + 1)
                    pe.wait_ge(k_spread, n.t + 1)
                    wait(pe, shifted, n.t)
                    for j in range(4):
                        nc.tensor.matmul(scores_ps[:, j, :], identb[:, :],
                                         causal[:, :, :].rearrange("p g k -> p (g k)"),
                                         start=True, stop=False, skip_group_check=True)
                    for b in range(2):
                        for j in range(4):
                            last = nc.tensor.matmul(scores_ps[SEQ * b:SEQ * b + SEQ, j, :],
                                                    q_t[32 * j:32 * j + 32, SEQ * b:SEQ * b + SEQ],
                                                    k_blocks[32 * j:32 * j + 32, b, :, :].rearrange("p g k -> p (g k)"),
                                                    start=False, stop=True, skip_group_check=True)
                    last.then_inc(scores_done, 1)
                n = s.at(-1)
                if n.real():
                    pe.wait_ge(heads_scaled, n.t + 1)
                    nc.tensor.transpose(misc_ps, heads_out[:, :], ident[:, :]).then_inc(out_turned, 1)
                n = s
                if n.real():
                    pe.wait_ge(exp_done, n.t + 1)
                    wait(pe, turned_copied, n.t)
                    for c in range(8):
                        last = nc.tensor.transpose(turned_ps[:, c // 4, (c % 4) * P:(c % 4 + 1) * P],
                                                   probs[n.slot][:, 2 * c:2 * c + 2, :].rearrange("p h k -> p (h k)"),
                                                   ident[:, :])
                    last.then_inc(turned, 1)
                n = s.at(-1)
                if n.real():
                    pe.wait_ge(out_copied, n.t + 1)
                    nc.tensor.matmul(misc_ps, heads_out_t[:, :], w_self[:, 3 * DIM:4 * DIM],
                                     start=True, stop=True).then_inc(projected, 1)
                n, m = s.at(2), s.at(1)
                if n.real() or m.real():
                    wait(pe, q_copied, s.t + 2)
                    wait(pe, k_spread, s.t + 2)
                    wait(pe, v_spread, 2 * (s.t + 1))
                    if n.real():
                        pe.wait_ge(t_loaded[n.slot], 32 * (n.turn + 1))
                        for c in range(2):
                            last = nc.tensor.matmul(qkv_ps[:, c * P:(c + 1) * P], w_self[:, c * DIM:(c + 1) * DIM],
                                                    x_t[n.slot][:, :, 0, :], start=True, stop=True)
                    if m.real():
                        for b in range(2):
                            last = nc.tensor.matmul(qkv_ps[:, (2 + b) * P:(3 + b) * P],
                                                    x_t[m.slot][:, b, :, :].rearrange("p c s -> p (c s)"),
                                                    w_self[:, 2 * DIM:3 * DIM], start=True, stop=True)
                    last.then_inc(qkv_done, 1)
                n = s
                if n.real():
                    pe.wait_ge(turned_copied, n.t + 1)
                    pe.wait_ge(v_spread, 2 * (n.t + 1))
                    wait(pe, resid_done, n.t)
                    for b in range(2):
                        for c in range(8):
                            last = nc.tensor.matmul(pv_ps[SEQ * b:SEQ * b + SEQ, c, :],
                                                    probs_t[:, c, SEQ * b:SEQ * b + SEQ],
                                                    v_blocks[n.slot][:, b, c, :], start=True, stop=True)
                    last.then_inc(pv_done, 1)
            steps(pe, step, -2, PAIRS, **LOOP)

        @block.scalar
        def _(act):
            def step(s):
                n = s.at(-1)
                if n.real():
                    act.wait_ge(out_turned, n.t + 1)
                    wait(act, projected, n.t)
                    nc.scalar.activation(heads_out_t[:, :], misc_ps, ACT.Copy).then_inc(out_copied, 1)
                n = s
                if n.real():
                    act.wait_ge(turned, n.t + 1)
                    wait(act, pv_done, n.t)
                    nc.scalar.activation(probs_t[:, :, :].rearrange("p c k -> p (c k)"),
                                         turned_ps.rearrange("p c k -> p (c k)"), ACT.Copy).then_inc(turned_copied, 1)
                n, m = s.at(2), s.at(1)
                if n.real() or m.real():
                    act.wait_ge(qkv_done, s.t + 3)
                if n.real():
                    wait(act, scores_done, n.t)
                    nc.scalar.activation(q_t[:, :], qkv_ps[:, 0:P], ACT.Copy).then_inc(q_copied, 1)
                if m.real():
                    act.wait_ge(zeroed, 2)
                    wait(act, pv_done, m.t - 1)
                    for e in range(2):
                        rows = slice(SEQ * e, SEQ * e + SEQ)
                        nc.scalar.activation(v_blocks[m.slot][rows, :, :, HD * e:HD * e + HD],
                                             qkv_ps[rows, 2 * P:4 * P].rearrange("p (b c e r) -> p b c e r",
                                                                                 b=2, c=8, e=2)[:, :, :, e, :],
                                             ACT.Copy).then_inc(v_spread, 1)
                    act.wait_ge(shifted, m.t + 1)
                    nc.scalar.activation(probs[m.slot][:, :, :], probs[m.slot][:, :, :], ACT.Exp).then_inc(exp_done, 1)
            steps(act, step, -2, PAIRS, **LOOP)

        @block.gpsimd
        def _(pool):
            def step(n):
                if not n.real():
                    return
                pool.wait_ge(mv_done, n.t + 1)
                wait(pool, normed, n.t)
                nc.gpsimd.tensor_tensor(var_eps[:, :], mv[:, 1:2], eps_t[:, 0:1], ALU.add).then_inc(eps_added, 1)
                pool.wait_ge(eps_added, n.t + 1)
                nc.gpsimd.tensor_tensor(rstd[:, :], var_eps[:, :], mhalf[:, 0:1], ALU.pow).then_inc(rstd_done, 1)
            steps(pool, step, 0, PAIRS, **LOOP)

        @block.vector
        def _(dve):
            for p in range(2):
                nc.vector.memset(v_blocks[p][:, :, :, :].rearrange("p a b c -> p (a b c)"), 0.0).then_inc(zeroed, 1)
            dve.wait_ge(zeroed, 2)
            for p in range(2):
                for e in range(2):
                    nc.vector.memset(v_blocks[p][SEQ * e:SEQ * e + SEQ, :, :, 2 * HD + e], 1.0).then_inc(zeroed, 1)
            dve.wait_ge(zeroed, 6)

            def step(s):
                n = s.at(1)
                heads = scores_ps.rearrange("p j (g k) -> p j g k", g=4)
                if n.real():
                    dve.wait_ge(scores_done, n.t + 1)
                    nc.vector.tensor_reduce(top[:, :], heads, AX_X, ALU.max).then_inc(top_done, 1)
                n = s.at(-1)
                if n.real():
                    dve.wait_ge(projected, n.t + 1)
                    dve.wait_ge(row_loaded[n.slot], 16 * (n.turn + 1))
                    wait(dve, normed, n.t)
                    nc.vector.tensor_tensor(resid[:, :], x_row[n.slot][:, :], misc_ps, ALU.add).then_inc(resid_done, 1)
                n = s.at(1)
                if n.real():
                    dve.wait_ge(top_done, n.t + 1)
                    wait(dve, turned, n.t - 1)
                    nc.vector.tensor_tensor(
                        probs[n.slot][:, :, :].rearrange("p (j g) k -> p j g k", g=4), heads,
                        top[:, :].rearrange("p (j g k) -> p j g k", g=4, k=1).broadcast_to([P, 4, 4, SEQ]),
                        ALU.subtract).then_inc(shifted, 1)
                n = s.at(-1)
                if n.real():
                    dve.wait_ge(resid_done, n.t + 1)
                    nc.vector.bn_stats(stats[:, :], resid[:, :]).then_inc(stats_done, 1)
                n, m = s.at(2), s.at(1)
                if n.real():
                    dve.wait_ge(qkv_done, s.t + 3)
                    dve.wait_ge(q_copied, n.t + 1)
                    wait(dve, v_spread, 2 * n.t)
                    wait(dve, scores_done, n.t)
                    nc.vector.tensor_tensor(
                        k_blocks[:, :, :, :],
                        qkv_ps[:, P:2 * P].rearrange("p (b g k) -> p b g k", b=2, g=1).broadcast_to([P, 2, 4, SEQ]),
                        head_of[:, :].rearrange("p (b g k) -> p b g k", b=1, k=1).broadcast_to([P, 2, 4, SEQ]),
                        ALU.mult).then_inc(k_spread, 1)
                n = s.at(-1)
                if n.real():
                    wait_apart(dve, stats_done, n.t + 1)
                    nc.vector.bn_aggr(mv[:, :], stats[:, :]).then_inc(mv_done, 1)
                n = s
                if n.real():
                    dve.wait_ge(pv_done, n.t + 1)
                    nc.vector.reciprocal(inv[:, :, :], pv_ps[:, :, 2 * HD:VW]).then_inc(inv_done, 1)
                    dve.wait_ge(inv_done, n.t + 1)
                    wait(dve, out_turned, n.t)
                    nc.vector.tensor_tensor(
                        heads_out[:, :].rearrange("p (c e r) -> p c e r", c=8, e=2),
                        pv_ps[:, :, 0:2 * HD].rearrange("p c (e r) -> p c e r", e=2),
                        inv[:, :, :].rearrange("p c (e r) -> p c e r", r=1).broadcast_to([P, 8, 2, HD]),
                        ALU.mult).then_inc(heads_scaled, 1)
                n = s.at(-1)
                if n.real():
                    dve.wait_ge(rstd_done, n.t + 1)
                    nc.vector.tensor_scalar(X[:, n.t, :], resid[:, :], mv[:, 0:1], rstd[:, 0:1],
                                            ALU.subtract, ALU.mult).then_inc(normed, 1)
            steps(dve, step, -2, PAIRS, **LOOP)
            dve.wait_ge(normed, PAIRS)


def cross_attention_and_experts(nc, bank, ctx_in, X, gb, kv_gb, fold_a, fold_b, ident, ones_row, onesb_row, key_mask, eps_t,
                                mhalf, fold_g, hid_w, out_w, last_row, table, rev_row, out):
    GX, BX, GL, BL, GO, BO = range(6)
    EXP = FH + 1
    LOOP = {"ahead": 2, "behind": 5}
    with ExitStack() as stack:
        def sb(name, shape, dt=F32):
            return stack.enter_context(nc.sbuf_tensor(name, shape, dt))

        def sem(name):
            return stack.enter_context(nc.semaphore(name))

        c_row = [sb(f"c_row{p}", [P, DIM]) for p in range(2)]
        kv_stats = sb("kv_stats", [P, 2, 6])
        kv_mv = sb("kv_mv", [P, 2, 2])
        kv_eps = sb("kv_eps", [P, 2])
        kv_rstd = sb("kv_rstd", [P, 2])
        kv_hat = sb("kv_hat", [P, 2, DIM])
        kv = [sb(f"kv{p}", [P, 2, DIM]) for p in range(2)]
        kv_t = [sb(f"kv_t{p}", [P, 2, P]) for p in range(2)]
        q_t = [sb(f"xq_t{p}", [P, 2, HEADS, SEQ]) for p in range(2)]
        ntop = [sb(f"ntop{p}", [P, 4]) for p in range(2)]
        total = [sb(f"xtotal{p}", [P, 4]) for p in range(2)]
        inv = [sb(f"xinv{p}", [P, 4]) for p in range(2)]
        probs = [sb(f"xprobs{p}", [P, 4, P]) for p in range(2)]
        probs_t = [sb(f"xprobs_t{p}", [P, 512]) for p in range(2)]
        z_t = [sb(f"z_t{p}", [P, HEADS, 2, SEQ]) for p in range(2)]
        o_stats = sb("o_stats", [P, 2, 6])
        o_mv = sb("o_mv", [P, 2, 2])
        o_eps = sb("o_eps", [P, 2])
        o_rstd = sb("o_rstd", [P, 2])
        o_row = sb("o_row", [P, DIM])
        o_resid = sb("o_resid", [P, DIM])

        c_loaded = [sem(f"c_loaded{p}") for p in range(2)]
        kv_stats_done = sem("kv_stats_done")
        kv_mv_done = sem("kv_mv_done")
        kv_eps_done = sem("kv_eps_done")
        kv_rstd_done = sem("kv_rstd_done")
        kv_hat_done = sem("kv_hat_done")
        kv_gained = sem("kv_gained")
        kv_done = sem("kv_done")
        turned_in = sem("turned_in")
        kv_copied = sem("kv_copied")
        q_done = sem("q_done")
        q_copied = sem("xq_copied")
        scores_done = sem("xscores_done")
        top_done = sem("xtop_done")
        exp_done = sem("xexp_done")
        inv_done = sem("xinv_done")
        scaled = sem("scaled")
        turned = sem("xturned")
        turned_copied = sem("xturned_copied")
        z_done = sem("z_done")
        z_copied = sem("z_copied")
        y_done = sem("y_done")
        y_read = sem("y_read")
        o_stats_done = sem("o_stats_done")
        o_mv_done = sem("o_mv_done")
        o_eps_done = sem("o_eps_done")
        o_rstd_done = sem("o_rstd_done")
        o_biased = sem("o_biased")
        o_resid_done = sem("o_resid_done")
        x_normed = sem("x_normed")

        x_now = sb("x_now", [P, DIM])
        x_t = [sb(f"ex_t{p}", [P, P]) for p in range(2)]
        x_lin = sb("x_lin", [P, DIM])
        best_x = sb("best_x", [P, FH])
        best_y = sb("best_y", [P, FH, 8])
        key_y = sb("key_y", [P, FH, 8], U32)
        row_hit = sb("row_hit", [P, FH, XROWS])
        row_rev = sb("row_rev", [P, FH, XROWS])
        row_code = sb("row_code", [P, FH])
        row_base = sb("row_base", [P, FH])
        index = [sb(f"index{p}", [P, FH], U32) for p in range(2)]
        gate_sum = sb("gate_sum", [P, FH])
        gate_all = sb("gate_all", [P, FH])
        gate_out = sb("gate_out", [P, FH])
        gate = [sb(f"gate{p}", [P, EXP]) for p in range(2)]
        rows = [sb(f"rows{p}", [P, FH, TABLE]) for p in range(2)]
        prod = sb("prod", [P, EXP, FFN])
        lin = sb("lin", [P, EXP])
        lin_g = sb("lin_g", [P, EXP])
        hidden = sb("hidden", [P, FFN])
        act_h = sb("act_h", [P, FFN])
        spare = sb("spare", [1, 2])
        spare_in = ones_row[:, 0:2]
        act_t = sb("act_t", [P, 2, P])
        lout = sb("lout", [P, EXP])
        lout_g = sb("lout_g", [P, EXP])
        e_resid = sb("e_resid", [P, DIM])
        e_stats = sb("e_stats", [P, 6])
        e_mv = sb("e_mv", [P, 2])
        e_eps = sb("e_eps", [P, 1])
        e_rstd = sb("e_rstd", [P, 1])
        result = [sb(f"result{p}", [P, DIM]) for p in range(2)]

        x_staged = sem("x_staged")
        x_t_copied = sem("x_t_copied")
        sims_done = sem("sims_done")
        best_done = sem("best_done")
        tops_y_done = sem("tops_y_done")
        sims_read = sem("sims_read")
        row_rev_done = sem("row_rev_done")
        row_code_done = sem("row_code_done")
        row_base_done = sem("row_base_done")
        gate_sum_done = sem("gate_sum_done")
        gate_all_done = sem("gate_all_done")
        index_done = sem("index_done")
        gate_done = sem("gate_done")
        rows_zeroed = sem("rows_zeroed")
        gathered = [sem(f"gathered{p}") for p in range(2)]
        x_lin_done = sem("x_lin_done")
        hid_done = sem("hid_done")
        lin_done = sem("lin_done")
        lin_g_done = sem("lin_g_done")
        hidden_step = sem("hidden_step")
        gelu_done = sem("gelu_done")
        table_back = sem("table_back")
        act_turned = sem("act_turned")
        act_copied = sem("act_copied")
        out_done = sem("out_done")
        lout_done = sem("lout_done")
        lout_g_done = sem("lout_g_done")
        resid_step = sem("resid_step")
        e_stats_done = sem("e_stats_done")
        e_mv_done = sem("e_mv_done")
        e_eps_done = sem("e_eps_done")
        e_rstd_done = sem("e_rstd_done")
        result_done = sem("x_result_done")
        stored = [sem(f"stored{p}") for p in range(2)]

        scores_ps = [bank[:, 0, :], bank[:, 1, :]]
        turned_ps = bank[:, 2, :]
        z_ps = bank[:, 3, :]
        q_ps = bank[:, 4, :]
        kv_turn_ps = bank[:, 4, 0:2 * P]
        x_turn_ps = bank[:, 4, 2 * P:3 * P]
        y_ps = bank[:, 4, 0:DIM]
        sims_ps = [bank[:, 5, :], bank[:, 6, :]]
        hid_ps = bank[:, 7, 0:FFN + 2]
        act_turn_ps = bank[:, 7, 0:2 * P]
        out_ps = bank[:, 7, 0:DIM]
        block = stack.enter_context(nc.Block())

        @block.sync
        def _(sp):
            def step(s):
                n = s.at(2)
                if n.real():
                    wait(sp, kv_hat_done, 4 * (n.t - 1))
                    for b in range(2):
                        sp.dma_start(c_row[n.slot][SEQ * (1 - b):SEQ * (2 - b), :],
                                     ctx_in[bass.ds(n.t * P + SEQ * b, SEQ), :]).then_inc(c_loaded[n.slot], 16)
                n = s.at(-5)
                if n.real():
                    sp.wait_ge(result_done, n.t + 1)
                    sp.dma_start(out[bass.ds(n.t * P, P), :], result[n.slot][:, :]).then_inc(stored[n.slot], 16)
            steps(sp, step, -2, PAIRS + 4, **LOOP)
            for p in range(2):
                sp.wait_ge(stored[p], 16 * (PAIRS // 2))

        @block.tensor
        def _(pe):
            def inputs_turn(n, r):
                if n.real():
                    pe.wait_ge(kv_done, n.t + 1)
                    wait(pe, y_read, n.t - 1)
                    for b in range(2):
                        last = nc.tensor.transpose(kv_turn_ps[:, b * P:(b + 1) * P], kv[n.slot][:, b, :], ident[:, :])
                if r.real():
                    pe.wait_ge(x_staged, r.t + 1)
                    wait(pe, y_read, r.t + 2 if r.at(1).real() else PAIRS)
                    last = nc.tensor.transpose(x_turn_ps, x_now[:, :], ident[:, :])
                if n.real() or r.real():
                    last.then_inc(turned_in, 1)

            def queries(n, c):
                if not n.real():
                    return
                pe.wait_ge(kv_copied, n.t + 1)
                wait(pe, x_t_copied, n.t - 2)
                wait(pe, q_copied, 4 * n.t + c)
                x_tokens = kv_t[n.slot][:, :, :].rearrange("p b (e q) -> p (b e) q", e=2)[:, 0:4:3, :]
                for h in range(4):
                    last = nc.tensor.matmul(q_ps[:, h * P:(h + 1) * P], fold_a[:, 4 * c + h, :], x_tokens,
                                            start=True, stop=True)
                last.then_inc(q_done, 1)

            def scores(n, u):
                if not n.real():
                    return
                b, half = u % 2, u // 2
                wait_apart(pe, q_copied, 4 * n.t + 2 * half + 2)
                wait_apart(pe, exp_done, 4 * (4 * n.t + u - 1))
                ps = scores_ps[u % 2].rearrange("p (i k) -> p i k", i=4)
                nc.tensor.matmul(ps[:, :, SEQ * (1 - b):SEQ * (2 - b)], onesb_row[:, :],
                                 key_mask[:, 2 * n.t + b, :].rearrange("a (i s) -> a i s", i=1)
                                 .broadcast_to([1, 4, SEQ]), start=True, stop=False, skip_group_check=True)
                for i in range(4):
                    h = 8 * half + 2 * i
                    last = nc.tensor.matmul(ps[:, i, :], q_t[n.slot][:, b, h:h + 2, :].rearrange("p h q -> p (h q)"),
                                            kv_t[n.slot][:, b, :], start=False, stop=True, skip_group_check=True)
                last.then_inc(scores_done, 1)

            def turn(n, u):
                if not n.real():
                    return
                pe.wait_ge(scaled, 4 * n.t + u + 1)
                wait(pe, turned_copied, 4 * n.t + u)
                for i in range(4):
                    last = nc.tensor.transpose(turned_ps[:, i * P:(i + 1) * P], probs[u % 2][:, i, :], ident[:, :])
                last.then_inc(turned, 1)

            def values(n, u):
                if not n.real():
                    return
                pe.wait_ge(turned_copied, 4 * n.t + u + 1)
                wait(pe, z_copied, 4 * n.t + u)
                nc.tensor.matmul(z_ps, kv[n.slot][:, u % 2, :], probs_t[u % 2][:, :],
                                 start=True, stop=True).then_inc(z_done, 1)

            def output(n):
                if not n.real():
                    return
                pe.wait_ge(z_copied, 4 * (n.t + 1))
                wait(pe, q_copied, 4 * (n.t + 2) if n.at(1).real() else 0)
                for h in range(HEADS):
                    last = nc.tensor.matmul(y_ps, z_t[n.slot][:, h, :, :].rearrange("p b q -> p (b q)"),
                                            fold_b[:, h, :], start=(h == 0), stop=(h == HEADS - 1))
                last.then_inc(y_done, 1)

            def similarities(n, c):
                if not n.real():
                    return
                pe.wait_ge(x_t_copied, n.t + 1)
                wait(pe, sims_read, 4 * n.t + c - 1)
                nc.tensor.matmul(sims_ps[c % 2], x_t[n.slot][:, :],
                                 fold_g[:, 4 * c:4 * c + 4, :].rearrange("p h k -> p (h k)"),
                                 start=True, stop=True).then_inc(sims_done, 1)

            def expert_hidden(n):
                if not n.real():
                    return
                wait(pe, resid_step, (EXP + 1) * (n.t - 1) + 1 if not isinstance(n.t, int) or n.t else 0)
                nc.tensor.matmul(hid_ps, x_t[n.slot][:, :], hid_w[:, :], start=True, stop=True).then_inc(hid_done, 1)

            def expert_turn(n):
                if not n.real():
                    return
                pe.wait_ge(gelu_done, n.t + 1)
                pe.wait_ge(hidden_step, EXP * n.t + 1)
                for c in range(2):
                    last = nc.tensor.transpose(act_turn_ps[:, c * P:(c + 1) * P], act_h[:, c * P:(c + 1) * P],
                                               ident[:, :])
                last.then_inc(act_turned, 1)

            def expert_out(n):
                if not n.real():
                    return
                pe.wait_ge(act_copied, n.t + 1)
                for c in range(2):
                    last = nc.tensor.matmul(out_ps, act_t[:, c, :], out_w[:, c, :], start=(c == 0), stop=(c == 1))
                last.then_inc(out_done, 1)

            def step(s):
                r, e = s.at(-2), s.at(-4)
                scores(s, 1)
                turn(s, 0)
                output(s.at(-1))
                expert_hidden(e)
                values(s, 0)

                scores(s, 2)
                turn(s, 1)
                inputs_turn(s.at(1), r)
                values(s, 1)
                queries(s.at(1), 0)
                similarities(r, 0)
                queries(s.at(1), 1)

                scores(s, 3)
                turn(s, 2)
                similarities(r, 1)
                values(s, 2)
                expert_turn(e)
                similarities(r, 2)

                scores(s.at(1), 0)
                turn(s, 3)
                queries(s.at(1), 2)
                expert_out(e)
                values(s, 3)
                similarities(r, 3)
                queries(s.at(1), 3)
            steps(pe, step, -1, PAIRS + 3, **LOOP)

        @block.scalar
        def _(act):
            def stage_x(n):
                if not n.real():
                    return
                act.wait_ge(x_normed, n.t + 1)
                wait(act, x_t_copied, n.t)
                nc.scalar.activation(x_now[:, :], X[:, n.t, :], ACT.Copy).then_inc(x_staged, 1)

            def inputs_copy(s, n, r):
                if n.real() or r.real():
                    act.wait_ge(turned_in, s.t + 2)
                if n.real():
                    wait(act, scores_done, 4 * (n.t - 1))
                    nc.scalar.activation(kv_t[n.slot][:, :, :].rearrange("p b k -> p (b k)"), kv_turn_ps,
                                         ACT.Copy).then_inc(kv_copied, 1)
                if r.real():
                    wait(act, hid_done, r.t - 1)
                    nc.scalar.activation(x_t[r.slot][:, :], x_turn_ps, ACT.Copy).then_inc(x_t_copied, 1)

            def q_copy(n, c):
                if not n.real():
                    return
                act.wait_ge(q_done, 4 * n.t + c + 1)
                wait(act, scores_done, 4 * (n.t - 1))
                nc.scalar.activation(q_t[n.slot][:, :, 4 * c:4 * c + 4, :].rearrange("p b h q -> p h b q"),
                                     q_ps.rearrange("p (h b q) -> p h b q", h=4, b=2), ACT.Copy).then_inc(q_copied, 1)

            def exps(n, u):
                if not n.real():
                    return
                act.wait_ge(top_done, 4 * n.t + u + 1)
                wait(act, turned, 4 * n.t + u - 1)
                wait(act, inv_done, 4 * n.t + u - 1)
                for i in range(4):
                    nc.scalar.activation(probs[u % 2][:, i, :], scores_ps[u % 2][:, i * P:(i + 1) * P], ACT.Exp,
                                         bias=ntop[u % 2][:, i:i + 1],
                                         accum_out=total[u % 2][:, i:i + 1]).then_inc(exp_done, 1)

            def turn_copy(n, u):
                if not n.real():
                    return
                act.wait_ge(turned, 4 * n.t + u + 1)
                wait(act, z_done, 4 * n.t + u - 1)
                nc.scalar.activation(probs_t[u % 2][:, :], turned_ps, ACT.Copy).then_inc(turned_copied, 1)

            def z_copy(n, u):
                if not n.real():
                    return
                b, half = u % 2, u // 2
                act.wait_ge(z_done, 4 * n.t + u + 1)
                wait(act, y_done, n.t - 1)
                nc.scalar.activation(z_t[n.slot][:, 8 * half:8 * half + 8, b, :],
                                     z_ps.rearrange("p (h q) -> p h q", h=8), ACT.Copy).then_inc(z_copied, 1)

            def gelu(n):
                if not n.real():
                    return
                act.wait_ge(hidden_step, EXP * (n.t + 1))
                wait(act, lout_done, EXP * n.t)
                wait(act, act_turned, n.t)
                nc.scalar.activation(act_h[:, :], hidden[:, :], ACT.Gelu).then_inc(gelu_done, 1)
                wait(act, table_back, n.t)
                nc.scalar.activation(spare[:, :], spare_in[:, :], ACT.Exp).then_inc(table_back, 1)

            def act_copy(n):
                if not n.real():
                    return
                act.wait_ge(act_turned, n.t + 1)
                wait(act, out_done, n.t)
                nc.scalar.activation(act_t[:, :, :].rearrange("p c k -> p (c k)"), act_turn_ps,
                                     ACT.Copy).then_inc(act_copied, 1)

            def step(s):
                r, e = s.at(-2), s.at(-4)
                turn_copy(s, 0)
                exps(s, 1)
                stage_x(r)
                z_copy(s, 0)

                turn_copy(s, 1)
                exps(s, 2)
                inputs_copy(s, s.at(1), r)
                z_copy(s, 1)
                q_copy(s.at(1), 0)
                q_copy(s.at(1), 1)

                turn_copy(s, 2)
                exps(s, 3)
                gelu(e)
                z_copy(s, 2)
                act_copy(e)

                turn_copy(s, 3)
                exps(s.at(1), 0)
                q_copy(s.at(1), 2)
                z_copy(s, 3)
                q_copy(s.at(1), 3)
            steps(act, step, -1, PAIRS + 3, **LOOP)

        @block.gpsimd
        def _(pool):
            for p in range(2):
                nc.gpsimd.memset(rows[p][:, :, :].rearrange("p h c -> p (h c)"), 0.0).then_inc(rows_zeroed, 1)
            pool.wait_ge(rows_zeroed, 2)
            in_table = nc.gpsimd.to_reg(LAST - 1)

            def kv_scales(n):
                if not n.real():
                    return
                pool.wait_ge(kv_mv_done, 2 * (n.t + 1))
                wait(pool, kv_hat_done, 4 * n.t)
                nc.gpsimd.tensor_tensor(kv_eps[:, :], kv_mv[:, :, 1], eps_t[:, :], ALU.add).then_inc(kv_eps_done, 1)
                pool.wait_ge(kv_eps_done, n.t + 1)
                nc.gpsimd.tensor_tensor(kv_rstd[:, :], kv_eps[:, :], mhalf[:, :], ALU.pow).then_inc(kv_rstd_done, 1)

            def kv_affine(n):
                if not n.real():
                    return
                pool.wait_ge(kv_hat_done, 4 * (n.t + 1))
                wait(pool, z_done, 4 * (n.t - 1))
                wait(pool, turned_in, n.t)
                nc.gpsimd.tensor_tensor(kv[n.slot][:, :, :], kv_hat[:, :, :], kv_gb[:, 0, :, :],
                                        ALU.mult).then_inc(kv_gained, 1)
                pool.wait_ge(kv_gained, n.t + 1)
                nc.gpsimd.tensor_tensor(kv[n.slot][:, :, :], kv[n.slot][:, :, :], kv_gb[:, 1, :, :],
                                        ALU.add).then_inc(kv_done, 1)

            def out_scale(n, k):
                if not n.real():
                    return
                pool.wait_ge(o_mv_done, 2 * n.t + k + 1)
                if k:
                    wait(pool, x_normed, n.t)
                else:
                    wait(pool, o_biased, n.t)
                nc.gpsimd.tensor_tensor(o_eps[:, k:k + 1], o_mv[:, k, 1:2], eps_t[:, 0:1],
                                        ALU.add).then_inc(o_eps_done, 1)
                pool.wait_ge(o_eps_done, 2 * n.t + k + 1)
                nc.gpsimd.tensor_tensor(o_rstd[:, k:k + 1], o_eps[:, k:k + 1], mhalf[:, 0:1],
                                        ALU.pow).then_inc(o_rstd_done, 1)

            def scale(n, u):
                if not n.real():
                    return
                pool.wait_ge(exp_done, 4 * (4 * n.t + u + 1))
                pool.wait_ge(inv_done, 4 * n.t + u + 1)
                nc.gpsimd.tensor_tensor(
                    probs[u % 2][:, :, :], probs[u % 2][:, :, :],
                    inv[u % 2][:, :].rearrange("p (i k) -> p i k", k=1).broadcast_to([P, 4, P]),
                    ALU.mult).then_inc(scaled, 1)

            def gather(n, heads):
                if not n.real():
                    return
                if heads[0] == 0:
                    wait_apart(pool, index_done, n.t + 1)
                wait_apart(pool, resid_step, (EXP + 1) * (n.t - 2) + heads[-1] + 2)
                for h in heads:
                    nc.gpsimd.indirect_dma_start(
                        out=rows[n.slot][:, h, :], out_offset=None, in_=table,
                        in_offset=bass.IndirectOffsetOnAxis(ap=index[n.slot][:, h:h + 1], axis=0),
                        bounds_check=in_table, oob_is_err=False).then_inc(gathered[n.slot], 16)

            def result_scale(n):
                if not n.real():
                    return
                pool.wait_ge(e_mv_done, n.t + 1)
                wait(pool, result_done, n.t)
                nc.gpsimd.tensor_tensor(e_eps[:, :], e_mv[:, 1:2], eps_t[:, 0:1], ALU.add).then_inc(e_eps_done, 1)
                pool.wait_ge(e_eps_done, n.t + 1)
                nc.gpsimd.tensor_tensor(e_rstd[:, :], e_eps[:, :], mhalf[:, 0:1], ALU.pow).then_inc(e_rstd_done, 1)

            def step(s):
                g = s.at(-3)
                kv_affine(s.at(1))
                scale(s, 1)

                out_scale(s.at(-1), 0)
                scale(s, 2)
                kv_scales(s.at(2))
                gather(g, (0, 1))

                scale(s, 3)
                out_scale(s.at(-1), 1)
                result_scale(s.at(-5))
                gather(g, (2, 3, 4))

                scale(s.at(1), 0)
                gather(g, (5, 6, 7))
            kv_scales(Pair(0, 0))
            steps(pool, step, -1, PAIRS + 4, **LOOP)

        @block.vector
        def _(dve):
            def tops(n, u):
                if not n.real():
                    return
                dve.wait_ge(scores_done, 4 * n.t + u + 1)
                wait(dve, exp_done, 4 * (4 * n.t + u - 1))
                nc.vector.tensor_reduce(ntop[u % 2][:, :], scores_ps[u % 2].rearrange("p (i k) -> p i k", i=4),
                                        AX_X, ALU.max, negate=True).then_inc(top_done, 1)

            def invert(n, u):
                if not n.real():
                    return
                dve.wait_ge(exp_done, 4 * (4 * n.t + u + 1))
                wait(dve, scaled, 4 * n.t + u - 1)
                nc.vector.reciprocal(inv[u % 2][:, :], total[u % 2][:, :]).then_inc(inv_done, 1)

            def kv_moments(n):
                if not n.real():
                    return
                dve.wait_ge(c_loaded[n.slot], 32 * (n.turn + 1))
                wait(dve, kv_mv_done, 2 * n.t)
                nc.vector.bn_stats(kv_stats[:, 0, :], X[:, n.t, :]).then_inc(kv_stats_done, 1)
                nc.vector.bn_stats(kv_stats[:, 1, :], c_row[n.slot][:, :]).then_inc(kv_stats_done, 1)

            def kv_moments_end(n):
                if not n.real():
                    return
                wait_apart(dve, kv_stats_done, 2 * n.t + 2)
                wait_apart(dve, kv_rstd_done, n.t)
                wait_apart(dve, kv_hat_done, 4 * n.t)
                for k in range(2):
                    nc.vector.bn_aggr(kv_mv[:, k, :], kv_stats[:, k, :]).then_inc(kv_mv_done, 1)

            def kv_norm(n):
                if not n.real():
                    return
                dve.wait_ge(kv_rstd_done, n.t + 1)
                dve.wait_ge(kv_mv_done, 2 * (n.t + 1))
                wait(dve, kv_gained, n.t)
                for half in range(2):
                    r = slice(SEQ * half, SEQ * half + SEQ)
                    nc.vector.tensor_scalar(kv_hat[r, half, :], X[r, n.t, :], kv_mv[r, 0, 0:1], kv_rstd[r, 0:1],
                                            ALU.subtract, ALU.mult).then_inc(kv_hat_done, 1)
                    nc.vector.tensor_scalar(kv_hat[r, 1 - half, :], c_row[n.slot][r, :], kv_mv[r, 1, 0:1],
                                            kv_rstd[r, 1:2], ALU.subtract, ALU.mult).then_inc(kv_hat_done, 1)

            def out_moments(n):
                if not n.real():
                    return
                dve.wait_ge(y_done, n.t + 1)
                wait(dve, o_mv_done, 2 * n.t)
                nc.vector.bn_stats(o_stats[:, 0, :], y_ps).then_inc(o_stats_done, 1)

            def out_gain(n):
                if not n.real():
                    return
                wait_apart(dve, o_stats_done, 2 * n.t + 1)
                wait_apart(dve, o_biased, n.t)
                nc.vector.bn_aggr(o_mv[:, 0, :], o_stats[:, 0, :]).then_inc(o_mv_done, 1)
                dve.wait_ge(o_mv_done, 2 * n.t + 1)
                nc.vector.scalar_tensor_tensor(o_row[:, :], y_ps, o_mv[:, 0, 0:1], gb[:, GO, :],
                                               ALU.subtract, ALU.mult).then_inc(y_read, 1)

            def out_bias(n):
                if not n.real():
                    return
                dve.wait_ge(o_rstd_done, 2 * n.t + 1)
                dve.wait_ge(y_read, n.t + 1)
                wait(dve, x_normed, n.t)
                nc.vector.scalar_tensor_tensor(o_resid[:, :], o_row[:, :], o_rstd[:, 0:1], gb[:, BO, :],
                                               ALU.mult, ALU.add).then_inc(o_biased, 1)

            def out_add(n):
                if not n.real():
                    return
                dve.wait_ge(o_biased, n.t + 1)
                nc.vector.tensor_tensor(o_resid[:, :], o_resid[:, :], X[:, n.t, :], ALU.add).then_inc(o_resid_done, 1)

            def out_moments_2(n):
                if not n.real():
                    return
                dve.wait_ge(o_resid_done, n.t + 1)
                nc.vector.bn_stats(o_stats[:, 1, :], o_resid[:, :]).then_inc(o_stats_done, 1)

            def out_aggregate_2(n):
                if not n.real():
                    return
                wait_apart(dve, o_stats_done, 2 * n.t + 2)
                nc.vector.bn_aggr(o_mv[:, 1, :], o_stats[:, 1, :]).then_inc(o_mv_done, 1)

            def out_norm(n):
                if not n.real():
                    return
                dve.wait_ge(o_rstd_done, 2 * n.t + 2)
                nc.vector.tensor_scalar(X[:, n.t, :], o_resid[:, :], o_mv[:, 1, 0:1], o_rstd[:, 1:2],
                                        ALU.subtract, ALU.mult).then_inc(x_normed, 1)

            def sims_of(c):
                return sims_ps[c % 2].rearrange("p (h k) -> p h k", h=4)

            def row_best(n, c):
                if not n.real():
                    return
                dve.wait_ge(sims_done, 4 * n.t + c + 1)
                wait(dve, gate_sum_done, n.t)
                nc.vector.tensor_reduce(best_x[:, 4 * c:4 * c + 4], sims_of(c), AX_X, ALU.max).then_inc(best_done, 1)

            def row_hits(n, c):
                if not n.real():
                    return
                dve.wait_ge(best_done, 2 * n.t + c + 1)
                wait(dve, row_rev_done, n.t)
                nc.vector.tensor_tensor(row_hit[:, 4 * c:4 * c + 4, :], sims_of(c)[:, :, 0:XROWS],
                                        best_x[:, 4 * c:4 * c + 4].rearrange("p (h k) -> p h k", k=1)
                                        .broadcast_to([P, 4, XROWS]), ALU.is_equal).then_inc(sims_read, 1)

            def row_codes(n):
                if not n.real():
                    return
                dve.wait_ge(sims_read, 4 * n.t + 2)
                wait(dve, row_code_done, n.t)
                nc.vector.tensor_tensor(row_rev[:, :, :], row_hit[:, :, :],
                                        rev_row[:, :].rearrange("p (h k) -> p h k", h=1).broadcast_to([P, FH, XROWS]),
                                        ALU.mult).then_inc(row_rev_done, 1)

            def row_codes_end(n):
                if not n.real():
                    return
                dve.wait_ge(row_rev_done, n.t + 1)
                wait(dve, row_base_done, n.t)
                nc.vector.tensor_reduce(row_code[:, :], row_rev[:, :, :], AX_X, ALU.max).then_inc(row_code_done, 1)

            def key_tops(n, c):
                if not n.real():
                    return
                wait_apart(dve, sims_done, 4 * n.t + c + 1)
                wait_apart(dve, gate_sum_done, n.t)
                for h in range(4):
                    nc.vector.max(best_y[:, 4 * (c - 2) + h, :], sims_of(c)[:, h, :]).then_inc(tops_y_done, 1)

            def key_places(n, c):
                if not n.real():
                    return
                wait_apart(dve, tops_y_done, 8 * n.t + 4 * (c - 1))
                wait_apart(dve, index_done, n.t)
                for h in range(4):
                    i = 4 * (c - 2) + h
                    last = nc.vector.max_index(key_y[:, i, :], best_y[:, i, :], sims_of(c)[:, h, :])
                last.then_inc(sims_read, 1)

            def route_1(n):
                if not n.real():
                    return
                dve.wait_ge(row_code_done, n.t + 1)
                nc.vector.tensor_scalar(row_base[:, :], row_code[:, :], -float(KEYS), float(XROWS * KEYS),
                                        ALU.mult, ALU.add).then_inc(row_base_done, 1)
                dve.wait_ge(tops_y_done, 8 * (n.t + 1))
                nc.vector.tensor_tensor(gate_sum[:, :], best_x[:, :], best_y[:, :, 0], ALU.add).then_inc(gate_sum_done, 1)

            def route_2(n):
                if not n.real():
                    return
                dve.wait_ge(sims_read, 4 * (n.t + 1))
                dve.wait_ge(row_base_done, n.t + 1)
                wait(dve, gathered[n.slot], 16 * FH * n.turn)
                nc.vector.tensor_tensor(index[n.slot][:, :], row_base[:, :], key_y[:, :, 0], ALU.add).then_inc(index_done, 1)
                dve.wait_ge(gate_sum_done, n.t + 1)
                wait(dve, gate_done, 3 * n.t)
                nc.vector.tensor_scalar(gate_all[:, :], gate_sum[:, :], 0.0, None, ALU.max).then_inc(gate_all_done, 1)

            def route_3(n):
                if not n.real():
                    return
                dve.wait_ge(index_done, n.t + 1)
                dve.wait_ge(gate_all_done, n.t + 1)
                wait(dve, lout_g_done, n.t - 1)
                nc.vector.scalar_tensor_tensor(gate[n.slot][:, 0:FH], index[n.slot][:, :], float(LAST) - 0.5,
                                               gate_all[:, :], ALU.is_le, ALU.mult).then_inc(gate_done, 1)

            def route_4(n):
                if not n.real():
                    return
                dve.wait_ge(gate_done, 3 * n.t + 1)
                nc.vector.tensor_tensor(gate_out[:, :], gate_all[:, :], gate[n.slot][:, 0:FH],
                                        ALU.subtract).then_inc(gate_done, 1)

            def route_5(n):
                if not n.real():
                    return
                dve.wait_ge(gate_done, 3 * n.t + 2)
                nc.vector.tensor_reduce(gate[n.slot][:, FH:EXP], gate_out[:, :], AX_X, ALU.add).then_inc(gate_done, 1)

            def lin_start(n):
                if not n.real():
                    return
                wait(dve, resid_step, (EXP + 1) * (n.t - 1) + 1)
                nc.vector.tensor_copy(x_lin[:, :], X[:, n.t, :]).then_inc(x_lin_done, 1)

            def lin_last(n):
                if not n.real():
                    return
                dve.wait_ge(hid_done, n.t + 1)
                wait(dve, lin_g_done, n.t)
                nc.vector.tensor_copy(lin[:, FH:EXP], hid_ps[:, FFN:FFN + 1]).then_inc(lin_done, 1)

            def lins(n, heads):
                if not n.real():
                    return
                if heads[0] == 0:
                    dve.wait_ge(gathered[n.slot], 16 * FH * (n.turn + 1))
                    dve.wait_ge(x_lin_done, n.t + 1)
                    wait(dve, lout_done, EXP * n.t)
                for h in heads:
                    nc.vector.tensor_tensor_reduce(prod[:, h, 0:DIM], x_lin[:, :], rows[n.slot][:, h, A_IN:A_IN + DIM],
                                                   1.0, 0.0, ALU.mult, ALU.add, lin[:, h:h + 1]).then_inc(lin_done, 1)

            def lin_gates(n):
                if not n.real():
                    return
                dve.wait_ge(lin_done, EXP * (n.t + 1))
                dve.wait_ge(gate_done, 3 * (n.t + 1))
                wait(dve, hidden_step, EXP * n.t)
                nc.vector.tensor_tensor(lin_g[:, :], lin[:, :], gate[n.slot][:, :], ALU.mult).then_inc(lin_g_done, 1)

            def hidden_sum(n, h):
                if not n.real():
                    return
                if h == 0:
                    dve.wait_ge(lin_g_done, n.t + 1)
                    wait(dve, gelu_done, n.t)
                else:
                    dve.wait_ge(hidden_step, EXP * n.t + h)
                weights = rows[n.slot][:, h, B_IN:B_IN + FFN] if h < FH else last_row[:, B_IN:B_IN + FFN]
                nc.vector.scalar_tensor_tensor(hidden[:, :], weights, lin_g[:, h:h + 1],
                                               hidden[:, :] if h else hid_ps[:, 0:FFN],
                                               ALU.mult, ALU.add).then_inc(hidden_step, 1)

            def louts(n, experts):
                if not n.real():
                    return
                if experts[0] == 0:
                    dve.wait_ge(gelu_done, n.t + 1)
                    wait(dve, lout_g_done, n.t)
                    wait(dve, lin_done, EXP * (n.t + 1))
                for h in experts:
                    weights = rows[n.slot][:, h, A_OUT:A_OUT + FFN] if h < FH else last_row[:, A_OUT:A_OUT + FFN]
                    nc.vector.tensor_tensor_reduce(prod[:, h, :], act_h[:, :], weights, 1.0, 0.0,
                                                   ALU.mult, ALU.add, lout[:, h:h + 1]).then_inc(lout_done, 1)

            def lout_gates(n):
                if not n.real():
                    return
                dve.wait_ge(lout_done, EXP * (n.t + 1))
                wait(dve, resid_step, (EXP + 1) * n.t)
                nc.vector.tensor_tensor(lout_g[:, :], lout[:, :], gate[n.slot][:, :], ALU.mult).then_inc(lout_g_done, 1)

            def resid_start(n):
                if not n.real():
                    return
                dve.wait_ge(out_done, n.t + 1)
                wait(dve, result_done, n.t)
                nc.vector.tensor_tensor(e_resid[:, :], x_lin[:, :], out_ps, ALU.add).then_inc(resid_step, 1)

            def resid_sum(n, h):
                if not n.real():
                    return
                if h == 0:
                    dve.wait_ge(lout_g_done, n.t + 1)
                dve.wait_ge(resid_step, (EXP + 1) * n.t + 1 + h)
                weights = rows[n.slot][:, h, B_OUT:B_OUT + DIM] if h < FH else last_row[:, B_OUT:B_OUT + DIM]
                nc.vector.scalar_tensor_tensor(e_resid[:, :], weights, lout_g[:, h:h + 1], e_resid[:, :],
                                               ALU.mult, ALU.add).then_inc(resid_step, 1)

            def result_moments(n):
                if not n.real():
                    return
                dve.wait_ge(resid_step, (EXP + 1) * (n.t + 1))
                wait(dve, e_mv_done, n.t)
                nc.vector.bn_stats(e_stats[:, :], e_resid[:, :]).then_inc(e_stats_done, 1)

            def result_aggregate(n):
                if not n.real():
                    return
                wait_apart(dve, e_stats_done, n.t + 1)
                wait_apart(dve, result_done, n.t)
                nc.vector.bn_aggr(e_mv[:, :], e_stats[:, :]).then_inc(e_mv_done, 1)

            def result_norm(n):
                if not n.real():
                    return
                dve.wait_ge(e_rstd_done, n.t + 1)
                wait(dve, stored[n.slot], 16 * n.turn)
                nc.vector.tensor_scalar(result[n.slot][:, :], e_resid[:, :], e_mv[:, 0:1], e_rstd[:, 0:1],
                                        ALU.subtract, ALU.mult).then_inc(result_done, 1)

            def step(s):
                r, g, e, o, f = s.at(-2), s.at(-3), s.at(-4), s.at(-1), s.at(-5)
                tops(s, 1)
                key_tops(g, 3)
                lin_start(e)
                key_places(g, 3)
                invert(s, 1)
                route_1(g)
                lins(e, (0, 1, 2))
                route_2(g)
                lins(e, (3, 4))
                route_3(g)
                lins(e, (5,))
                route_4(g)
                lins(e, (6,))
                route_5(g)
                lins(e, (7,))
                lin_last(e)
                resid_sum(f, 0)
                lin_gates(e)
                out_moments(o)
                hidden_sum(e, 0)
                out_gain(o)

                tops(s, 2)
                for h in range(1, 4):
                    resid_sum(f, h)
                    hidden_sum(e, h)
                invert(s, 2)
                kv_moments(s.at(2))
                resid_sum(f, 4)
                hidden_sum(e, 4)
                kv_moments_end(s.at(2))
                for h in range(5, EXP):
                    resid_sum(f, h)
                    hidden_sum(e, h)

                tops(s, 3)
                row_best(r, 0)
                out_bias(o)
                result_moments(f)
                row_hits(r, 0)
                out_add(o)
                result_aggregate(f)
                invert(s, 3)
                out_moments_2(o)
                row_best(r, 1)
                out_aggregate_2(o)
                row_hits(r, 1)
                kv_norm(s.at(2))
                row_codes(r)
                result_norm(f)
                row_codes_end(r)
                key_tops(r, 2)

                tops(s.at(1), 0)
                key_places(r, 2)
                louts(e, (0, 1))
                out_norm(o)
                invert(s.at(1), 0)
                louts(e, (2, 3, 4, 5, 6, 7, 8))
                resid_start(e)
                lout_gates(e)
            kv_moments(Pair(0, 0))
            kv_moments_end(Pair(0, 0))
            kv_norm(Pair(0, 0))
            steps(dve, step, -1, PAIRS + 4, **LOOP)


def kernel(**inputs):
    import numpy as np
    import concourse.bacc as bacc
    from concourse.bass_utils import run_bass_kernel_spmd

    a = {k: np.asarray(v) for k, v in inputs.items()}

    def cat(*names, axis=-1):
        return np.concatenate([a[n] for n in names], axis=axis)

    def turned(m):
        return np.ascontiguousarray(m.T)

    wkv = a["L0_xattn_Wkv"]
    host = {
        "x": a["x"].reshape(BATCH * SEQ, DIM),
        "xT": turned(a["x"].reshape(BATCH * SEQ, DIM)),
        "ctx": a["ctx_1024"].reshape(BATCH * SEQ, DIM),
        "mask": a["mask_BxS2_bf1"].view(np.uint8),
        "w_attn": cat("L0_attn_W_qkv", "L0_attn_W_proj"),
        "u_attn": cat("L0_attn_u_qkv", "L0_attn_u_proj"),
        "sig_qkv": a["L0_attn_sigma_qkv"],
        "sig_proj": a["L0_attn_sigma_proj"],
        "gains": cat("L0_xattn_g_x", "L0_xattn_b_x", "L0_xattn_g_l", "L0_xattn_b_l", "L0_xattn_g_o", "L0_xattn_b_o"),
        "wq_t": turned(a["L0_xattn_Wq"]),
        "wk_t": turned(wkv[:, :INNER]),
        "wv_t": turned(wkv[:, INNER:]),
        "wout": a["L0_xattn_Wout"],
        "ffn_wq": a["L0_ffn_Wq"],
        "keys_t": a["L0_ffn_keys"].transpose(2, 0, 3, 1).reshape(2 * FH * XH, KEYS),
        "w_in_t": turned(a["L0_ffn_W_in"]),
        "w_out_t": turned(a["L0_ffn_W_out"]),
        "table": cat("L0_ffn_in_a", "L0_ffn_in_b", "L0_ffn_out_a", "L0_ffn_out_b"),
    }
    nc = bacc.Bacc("TRN2", target_bir_lowering=False, num_devices=1)
    arrays, args = {}, []
    for name, value in host.items():
        value = np.ascontiguousarray(value)
        arrays[f"in_{name}"] = value
        args.append(nc.dram_tensor(f"in_{name}", value.shape, mybir.dt.from_np(value.dtype), kind="ExternalInput").ap())
    out = nc.dram_tensor("result", (BATCH * SEQ, DIM), F32, kind="ExternalOutput").ap()
    decoder_layer(nc, *args, out)
    r = run_bass_kernel_spmd(nc, [arrays], core_ids=[0])
    return r.results[0]["result"].reshape(BATCH, SEQ, DIM)
```

```python
from contextlib import ExitStack

import concourse.bass as bass
from concourse import mybir

ALU = mybir.AluOpType
ACT = mybir.ActivationFunctionType
AX_X = mybir.AxisListType.X
F32 = mybir.dt.float32
BF16 = mybir.dt.bfloat16
U32 = mybir.dt.uint32
U8 = mybir.dt.uint8

P = 128
BATCH, SEQ, DIM = 128, 64, 128
PAIRS = BATCH // 2
HEADS = 16
HD = DIM // HEADS
XH = 64
INNER = HEADS * XH
EPS = 1e-5
NEG = -1e30
FH = 8
KEYS = 128
EXPERTS = 2048
LAST = EXPERTS - 1
XROWS = EXPERTS // KEYS
FFN = 2 * DIM
TABLE = 2 * DIM + 2 * FFN
A_IN, B_IN, A_OUT, B_OUT = 0, DIM, DIM + FFN, DIM + 2 * FFN


class Pair:

    def __init__(self, base, off):
        self.base, self.off = base, off
        self.t = 2 * base + off
        self.slot = off % 2
        self.turn = base + off // 2

    def at(self, d):
        return Pair(self.base, self.off + d)

    def real(self):
        return not isinstance(self.t, int) or 0 <= self.t < PAIRS


def wait(eng, sem, value):
    if isinstance(value, int) and value <= 0:
        return
    eng.wait_ge(sem, value)


def wait_apart(eng, sem, value):
    if isinstance(value, int):
        return wait(eng, sem, value)
    eng.wait_ge(sem, value)
    eng.nop(nofuse=True)


def steps(eng, body, first, last, ahead, behind):
    peeled = behind + 3
    for s in range(first, peeled):
        body(Pair(0, s))
    turns = (PAIRS - ahead - peeled) // 2
    with eng.Fori(0, turns) as i:
        body(Pair(i, peeled))
        body(Pair(i, peeled + 1))
    for s in range(2 * turns + peeled, last + 1):
        body(Pair(0, s))


def decoder_layer(nc, x, xT, ctx_in, mask, w_attn, u_attn, sig_qkv, sig_proj,
                  gains, wq_t, wk_t, wv_t, wout, ffn_wq, keys_t, w_in_last, w_out_last, table, out):
    with ExitStack() as stack:
        def sb(name, shape, dt=F32):
            return stack.enter_context(nc.sbuf_tensor(name, shape, dt))

        def sem(name):
            return stack.enter_context(nc.semaphore(name))

        bank = stack.enter_context(nc.psum_tensor("bank", [P, 8, 512], F32))

        ident = sb("ident", [P, P])
        identb = sb("identb", [P, P], BF16)
        ones_row = sb("ones_row", [1, P])
        onesb_row = sb("onesb_row", [1, P], BF16)
        causal = sb("causal", [P, 4, SEQ], BF16)
        head_of = sb("head_of", [P, 4])
        key_mask = sb("key_mask", [1, BATCH, SEQ], BF16)
        kv_gb = sb("kv_gb", [P, 2, 2, DIM])
        eps_t = sb("eps_t", [P, 2])
        mhalf = sb("mhalf", [P, 2])
        mones = sb("mones", [P, 2])
        rev_row = sb("rev_row", [P, XROWS])
        gb = sb("gb", [P, 6, DIM])
        w_self = sb("w_self", [P, 4 * DIM])
        fold_a = sb("fold_a", [P, HEADS, DIM])
        fold_b = sb("fold_b", [P, HEADS, DIM])
        fold_g = sb("fold_g", [P, HEADS, KEYS])
        hid_w = sb("hid_w", [P, FFN + 2])
        out_w = sb("out_w", [P, 2, DIM + 2])
        last_row = sb("last_row", [P, TABLE])
        X = sb("X", [P, PAIRS, DIM])

        rows = [sb(f"rows{p}", [P, FH, TABLE]) for p in range(2)]

        GX, BX, GL, BL, GO, BO = range(6)

        consts_ready = sem("consts_ready")
        const_step = sem("const_step")
        rows_zeroed = sem("rows_zeroed")
        weights_in = sem("weights_in")
        self_in = sem("self_in")
        fold_in = [sem(f"fold_in{n}") for n in range(3)]
        norm_a = sem("norm_a")
        norm_row = sem("norm_row")
        norm_copied = sem("norm_copied")
        norm_sq = sem("norm_sq")
        norm_pow = sem("norm_pow")
        norm_c = sem("norm_c")
        norm_cb = sem("norm_cb")
        self_ready = sem("self_ready")
        fold_done = sem("fold_done")
        fold_a_copied = sem("fold_a_copied")
        fold_copied = sem("fold_copied")
        mask_in = sem("mask_in")
        mask_ready = sem("mask_ready")

        with ExitStack() as prep:
            def prep_sb(name, shape, dt=F32):
                return prep.enter_context(nc.sbuf_tensor(name, shape, dt))

            factors = prep_sb("factors", [P, 6, 8, DIM])
            rows_i = prep_sb("rows_i", [P, KEYS], mybir.dt.int32)
            mask_u8 = prep_sb("mask_u8", [1, BATCH, SEQ], U8)
            u_self = prep_sb("u_self", [P, 4 * DIM])
            wu = prep_sb("wu", [P, 4 * DIM])
            a_self = prep_sb("a_self", [P, 2])
            row_self = prep_sb("row_self", [1, 4 * DIM])
            row_sq = prep_sb("row_sq", [1, 4 * DIM])
            norms = prep_sb("norms", [1, 4])
            norms_p = prep_sb("norms_p", [1, 4])
            powers = prep_sb("powers", [1, 4])
            sigmas = prep_sb("sigmas", [1, 2])
            c_row = prep_sb("c_row", [1, 2])
            c_all = prep_sb("c_all", [P, 2])

            block = prep.enter_context(nc.Block())

            def fold_ps(n):
                return bank[:, 2 + 2 * n:4 + 2 * n, 0:2 * DIM].rearrange("p e (c d) -> p e c d", c=2)

            @block.sync
            def _(sp):
                sp.dma_start(w_self[:, :], w_attn).then_inc(self_in, 16)
                sp.dma_start(u_self[:, :], u_attn.partition_broadcast(P)).then_inc(self_in, 16)
                sp.dma_start(sigmas[:, 0:1], sig_qkv.rearrange("(a n) -> a n", a=1)).then_inc(self_in, 16)
                sp.dma_start(sigmas[:, 1:2], sig_proj.rearrange("(a n) -> a n", a=1)).then_inc(self_in, 16)
                sp.dma_start(mask_u8[:, :, :], mask.rearrange("(a b) s -> a b s", a=1)).then_inc(mask_in, 16)
                for n, w in enumerate((wq_t, wk_t, wv_t, wout, ffn_wq, keys_t)):
                    sp.dma_start(factors[:, n, :, :], w.rearrange("(c p) d -> p c d", p=P)).then_inc(fold_in[n // 2], 16)
                sp.dma_start(gb[:, :, :].rearrange("p a b -> p (a b)"), gains.partition_broadcast(P)).then_inc(weights_in, 16)
                sp.dma_start(hid_w[:, :], w_in_last).then_inc(weights_in, 16)
                sp.dma_start(out_w[:, :, :], w_out_last.rearrange("(c p) d -> p c d", p=P)).then_inc(weights_in, 16)
                sp.dma_start(last_row[:, :], table[LAST, :].partition_broadcast(P)).then_inc(weights_in, 16)
                sp.wait_ge(weights_in, 4 * 16)

            @block.gpsimd
            def _(pool):
                made = 0

                def settle(instruction):
                    nonlocal made
                    made += 1
                    instruction.then_inc(const_step, 1)
                    pool.wait_ge(const_step, made)

                settle(nc.gpsimd.memset(ident[:, :], 0.0))
                settle(nc.gpsimd.affine_select(out=ident[:, :], in_=ident[:, :], compare_op=ALU.not_equal, fill=1.0,
                                               base=0, pattern=[[-1, P]], channel_multiplier=1))
                settle(nc.gpsimd.iota(rows_i[:, :], pattern=[[-1, KEYS]], base=KEYS, channel_multiplier=0))
                settle(nc.gpsimd.memset(powers[:, 0:2], 0.5))
                settle(nc.gpsimd.memset(powers[:, 2:4], -0.5))
                settle(nc.gpsimd.memset(eps_t[:, :], EPS))
                settle(nc.gpsimd.memset(mhalf[:, :], -0.5))
                settle(nc.gpsimd.memset(mones[:, :], -1.0))
                settle(nc.gpsimd.memset(causal[:, :, :], 0.0))
                for b in range(2):
                    half = causal[SEQ * b:SEQ * b + SEQ, :, :]
                    settle(nc.gpsimd.affine_select(out=half, in_=half, compare_op=ALU.is_ge, fill=NEG, base=0,
                                                   pattern=[[0, 4], [-1, SEQ]], channel_multiplier=1))
                settle(nc.gpsimd.memset(head_of[:, :], 1.0))
                for j in range(4):
                    quad = head_of[32 * j:32 * j + 32, :]
                    settle(nc.gpsimd.affine_select(out=quad, in_=quad, compare_op=ALU.is_ge, fill=0.0, base=0,
                                                   pattern=[[-HD, 4]], channel_multiplier=1))
                    settle(nc.gpsimd.affine_select(out=quad, in_=quad, compare_op=ALU.is_ge, fill=0.0, base=HD - 1,
                                                   pattern=[[HD, 4]], channel_multiplier=-1))
                pool.wait_ge(norm_sq, 4)
                nc.gpsimd.tensor_tensor(norms_p[:, :], norms[:, :], powers[:, :], ALU.pow).then_inc(norm_pow, 1)
                for p in range(2):
                    nc.gpsimd.memset(rows[p][:, :, :].rearrange("p h c -> p (h c)"), 0.0).then_inc(rows_zeroed, 1)

            @block.vector
            def _(dve):
                nc.vector.memset(ones_row[:, :], 1.0).then_inc(consts_ready, 1)
                nc.vector.memset(onesb_row[:, :], 1.0).then_inc(consts_ready, 1)
                dve.wait_ge(const_step, 2)
                nc.vector.tensor_copy(identb[:, :], ident[:, :]).then_inc(consts_ready, 1)
                dve.wait_ge(const_step, 3)
                nc.vector.tensor_scalar(rev_row[:, :], rows_i[:, 0:XROWS], float(XROWS - KEYS), None,
                                        ALU.add).then_inc(consts_ready, 1)
                dve.wait_ge(self_in, 4 * 16)
                nc.vector.tensor_tensor(wu[:, :], w_self[:, :], u_self[:, :], ALU.mult).then_inc(norm_a, 1)
                dve.wait_ge(norm_a, 1)
                nc.vector.tensor_reduce(a_self[:, 0:1], wu[:, 0:3 * DIM], AX_X, ALU.add).then_inc(norm_a, 1)
                nc.vector.tensor_reduce(a_self[:, 1:2], wu[:, 3 * DIM:4 * DIM], AX_X, ALU.add).then_inc(norm_a, 1)
                dve.wait_ge(norm_row, 1)
                nc.vector.tensor_copy(row_self[:, :], bank[0:1, 0, :]).then_inc(norm_copied, 1)
                nc.vector.tensor_copy(norms[:, 0:2], bank[0:1, 1, 0:2]).then_inc(norm_sq, 1)
                dve.wait_ge(norm_copied, 1)
                nc.vector.tensor_tensor(row_sq[:, :], row_self[:, :], row_self[:, :], ALU.mult).then_inc(norm_sq, 1)
                dve.wait_ge(norm_sq, 2)
                nc.vector.tensor_reduce(norms[:, 2:3], row_sq[:, 0:3 * DIM], AX_X, ALU.add).then_inc(norm_sq, 1)
                nc.vector.tensor_reduce(norms[:, 3:4], row_sq[:, 3 * DIM:4 * DIM], AX_X, ALU.add).then_inc(norm_sq, 1)
                dve.wait_ge(norm_pow, 1)
                nc.vector.tensor_tensor(c_row[:, :], norms_p[:, 0:2], norms_p[:, 2:4], ALU.mult).then_inc(norm_c, 1)
                dve.wait_ge(norm_c, 1)
                nc.vector.tensor_tensor(c_row[:, :], c_row[:, :], sigmas[:, :], ALU.mult).then_inc(norm_c, 1)
                dve.wait_ge(norm_cb, 1)
                nc.vector.tensor_copy(c_all[:, :], bank[:, 1, 0:2]).then_inc(norm_c, 1)
                dve.wait_ge(norm_c, 3)
                nc.vector.tensor_scalar(w_self[:, 0:DIM], w_self[:, 0:DIM], c_all[:, 0:1], float(HD) ** -0.5,
                                        ALU.mult, ALU.mult).then_inc(self_ready, 1)
                nc.vector.tensor_scalar(w_self[:, DIM:3 * DIM], w_self[:, DIM:3 * DIM], c_all[:, 0:1], None,
                                        ALU.mult).then_inc(self_ready, 1)
                nc.vector.tensor_scalar(w_self[:, 3 * DIM:], w_self[:, 3 * DIM:], c_all[:, 1:2], None,
                                        ALU.mult).then_inc(self_ready, 1)
                for g in range(4):
                    for n, dst in enumerate((fold_b, fold_g)):
                        dve.wait_ge(fold_done, 3 * g + 2 + n)
                        nc.vector.tensor_copy(dst[:, 4 * g:4 * g + 4, :].rearrange("p (c e) d -> p e c d", e=2),
                                              fold_ps(n + 1)).then_inc(fold_copied, 1)
                dve.wait_ge(weights_in, 4 * 16)
                for n, (of_x, of_ctx) in enumerate(((GL, GX), (BL, BX))):
                    for b in range(2):
                        for half in range(2):
                            rows = slice(SEQ * half, SEQ * half + SEQ)
                            which = of_x if half == b else of_ctx
                            nc.vector.tensor_copy(kv_gb[rows, n, b, :], gb[rows, which, :]).then_inc(mask_ready, 1)

            @block.scalar
            def _(act):
                act.wait_ge(mask_in, 16)
                nc.scalar.activation(key_mask[:, :, :], mask_u8[:, :, :], ACT.Copy, bias=NEG,
                                     scale=-NEG).then_inc(mask_ready, 1)
                for g in range(4):
                    act.wait_ge(fold_done, 3 * g + 1)
                    nc.scalar.activation(fold_a[:, 4 * g:4 * g + 4, :].rearrange("p (c e) d -> p e c d", e=2),
                                         fold_ps(0), ACT.Copy, scale=XH ** -0.5).then_inc(fold_a_copied, 1)

            @block.tensor
            def _(pe):
                pe.wait_ge(norm_a, 3)
                nc.tensor.matmul(bank[0:1, 0, 0:3 * DIM], a_self[:, 0:1], w_self[:, 0:3 * DIM], start=True, stop=True)
                nc.tensor.matmul(bank[0:1, 0, 3 * DIM:4 * DIM], a_self[:, 1:2], w_self[:, 3 * DIM:4 * DIM],
                                 start=True, stop=True)
                for n in range(2):
                    last = nc.tensor.matmul(bank[0:1, 1, n:n + 1], a_self[:, n:n + 1], a_self[:, n:n + 1],
                                            start=True, stop=True)
                last.then_inc(norm_row, 1)
                for g in range(4):
                    for n in range(3):
                        if g == 0:
                            pe.wait_ge(fold_in[n], 2 * 16)
                        elif n == 0:
                            pe.wait_ge(fold_a_copied, g)
                        else:
                            pe.wait_ge(fold_copied, 2 * (g - 1) + n)
                        for k in range(4):
                            lo = XH * (k % 2)
                            c = 2 * g + k // 2
                            last = nc.tensor.matmul(bank[:, 2 + 2 * n + k % 2, (k // 2) * DIM:(k // 2 + 1) * DIM],
                                                    factors[lo:lo + XH, 2 * n, c, :],
                                                    factors[lo:lo + XH, 2 * n + 1, c, :], start=True, stop=True)
                        last.then_inc(fold_done, 1)
                    if g == 0:
                        pe.wait_ge(norm_c, 2)
                        pe.wait_ge(norm_sq, 2)
                        nc.tensor.matmul(bank[:, 1, 0:2], ones_row[:, :], c_row[:, :],
                                         start=True, stop=True).then_inc(norm_cb, 1)

        self_attention(nc, bank, x, xT, X, w_self, ident, identb, causal, head_of, eps_t, mhalf)
        cross_attention_and_experts(nc, bank, ctx_in, X, gb, kv_gb, fold_a, fold_b, ident, ones_row, onesb_row,
                                    key_mask, eps_t,
                                    mhalf, mones, fold_g, hid_w, out_w, last_row, table, rev_row, rows, out)


def self_attention(nc, bank, x, xT, X, w_self, ident, identb, causal, head_of, eps_t, mhalf):
    with ExitStack() as stack:
        def sb(name, shape, dt=F32):
            return stack.enter_context(nc.sbuf_tensor(name, shape, dt))

        def sem(name):
            return stack.enter_context(nc.semaphore(name))

        x_t = [sb(f"x_t{p}", [P, 2, 2, SEQ]) for p in range(2)]
        x_row = [sb(f"x_row{p}", [P, DIM]) for p in range(2)]
        q_t = sb("q_t", [P, 2 * SEQ])
        k_blocks = sb("k_blocks", [P, 2, 4, SEQ])
        v_blocks = [sb(f"v_blocks{p}", [P, 2, 4, 4, 2 * HD]) for p in range(2)]
        ones_blocks = sb("ones_blocks", [P, 4, 2 * HD])
        probs = [sb(f"probs{p}", [P, HEADS, SEQ]) for p in range(2)]
        probs_t = sb("probs_t", [P, 8, P])
        top = sb("top", [P, HEADS])
        inv = sb("inv", [P, P])
        heads_out_t = sb("heads_out_t", [P, DIM])
        resid = sb("resid", [P, DIM])
        stats = sb("stats", [P, 6])
        mv = sb("mv", [P, 2])
        var_eps = sb("var_eps", [P, 1])
        rstd = sb("rstd", [P, 1])

        t_loaded = [sem(f"a_t_loaded{p}") for p in range(2)]
        row_loaded = [sem(f"a_row_loaded{p}") for p in range(2)]
        zeroed = sem("a_zeroed")
        qkv_done = sem("a_qkv_done")
        q_copied = sem("a_q_copied")
        v_spread = sem("a_v_spread")
        k_spread = sem("a_k_spread")
        scores_done = sem("a_scores_done")
        top_done = sem("a_top_done")
        shifted = sem("a_shifted")
        exp_done = sem("a_exp_done")
        inv_done = sem("a_inv_done")
        turned = sem("a_turned")
        turned_copied = sem("a_turned_copied")
        pv_done = sem("a_pv_done")
        heads_scaled = sem("a_heads_scaled")
        projected = sem("a_projected")
        resid_done = sem("a_resid_done")
        stats_done = sem("a_stats_done")
        mv_done = sem("a_mv_done")
        eps_added = sem("a_eps_added")
        rstd_done = sem("a_rstd_done")
        normed = sem("a_normed")

        qkv_ps = bank[:, 0, :]
        scores_ps = bank[:, 1:5, 0:4 * SEQ]
        turned_ps = bank[:, 5:7, :]
        pv_ps = bank[:, 7, 0:P]
        sums_ps = bank[:, 7, P:2 * P]
        projected_ps = bank[:, 7, 2 * P:2 * P + DIM]
        LOOP = {"ahead": 2, "behind": 1}
        block = stack.enter_context(nc.Block())

        @block.sync
        def _(sp):
            def step(n):
                if n.real():
                    wait(sp, v_spread, 2 * (n.t - 1))
                    for c in range(2):
                        sp.dma_start(x_t[n.slot][:, :, c, :],
                                     xT[:, bass.ds(n.t * P, P)].rearrange("d (b s) -> d b s", b=2)
                                     ).then_inc(t_loaded[n.slot], 16)
                n = n.at(-1)
                if n.real():
                    wait(sp, resid_done, n.t - 1)
                    sp.dma_start(x_row[n.slot][:, :], x[bass.ds(n.t * P, P), :]).then_inc(row_loaded[n.slot], 16)
            steps(sp, step, 0, PAIRS + 1, **LOOP)

        @block.tensor
        def _(pe):
            def scores(n):
                if not n.real():
                    return
                pe.wait_ge(q_copied, n.t + 1)
                pe.wait_ge(k_spread, n.t + 1)
                wait(pe, shifted, n.t)
                for j in range(4):
                    nc.tensor.matmul(scores_ps[:, j, :], identb[:, :],
                                     causal[:, :, :].rearrange("p g k -> p (g k)"),
                                     start=True, stop=False, skip_group_check=True)
                for b in range(2):
                    for j in range(4):
                        last = nc.tensor.matmul(scores_ps[SEQ * b:SEQ * b + SEQ, j, :],
                                                q_t[32 * j:32 * j + 32, SEQ * b:SEQ * b + SEQ],
                                                k_blocks[32 * j:32 * j + 32, b, :, :].rearrange("p g k -> p (g k)"),
                                                start=False, stop=True, skip_group_check=True)
                last.then_inc(scores_done, 1)

            def turn(n):
                if not n.real():
                    return
                pe.wait_ge(exp_done, n.t + 1)
                wait(pe, turned_copied, n.t)
                for c in range(8):
                    last = nc.tensor.transpose(turned_ps[:, c // 4, (c % 4) * P:(c % 4 + 1) * P],
                                               probs[n.slot][:, 2 * c:2 * c + 2, :].rearrange("p h k -> p (h k)"),
                                               ident[:, :])
                last.then_inc(turned, 1)

            def project(n):
                if not n.real():
                    return
                pe.wait_ge(heads_scaled, n.t + 1)
                nc.tensor.matmul(projected_ps, heads_out_t[:, :], w_self[:, 3 * DIM:4 * DIM],
                                 start=True, stop=True).then_inc(projected, 1)

            def qkv(n):
                m = n.at(1)
                if not n.real() and not m.real():
                    return
                wait(pe, q_copied, n.t + 1)
                wait(pe, k_spread, n.t + 1)
                wait(pe, v_spread, 2 * n.t)
                if m.real():
                    pe.wait_ge(t_loaded[m.slot], 32 * (m.turn + 1))
                    for c in range(2):
                        last = nc.tensor.matmul(qkv_ps[:, c * P:(c + 1) * P], w_self[:, c * DIM:(c + 1) * DIM],
                                                x_t[m.slot][:, :, 0, :], start=True, stop=True)
                if n.real():
                    for b in range(2):
                        last = nc.tensor.matmul(qkv_ps[:, (2 + b) * P:(3 + b) * P],
                                                x_t[n.slot][:, b, :, :].rearrange("p c s -> p (c s)"),
                                                w_self[:, 2 * DIM:3 * DIM], start=True, stop=True)
                last.then_inc(qkv_done, 1)

            def values(n):
                if not n.real():
                    return
                pe.wait_ge(turned_copied, n.t + 1)
                pe.wait_ge(v_spread, 2 * (n.t + 1))
                wait(pe, resid_done, n.t)
                for j in range(4):
                    quad = slice(32 * j, 32 * j + 32)
                    for b in range(2):
                        for e in range(2):
                            nc.tensor.matmul(pv_ps[quad, SEQ * b:SEQ * b + SEQ],
                                             v_blocks[n.slot][:, b, j, 2 * e:2 * e + 2, :].rearrange("p c r -> p (c r)"),
                                             probs_t[:, 2 * j + e, SEQ * b:SEQ * b + SEQ], start=(e == 0),
                                             stop=(e == 1), skip_group_check=True)
                    for e in range(2):
                        last = nc.tensor.matmul(sums_ps[quad, :],
                                                ones_blocks[:, 2 * e:2 * e + 2, :].rearrange("p c r -> p (c r)"),
                                                probs_t[:, 2 * j + e, :], start=(e == 0), stop=(e == 1),
                                                skip_group_check=True)
                last.then_inc(pv_done, 1)

            def step(s):
                scores(s.at(1))
                project(s.at(-1))
                turn(s)
                qkv(s.at(1))
                values(s)
            steps(pe, step, -3, PAIRS + 3, **LOOP)

        @block.scalar
        def _(act):
            def turn_copy(n):
                if not n.real():
                    return
                act.wait_ge(turned, n.t + 1)
                wait(act, pv_done, n.t)
                nc.scalar.activation(probs_t[:, :, :].rearrange("p c k -> p (c k)"),
                                     turned_ps.rearrange("p c k -> p (c k)"), ACT.Copy).then_inc(turned_copied, 1)

            def q_copy(n):
                if not n.real():
                    return
                act.wait_ge(qkv_done, n.t + 1)
                wait(act, scores_done, n.t)
                nc.scalar.activation(q_t[:, :], qkv_ps[:, 0:P], ACT.Copy).then_inc(q_copied, 1)

            def v_copy(n):
                if not n.real():
                    return
                act.wait_ge(qkv_done, n.t + 2)
                act.wait_ge(zeroed, 2)
                wait(act, pv_done, n.t - 1)
                for e in range(2):
                    rows = slice(SEQ * e, SEQ * e + SEQ)
                    nc.scalar.activation(v_blocks[n.slot][rows, :, :, 0:4:3, HD * e:HD * e + HD]
                                         .rearrange("p b j c r -> p (b j) c r"),
                                         qkv_ps[rows, 2 * P:4 * P].rearrange("p (x c e r) -> p x c e r",
                                                                             x=8, c=2, e=2)[:, :, :, e, :],
                                         ACT.Copy).then_inc(v_spread, 1)

            def exps(n):
                if not n.real():
                    return
                act.wait_ge(shifted, n.t + 1)
                nc.scalar.activation(probs[n.slot][:, :, :], probs[n.slot][:, :, :], ACT.Exp).then_inc(exp_done, 1)

            def step(s):
                turn_copy(s)
                q_copy(s.at(2))
                v_copy(s.at(1))
                exps(s.at(1))
            steps(act, step, -3, PAIRS + 3, **LOOP)

        @block.gpsimd
        def _(pool):
            def scale(n):
                if not n.real():
                    return
                pool.wait_ge(mv_done, n.t + 1)
                wait(pool, normed, n.t)
                nc.gpsimd.tensor_tensor(var_eps[:, :], mv[:, 1:2], eps_t[:, 0:1], ALU.add).then_inc(eps_added, 1)
                pool.wait_ge(eps_added, n.t + 1)
                nc.gpsimd.tensor_tensor(rstd[:, :], var_eps[:, :], mhalf[:, 0:1], ALU.pow).then_inc(rstd_done, 1)

            def step(s):
                scale(s)
            steps(pool, step, -3, PAIRS + 3, **LOOP)

        @block.vector
        def _(dve):
            for p in range(2):
                nc.vector.memset(v_blocks[p][:, :, :, :, :].rearrange("p a b c d -> p (a b c d)"), 0.0).then_inc(zeroed, 1)
            nc.vector.memset(ones_blocks[:, :, :].rearrange("p a b -> p (a b)"), 0.0).then_inc(zeroed, 1)
            dve.wait_ge(zeroed, 3)
            for e in range(2):
                nc.vector.memset(ones_blocks[SEQ * e:SEQ * e + SEQ, 0:4:3, HD * e:HD * e + HD], 1.0).then_inc(zeroed, 1)
            dve.wait_ge(zeroed, 5)

            heads = scores_ps.rearrange("p j (g k) -> p j g k", g=4)

            def tops(n):
                if not n.real():
                    return
                dve.wait_ge(scores_done, n.t + 1)
                nc.vector.tensor_reduce(top[:, :], heads, AX_X, ALU.max).then_inc(top_done, 1)

            def residual(n):
                if not n.real():
                    return
                dve.wait_ge(projected, n.t + 1)
                dve.wait_ge(row_loaded[n.slot], 16 * (n.turn + 1))
                wait(dve, normed, n.t)
                nc.vector.tensor_tensor(resid[:, :], x_row[n.slot][:, :], projected_ps, ALU.add).then_inc(resid_done, 1)

            def shift(n):
                if not n.real():
                    return
                dve.wait_ge(top_done, n.t + 1)
                wait(dve, turned, n.t - 1)
                nc.vector.tensor_tensor(
                    probs[n.slot][:, :, :].rearrange("p (j g) k -> p j g k", g=4), heads,
                    top[:, :].rearrange("p (j g k) -> p j g k", g=4, k=1).broadcast_to([P, 4, 4, SEQ]),
                    ALU.subtract).then_inc(shifted, 1)

            def moments(n):
                if not n.real():
                    return
                dve.wait_ge(resid_done, n.t + 1)
                nc.vector.bn_stats(stats[:, :], resid[:, :]).then_inc(stats_done, 1)

            def spread(n):
                if not n.real():
                    return
                dve.wait_ge(qkv_done, n.t + 1)
                dve.wait_ge(q_copied, n.t + 1)
                wait(dve, v_spread, 2 * n.t)
                wait(dve, scores_done, n.t)
                nc.vector.tensor_tensor(
                    k_blocks[:, :, :, :],
                    qkv_ps[:, P:2 * P].rearrange("p (b g k) -> p b g k", b=2, g=1).broadcast_to([P, 2, 4, SEQ]),
                    head_of[:, :].rearrange("p (b g k) -> p b g k", b=1, k=1).broadcast_to([P, 2, 4, SEQ]),
                    ALU.mult).then_inc(k_spread, 1)

            def aggregate(n):
                if not n.real():
                    return
                wait_apart(dve, stats_done, n.t + 1)
                nc.vector.bn_aggr(mv[:, :], stats[:, :]).then_inc(mv_done, 1)

            def invert(n):
                if not n.real():
                    return
                dve.wait_ge(pv_done, n.t + 1)
                nc.vector.reciprocal(inv[:, :], sums_ps).then_inc(inv_done, 1)

            def scale_heads(n):
                if not n.real():
                    return
                dve.wait_ge(inv_done, n.t + 1)
                wait(dve, projected, n.t)
                nc.vector.tensor_tensor(heads_out_t[:, :], pv_ps, inv[:, :], ALU.mult).then_inc(heads_scaled, 1)

            def norm(n):
                if not n.real():
                    return
                dve.wait_ge(rstd_done, n.t + 1)
                nc.vector.tensor_scalar(X[:, n.t, :], resid[:, :], mv[:, 0:1], rstd[:, 0:1],
                                        ALU.subtract, ALU.mult).then_inc(normed, 1)

            def step(s):
                tops(s.at(1))
                residual(s.at(-1))
                shift(s.at(1))
                spread(s.at(2))
                moments(s.at(-1))
                invert(s)
                aggregate(s.at(-1))
                scale_heads(s)
                norm(s.at(-1))
            steps(dve, step, -3, PAIRS + 3, **LOOP)
            dve.wait_ge(normed, PAIRS)


def cross_attention_and_experts(nc, bank, ctx_in, X, gb, kv_gb, fold_a, fold_b, ident, ones_row, onesb_row, key_mask, eps_t,
                                mhalf, mones, fold_g, hid_w, out_w, last_row, table, rev_row, rows, out):
    GX, BX, GL, BL, GO, BO = range(6)
    EXP = FH + 1
    LOOP = {"ahead": 2, "behind": 7}
    with ExitStack() as stack:
        def sb(name, shape, dt=F32):
            return stack.enter_context(nc.sbuf_tensor(name, shape, dt))

        def sem(name):
            return stack.enter_context(nc.semaphore(name))

        c_row = [sb(f"c_row{p}", [P, DIM]) for p in range(2)]
        kv_stats = sb("kv_stats", [P, 2, 6])
        kv_mv = sb("kv_mv", [P, 2, 2])
        kv_eps = sb("kv_eps", [P, 2])
        kv_rstd = sb("kv_rstd", [P, 2])
        kv_nmean = sb("kv_nmean", [P, 2])
        kv_shift = sb("kv_shift", [P, 2])
        kv_hat = sb("kv_hat", [P, 2, DIM])
        kv = [sb(f"kv{p}", [P, 2, DIM]) for p in range(2)]
        kv_t = [sb(f"kv_t{p}", [P, 2, P]) for p in range(2)]
        q_t = [sb(f"xq_t{p}", [P, 2, HEADS, SEQ]) for p in range(2)]
        ntop = [sb(f"ntop{p}", [P, 4]) for p in range(2)]
        total = [sb(f"xtotal{p}", [P, 4]) for p in range(2)]
        inv = [sb(f"xinv{p}", [P, 4]) for p in range(2)]
        probs = [sb(f"xprobs{p}", [P, 4, P]) for p in range(2)]
        probs_t = [sb(f"xprobs_t{p}", [P, 512]) for p in range(2)]
        z_t = [sb(f"z_t{p}", [P, HEADS, 2, SEQ]) for p in range(2)]
        o_stats = sb("o_stats", [P, 2, 6])
        o_mv = sb("o_mv", [P, 2, 2])
        o_eps = sb("o_eps", [P, 2])
        o_rstd = sb("o_rstd", [P, 2])
        o_nmean = sb("o_nmean", [P, 1])
        o_shift = sb("o_shift", [P, 1])
        o_row = sb("o_row", [P, DIM])
        x_bias = sb("x_bias", [P, DIM])
        o_resid = sb("o_resid", [P, DIM])

        c_loaded = [sem(f"c_loaded{p}") for p in range(2)]
        kv_stats_done = sem("kv_stats_done")
        kv_mv_done = sem("kv_mv_done")
        kv_eps_done = sem("kv_eps_done")
        kv_rstd_done = sem("kv_rstd_done")
        kv_nmean_done = sem("kv_nmean_done")
        kv_shift_done = sem("kv_shift_done")
        kv_hat_done = sem("kv_hat_done")
        kv_gained = sem("kv_gained")
        kv_done = sem("kv_done")
        turned_in = sem("turned_in")
        kv_copied = sem("kv_copied")
        q_done = sem("q_done")
        q_copied = sem("xq_copied")
        scores_done = sem("xscores_done")
        top_done = sem("xtop_done")
        exp_done = sem("xexp_done")
        inv_done = sem("xinv_done")
        scaled = sem("scaled")
        turned = sem("xturned")
        turned_copied = sem("xturned_copied")
        z_done = sem("z_done")
        z_copied = sem("z_copied")
        y_done = sem("y_done")
        y_read = sem("y_read")
        o_stats_done = sem("o_stats_done")
        o_mv_done = sem("o_mv_done")
        o_eps_done = sem("o_eps_done")
        o_rstd_done = sem("o_rstd_done")
        o_nmean_done = sem("o_nmean_done")
        o_shift_done = sem("o_shift_done")
        x_biased = sem("x_biased")
        o_resid_done = sem("o_resid_done")
        x_normed = sem("x_normed")

        x_now = sb("x_now", [P, DIM])
        x_t = [sb(f"ex_t{p}", [P, P]) for p in range(2)]
        x_lin = sb("x_lin", [P, DIM])
        best_x = sb("best_x", [P, FH])
        best_y = sb("best_y", [P, FH, 8])
        key_y = sb("key_y", [P, FH, 8], U32)
        row_hit = sb("row_hit", [P, FH, XROWS])
        row_rev = sb("row_rev", [P, FH, XROWS])
        row_code = sb("row_code", [P, FH])
        row_base = sb("row_base", [P, FH])
        index = [sb(f"index{p}", [P, FH], U32) for p in range(2)]
        gate_sum = sb("gate_sum", [P, FH])
        gate_all = sb("gate_all", [P, FH])
        gate_out = sb("gate_out", [P, FH])
        gate = [sb(f"gate{p}", [P, EXP]) for p in range(2)]
        prod = sb("prod", [P, FH, FFN])
        lin = sb("lin", [P, EXP])
        lin_g = sb("lin_g", [P, EXP])
        hidden = sb("hidden", [P, FFN])
        act_h = sb("act_h", [P, FFN])
        spare = sb("spare", [1, 2])
        spare_in = ones_row[:, 0:2]
        act_t = sb("act_t", [P, 2, P])
        lout = sb("lout", [P, EXP])
        lout_g = sb("lout_g", [P, EXP])
        e_resid = [sb(f"e_resid{p}", [P, DIM]) for p in range(2)]
        e_stats = sb("e_stats", [P, 6])
        e_mv = sb("e_mv", [P, 2])
        e_eps = sb("e_eps", [P, 1])
        e_rstd = sb("e_rstd", [P, 1])
        e_nmean = sb("e_nmean", [P, 1])
        e_shift = sb("e_shift", [P, 1])
        result = [sb(f"result{p}", [P, DIM]) for p in range(2)]

        x_staged = sem("x_staged")
        x_t_copied = sem("x_t_copied")
        sims_done = sem("sims_done")
        best_done = sem("best_done")
        tops_y_done = sem("tops_y_done")
        sims_read = sem("sims_read")
        row_rev_done = sem("row_rev_done")
        row_code_done = sem("row_code_done")
        row_base_done = sem("row_base_done")
        gate_sum_done = sem("gate_sum_done")
        gate_all_done = sem("gate_all_done")
        index_done = sem("index_done")
        gate_done = sem("gate_done")
        gathered = [sem(f"gathered{p}") for p in range(2)]
        x_lin_done = sem("x_lin_done")
        hid_done = sem("hid_done")
        lin_done = sem("lin_done")
        lin_g_done = sem("lin_g_done")
        hidden_step = sem("hidden_step")
        gelu_done = sem("gelu_done")
        table_back = sem("table_back")
        act_turned = sem("act_turned")
        act_copied = sem("act_copied")
        out_done = sem("out_done")
        lout_done = sem("lout_done")
        lout_g_done = sem("lout_g_done")
        resid_step = sem("resid_step")
        e_stats_done = sem("e_stats_done")
        e_mv_done = sem("e_mv_done")
        e_eps_done = sem("e_eps_done")
        e_rstd_done = sem("e_rstd_done")
        e_nmean_done = sem("e_nmean_done")
        e_shift_done = sem("e_shift_done")
        result_done = sem("x_result_done")
        stored = [sem(f"stored{p}") for p in range(2)]

        scores_ps = [bank[:, 0, :], bank[:, 1, :]]
        turned_ps = bank[:, 2, :]
        z_ps = bank[:, 3, :]
        q_ps = bank[:, 4, :]
        kv_turn_ps = bank[:, 4, 0:2 * P]
        x_turn_ps = bank[:, 4, 2 * P:3 * P]
        y_ps = bank[:, 4, 0:DIM]
        sims_ps = [bank[:, 5, :], bank[:, 6, :]]
        hid_ps = bank[:, 7, 0:FFN + 2]
        act_turn_ps = bank[:, 7, 0:2 * P]
        out_ps = bank[:, 7, 0:DIM + 2]
        block = stack.enter_context(nc.Block())

        @block.sync
        def _(sp):
            def step(s):
                n = s.at(2)
                if n.real():
                    wait(sp, kv_hat_done, 4 * (n.t - 1))
                    for b in range(2):
                        sp.dma_start(c_row[n.slot][SEQ * (1 - b):SEQ * (2 - b), :],
                                     ctx_in[bass.ds(n.t * P + SEQ * b, SEQ), :]).then_inc(c_loaded[n.slot], 16)
                n = s.at(-5)
                if n.real():
                    sp.wait_ge(result_done, n.t + 1)
                    sp.dma_start(out[bass.ds(n.t * P, P), :], result[n.slot][:, :]).then_inc(stored[n.slot], 16)
            steps(sp, step, -3, PAIRS + 6, **LOOP)
            for p in range(2):
                sp.wait_ge(stored[p], 16 * (PAIRS // 2))

        @block.tensor
        def _(pe):
            def inputs_turn(n, r):
                if n.real():
                    pe.wait_ge(kv_done, n.t + 1)
                    wait(pe, y_read, n.t - 1)
                    for b in range(2):
                        last = nc.tensor.transpose(kv_turn_ps[:, b * P:(b + 1) * P], kv[n.slot][:, b, :], ident[:, :])
                if r.real():
                    pe.wait_ge(x_staged, r.t + 1)
                    wait(pe, y_read, r.t + 2 if r.at(1).real() else PAIRS)
                    last = nc.tensor.transpose(x_turn_ps, x_now[:, :], ident[:, :])
                if n.real() or r.real():
                    last.then_inc(turned_in, 1)

            def queries(n, c):
                if not n.real():
                    return
                pe.wait_ge(kv_copied, n.t + 1)
                wait(pe, x_t_copied, n.t - 2)
                wait(pe, q_copied, 4 * n.t + c)
                x_tokens = kv_t[n.slot][:, :, :].rearrange("p b (e q) -> p (b e) q", e=2)[:, 0:4:3, :]
                for h in range(4):
                    last = nc.tensor.matmul(q_ps[:, h * P:(h + 1) * P], fold_a[:, 4 * c + h, :], x_tokens,
                                            start=True, stop=True)
                last.then_inc(q_done, 1)

            def scores(n, u):
                if not n.real():
                    return
                b, half = u % 2, u // 2
                wait_apart(pe, q_copied, 4 * n.t + 2 * half + 2)
                wait_apart(pe, exp_done, 4 * (4 * n.t + u - 1))
                ps = scores_ps[u % 2].rearrange("p (i k) -> p i k", i=4)
                nc.tensor.matmul(ps[:, :, SEQ * (1 - b):SEQ * (2 - b)], onesb_row[:, :],
                                 key_mask[:, 2 * n.t + b, :].rearrange("a (i s) -> a i s", i=1)
                                 .broadcast_to([1, 4, SEQ]), start=True, stop=False, skip_group_check=True)
                for i in range(4):
                    h = 8 * half + 2 * i
                    last = nc.tensor.matmul(ps[:, i, :], q_t[n.slot][:, b, h:h + 2, :].rearrange("p h q -> p (h q)"),
                                            kv_t[n.slot][:, b, :], start=False, stop=True, skip_group_check=True)
                last.then_inc(scores_done, 1)

            def turn(n, u):
                if not n.real():
                    return
                pe.wait_ge(scaled, 4 * n.t + u + 1)
                wait(pe, turned_copied, 4 * n.t + u)
                for i in range(4):
                    last = nc.tensor.transpose(turned_ps[:, i * P:(i + 1) * P], probs[u % 2][:, i, :], ident[:, :])
                last.then_inc(turned, 1)

            def values(n, u):
                if not n.real():
                    return
                pe.wait_ge(turned_copied, 4 * n.t + u + 1)
                wait(pe, z_copied, 4 * n.t + u)
                nc.tensor.matmul(z_ps, kv[n.slot][:, u % 2, :], probs_t[u % 2][:, :],
                                 start=True, stop=True).then_inc(z_done, 1)

            def output(n):
                if not n.real():
                    return
                pe.wait_ge(z_copied, 4 * (n.t + 1))
                wait(pe, q_copied, 4 * (n.t + 2) if n.at(1).real() else 0)
                for h in range(HEADS):
                    last = nc.tensor.matmul(y_ps, z_t[n.slot][:, h, :, :].rearrange("p b q -> p (b q)"),
                                            fold_b[:, h, :], start=(h == 0), stop=(h == HEADS - 1))
                last.then_inc(y_done, 1)

            def similarities(n, c):
                if not n.real():
                    return
                pe.wait_ge(x_t_copied, n.t + 1)
                wait(pe, sims_read, 4 * n.t + c - 1)
                nc.tensor.matmul(sims_ps[c % 2], x_t[n.slot][:, :],
                                 fold_g[:, 4 * c:4 * c + 4, :].rearrange("p h k -> p (h k)"),
                                 start=True, stop=True).then_inc(sims_done, 1)

            def expert_hidden(n):
                if not n.real():
                    return
                wait(pe, resid_step, (EXP + 1) * (n.t - 1) + 1 if not isinstance(n.t, int) or n.t else 0)
                wait(pe, lout_done, EXP * n.t)
                nc.tensor.matmul(hid_ps, x_t[n.slot][:, :], hid_w[:, :], start=True, stop=True).then_inc(hid_done, 1)

            def expert_turn(n):
                if not n.real():
                    return
                pe.wait_ge(gelu_done, n.t + 1)
                pe.wait_ge(hidden_step, EXP * n.t + 1)
                for c in range(2):
                    last = nc.tensor.transpose(act_turn_ps[:, c * P:(c + 1) * P], act_h[:, c * P:(c + 1) * P],
                                               ident[:, :])
                last.then_inc(act_turned, 1)

            def expert_out(n):
                if not n.real():
                    return
                pe.wait_ge(act_copied, n.t + 1)
                for c in range(2):
                    last = nc.tensor.matmul(out_ps, act_t[:, c, :], out_w[:, c, :], start=(c == 0), stop=(c == 1))
                last.then_inc(out_done, 1)

            def step(s):
                values(s.at(-1), 1)
                turn(s.at(-1), 2)
                scores(s, 0)
                queries(s, 2)
                similarities(s.at(-3), 3)
                expert_turn(s.at(-5))
                values(s.at(-1), 2)
                turn(s.at(-1), 3)
                expert_out(s.at(-5))
                queries(s, 3)
                scores(s, 1)
                values(s.at(-1), 3)
                scores(s, 2)
                expert_hidden(s.at(-4))
                output(s.at(-1))
                turn(s, 0)
                scores(s, 3)
                inputs_turn(s.at(1), s.at(-2))
                values(s, 0)
                turn(s, 1)
                queries(s.at(1), 0)
                similarities(s.at(-2), 0)
                queries(s.at(1), 1)
                similarities(s.at(-2), 1)
                similarities(s.at(-2), 2)
            steps(pe, step, -3, PAIRS + 6, **LOOP)

        @block.scalar
        def _(act):
            def kv_norm(n):
                if not n.real():
                    return
                wait_apart(act, kv_shift_done, n.t + 1)
                wait_apart(act, kv_gained, n.t)
                for half in range(2):
                    r = slice(SEQ * half, SEQ * half + SEQ)
                    nc.scalar.activation(kv_hat[r, half, :], X[r, n.t, :], ACT.Identity, bias=kv_shift[r, 0:1],
                                         scale=kv_rstd[r, 0:1]).then_inc(kv_hat_done, 1)
                    nc.scalar.activation(kv_hat[r, 1 - half, :], c_row[n.slot][r, :], ACT.Identity,
                                         bias=kv_shift[r, 1:2], scale=kv_rstd[r, 1:2]).then_inc(kv_hat_done, 1)

            def out_norm(n):
                if not n.real():
                    return
                wait_apart(act, o_shift_done, n.t + 1)
                nc.scalar.activation(X[:, n.t, :], o_resid[:, :], ACT.Identity, bias=o_shift[:, 0:1],
                                     scale=o_rstd[:, 1:2]).then_inc(x_normed, 1)

            def result_norm(n):
                if not n.real():
                    return
                act.wait_ge(e_shift_done, n.t + 1)
                wait(act, stored[n.slot], 16 * n.turn)
                nc.scalar.activation(result[n.slot][:, :], e_resid[n.slot][:, :], ACT.Identity, bias=e_shift[:, 0:1],
                                     scale=e_rstd[:, 0:1]).then_inc(result_done, 1)

            def stage_x_lin(n):
                if not n.real():
                    return
                wait_apart(act, resid_step, (EXP + 1) * (n.t - 1) + 1)
                nc.scalar.activation(x_lin[:, :], X[:, n.t, :], ACT.Copy).then_inc(x_lin_done, 1)

            def stage_x(n):
                if not n.real():
                    return
                wait_apart(act, x_normed, n.t + 1)
                wait_apart(act, x_t_copied, n.t)
                nc.scalar.activation(x_now[:, :], X[:, n.t, :], ACT.Copy).then_inc(x_staged, 1)

            def inputs_copy(s, n, r):
                if n.real() or r.real():
                    act.wait_ge(turned_in, s.t + 2)
                if n.real():
                    wait(act, scores_done, 4 * (n.t - 1))
                    nc.scalar.activation(kv_t[n.slot][:, :, :].rearrange("p b k -> p (b k)"), kv_turn_ps,
                                         ACT.Copy).then_inc(kv_copied, 1)
                if r.real():
                    wait(act, hid_done, r.t - 1)
                    nc.scalar.activation(x_t[r.slot][:, :], x_turn_ps, ACT.Copy).then_inc(x_t_copied, 1)

            def q_copy(n, c):
                if not n.real():
                    return
                act.wait_ge(q_done, 4 * n.t + c + 1)
                wait(act, scores_done, 4 * (n.t - 1))
                nc.scalar.activation(q_t[n.slot][:, :, 4 * c:4 * c + 4, :].rearrange("p b h q -> p h b q"),
                                     q_ps.rearrange("p (h b q) -> p h b q", h=4, b=2), ACT.Copy).then_inc(q_copied, 1)

            def exps(n, u):
                if not n.real():
                    return
                act.wait_ge(top_done, 4 * n.t + u + 1)
                wait(act, turned, 4 * n.t + u - 1)
                wait(act, inv_done, 4 * n.t + u - 1)
                for i in range(4):
                    nc.scalar.activation(probs[u % 2][:, i, :], scores_ps[u % 2][:, i * P:(i + 1) * P], ACT.Exp,
                                         bias=ntop[u % 2][:, i:i + 1],
                                         accum_out=total[u % 2][:, i:i + 1]).then_inc(exp_done, 1)

            def turn_copy(n, u):
                if not n.real():
                    return
                act.wait_ge(turned, 4 * n.t + u + 1)
                wait(act, z_done, 4 * n.t + u - 1)
                nc.scalar.activation(probs_t[u % 2][:, :], turned_ps, ACT.Copy).then_inc(turned_copied, 1)

            def z_copy(n, u):
                if not n.real():
                    return
                b, half = u % 2, u // 2
                act.wait_ge(z_done, 4 * n.t + u + 1)
                wait(act, y_done, n.t - 1)
                nc.scalar.activation(z_t[n.slot][:, 8 * half:8 * half + 8, b, :],
                                     z_ps.rearrange("p (h q) -> p h q", h=8), ACT.Copy).then_inc(z_copied, 1)

            def gelu(n):
                if not n.real():
                    return
                act.wait_ge(hidden_step, EXP * (n.t + 1))
                wait(act, lout_done, EXP * n.t)
                wait(act, act_turned, n.t)
                nc.scalar.activation(act_h[:, :], hidden[:, :], ACT.Gelu).then_inc(gelu_done, 1)
                wait(act, table_back, n.t)
                nc.scalar.activation(spare[:, :], spare_in[:, :], ACT.Exp).then_inc(table_back, 1)

            def act_copy(n):
                if not n.real():
                    return
                act.wait_ge(act_turned, n.t + 1)
                wait(act, out_done, n.t)
                nc.scalar.activation(act_t[:, :, :].rearrange("p c k -> p (c k)"), act_turn_ps,
                                     ACT.Copy).then_inc(act_copied, 1)

            def step(s):
                z_copy(s, 3)
                kv_norm(s.at(2))
                result_norm(s.at(-5))
                exps(s.at(1), 1)
                out_norm(s.at(-1))
                stage_x(s.at(-1))
                turn_copy(s.at(1), 0)
                exps(s.at(1), 2)
                inputs_copy(s.at(1), s.at(2), s.at(-1))
                z_copy(s.at(1), 0)
                turn_copy(s.at(1), 1)
                q_copy(s.at(2), 0)
                exps(s.at(1), 3)
                q_copy(s.at(2), 1)
                gelu(s.at(-3))
                turn_copy(s.at(1), 2)
                z_copy(s.at(1), 1)
                q_copy(s.at(2), 2)
                act_copy(s.at(-3))
                exps(s.at(2), 0)
                z_copy(s.at(1), 2)
                turn_copy(s.at(1), 3)
                stage_x_lin(s.at(-2))
                q_copy(s.at(2), 3)
            steps(act, step, -3, PAIRS + 6, **LOOP)

        @block.gpsimd
        def _(pool):
            in_table = nc.gpsimd.to_reg(LAST - 1)

            def kv_scales(n):
                if not n.real():
                    return
                pool.wait_ge(kv_mv_done, 2 * (n.t + 1))
                wait(pool, kv_hat_done, 4 * n.t)
                nc.gpsimd.tensor_tensor(kv_eps[:, :], kv_mv[:, :, 1], eps_t[:, :], ALU.add).then_inc(kv_eps_done, 1)
                nc.gpsimd.tensor_tensor(kv_nmean[:, :], kv_mv[:, :, 0], mones[:, :], ALU.mult).then_inc(kv_nmean_done, 1)
                pool.wait_ge(kv_eps_done, n.t + 1)
                nc.gpsimd.tensor_tensor(kv_rstd[:, :], kv_eps[:, :], mhalf[:, :], ALU.pow).then_inc(kv_rstd_done, 1)
                pool.wait_ge(kv_nmean_done, n.t + 1)
                pool.wait_ge(kv_rstd_done, n.t + 1)
                nc.gpsimd.tensor_tensor(kv_shift[:, :], kv_nmean[:, :], kv_rstd[:, :], ALU.mult).then_inc(kv_shift_done, 1)

            def kv_affine(n):
                if not n.real():
                    return
                pool.wait_ge(kv_hat_done, 4 * (n.t + 1))
                wait(pool, z_done, 4 * (n.t - 1))
                wait(pool, turned_in, n.t)
                nc.gpsimd.tensor_tensor(kv[n.slot][:, :, :], kv_hat[:, :, :], kv_gb[:, 0, :, :],
                                        ALU.mult).then_inc(kv_gained, 1)
                pool.wait_ge(kv_gained, n.t + 1)
                nc.gpsimd.tensor_tensor(kv[n.slot][:, :, :], kv[n.slot][:, :, :], kv_gb[:, 1, :, :],
                                        ALU.add).then_inc(kv_done, 1)

            def out_scale(n, k):
                if not n.real():
                    return
                pool.wait_ge(o_mv_done, 2 * n.t + k + 1)
                if k:
                    wait(pool, x_normed, n.t)
                else:
                    wait(pool, o_resid_done, n.t)
                nc.gpsimd.tensor_tensor(o_eps[:, k:k + 1], o_mv[:, k, 1:2], eps_t[:, 0:1],
                                        ALU.add).then_inc(o_eps_done, 1)
                pool.wait_ge(o_eps_done, 2 * n.t + k + 1)
                nc.gpsimd.tensor_tensor(o_rstd[:, k:k + 1], o_eps[:, k:k + 1], mhalf[:, 0:1],
                                        ALU.pow).then_inc(o_rstd_done, 1)
                if k:
                    nc.gpsimd.tensor_tensor(o_nmean[:, :], o_mv[:, 1, 0:1], mones[:, 0:1],
                                            ALU.mult).then_inc(o_nmean_done, 1)
                    pool.wait_ge(o_nmean_done, n.t + 1)
                    pool.wait_ge(o_rstd_done, 2 * n.t + 2)
                    nc.gpsimd.tensor_tensor(o_shift[:, :], o_nmean[:, :], o_rstd[:, 1:2],
                                            ALU.mult).then_inc(o_shift_done, 1)

            def bias_x(n):
                if not n.real():
                    return
                wait_apart(pool, o_resid_done, n.t)
                nc.gpsimd.tensor_tensor(x_bias[:, :], X[:, n.t, :], gb[:, BO, :], ALU.add).then_inc(x_biased, 1)

            def scale(n, u):
                if not n.real():
                    return
                pool.wait_ge(exp_done, 4 * (4 * n.t + u + 1))
                pool.wait_ge(inv_done, 4 * n.t + u + 1)
                nc.gpsimd.tensor_tensor(
                    probs[u % 2][:, :, :], probs[u % 2][:, :, :],
                    inv[u % 2][:, :].rearrange("p (i k) -> p i k", k=1).broadcast_to([P, 4, P]),
                    ALU.mult).then_inc(scaled, 1)

            def gather(n, heads):
                if not n.real():
                    return
                if heads[0] == 0:
                    wait_apart(pool, index_done, n.t + 1)
                wait_apart(pool, resid_step, (EXP + 1) * (n.t - 2) + heads[-1] + 2)
                for h in heads:
                    nc.gpsimd.indirect_dma_start(
                        out=rows[n.slot][:, h, :], out_offset=None, in_=table,
                        in_offset=bass.IndirectOffsetOnAxis(ap=index[n.slot][:, h:h + 1], axis=0),
                        bounds_check=in_table, oob_is_err=False).then_inc(gathered[n.slot], 16)

            def result_scale(n):
                if not n.real():
                    return
                pool.wait_ge(e_mv_done, n.t + 1)
                wait(pool, result_done, n.t)
                nc.gpsimd.tensor_tensor(e_eps[:, :], e_mv[:, 1:2], eps_t[:, 0:1], ALU.add).then_inc(e_eps_done, 1)
                pool.wait_ge(e_eps_done, n.t + 1)
                nc.gpsimd.tensor_tensor(e_rstd[:, :], e_eps[:, :], mhalf[:, 0:1], ALU.pow).then_inc(e_rstd_done, 1)
                nc.gpsimd.tensor_tensor(e_nmean[:, :], e_mv[:, 0:1], mones[:, 0:1], ALU.mult).then_inc(e_nmean_done, 1)
                pool.wait_ge(e_nmean_done, n.t + 1)
                pool.wait_ge(e_rstd_done, n.t + 1)
                nc.gpsimd.tensor_tensor(e_shift[:, :], e_nmean[:, :], e_rstd[:, :], ALU.mult).then_inc(e_shift_done, 1)

            def step(s):
                result_scale(s.at(-7))
                scale(s.at(-1), 0)
                bias_x(s.at(-2))
                kv_affine(s)
                scale(s.at(-1), 1)
                out_scale(s.at(-2), 0)
                gather(s.at(-4), (0, 1, 2))
                scale(s.at(-1), 2)
                gather(s.at(-4), (3, 4, 5))
                scale(s.at(-1), 3)
                gather(s.at(-4), (6, 7))
                kv_scales(s.at(1))
                out_scale(s.at(-2), 1)
            steps(pool, step, -3, PAIRS + 6, **LOOP)

        @block.vector
        def _(dve):
            def tops(n, u):
                if not n.real():
                    return
                dve.wait_ge(scores_done, 4 * n.t + u + 1)
                wait(dve, exp_done, 4 * (4 * n.t + u - 1))
                nc.vector.tensor_reduce(ntop[u % 2][:, :], scores_ps[u % 2].rearrange("p (i k) -> p i k", i=4),
                                        AX_X, ALU.max, negate=True).then_inc(top_done, 1)

            def invert(n, u):
                if not n.real():
                    return
                dve.wait_ge(exp_done, 4 * (4 * n.t + u + 1))
                wait(dve, scaled, 4 * n.t + u - 1)
                nc.vector.reciprocal(inv[u % 2][:, :], total[u % 2][:, :]).then_inc(inv_done, 1)

            def kv_moments(n):
                if not n.real():
                    return
                dve.wait_ge(c_loaded[n.slot], 32 * (n.turn + 1))
                wait(dve, kv_mv_done, 2 * n.t)
                nc.vector.bn_stats(kv_stats[:, 0, :], X[:, n.t, :]).then_inc(kv_stats_done, 1)
                nc.vector.bn_stats(kv_stats[:, 1, :], c_row[n.slot][:, :]).then_inc(kv_stats_done, 1)

            def kv_moments_end(n):
                if not n.real():
                    return
                wait_apart(dve, kv_stats_done, 2 * n.t + 2)
                wait_apart(dve, kv_rstd_done, n.t)
                wait_apart(dve, kv_hat_done, 4 * n.t)
                for k in range(2):
                    nc.vector.bn_aggr(kv_mv[:, k, :], kv_stats[:, k, :]).then_inc(kv_mv_done, 1)

            def out_moments(n):
                if not n.real():
                    return
                dve.wait_ge(y_done, n.t + 1)
                wait(dve, o_mv_done, 2 * n.t)
                nc.vector.bn_stats(o_stats[:, 0, :], y_ps).then_inc(o_stats_done, 1)

            def out_gain(n):
                if not n.real():
                    return
                wait_apart(dve, o_stats_done, 2 * n.t + 1)
                wait_apart(dve, o_resid_done, n.t)
                nc.vector.bn_aggr(o_mv[:, 0, :], o_stats[:, 0, :]).then_inc(o_mv_done, 1)
                dve.wait_ge(o_mv_done, 2 * n.t + 1)
                nc.vector.scalar_tensor_tensor(o_row[:, :], y_ps, o_mv[:, 0, 0:1], gb[:, GO, :],
                                               ALU.subtract, ALU.mult).then_inc(y_read, 1)

            def out_add(n):
                if not n.real():
                    return
                dve.wait_ge(o_rstd_done, 2 * n.t + 1)
                dve.wait_ge(y_read, n.t + 1)
                dve.wait_ge(x_biased, n.t + 1)
                wait(dve, x_normed, n.t)
                nc.vector.scalar_tensor_tensor(o_resid[:, :], o_row[:, :], o_rstd[:, 0:1], x_bias[:, :],
                                               ALU.mult, ALU.add).then_inc(o_resid_done, 1)

            def out_moments_2(n):
                if not n.real():
                    return
                dve.wait_ge(o_resid_done, n.t + 1)
                nc.vector.bn_stats(o_stats[:, 1, :], o_resid[:, :]).then_inc(o_stats_done, 1)

            def out_aggregate_2(n):
                if not n.real():
                    return
                wait_apart(dve, o_stats_done, 2 * n.t + 2)
                nc.vector.bn_aggr(o_mv[:, 1, :], o_stats[:, 1, :]).then_inc(o_mv_done, 1)

            def sims_of(c):
                return sims_ps[c % 2].rearrange("p (h k) -> p h k", h=4)

            def row_best(n, c):
                if not n.real():
                    return
                dve.wait_ge(sims_done, 4 * n.t + c + 1)
                wait(dve, gate_sum_done, n.t)
                nc.vector.tensor_reduce(best_x[:, 4 * c:4 * c + 4], sims_of(c), AX_X, ALU.max).then_inc(best_done, 1)

            def row_hits(n, c):
                if not n.real():
                    return
                dve.wait_ge(best_done, 2 * n.t + c + 1)
                wait(dve, row_rev_done, n.t)
                nc.vector.tensor_tensor(row_hit[:, 4 * c:4 * c + 4, :], sims_of(c)[:, :, 0:XROWS],
                                        best_x[:, 4 * c:4 * c + 4].rearrange("p (h k) -> p h k", k=1)
                                        .broadcast_to([P, 4, XROWS]), ALU.is_equal).then_inc(sims_read, 1)

            def row_codes(n):
                if not n.real():
                    return
                dve.wait_ge(sims_read, 4 * n.t + 2)
                wait(dve, row_code_done, n.t)
                nc.vector.tensor_tensor(row_rev[:, :, :], row_hit[:, :, :],
                                        rev_row[:, :].rearrange("p (h k) -> p h k", h=1).broadcast_to([P, FH, XROWS]),
                                        ALU.mult).then_inc(row_rev_done, 1)

            def row_codes_end(n):
                if not n.real():
                    return
                dve.wait_ge(row_rev_done, n.t + 1)
                wait(dve, row_base_done, n.t)
                nc.vector.tensor_reduce(row_code[:, :], row_rev[:, :, :], AX_X, ALU.max).then_inc(row_code_done, 1)

            def key_tops(n, c):
                if not n.real():
                    return
                wait_apart(dve, sims_done, 4 * n.t + c + 1)
                wait_apart(dve, gate_sum_done, n.t)
                for h in range(4):
                    nc.vector.max(best_y[:, 4 * (c - 2) + h, :], sims_of(c)[:, h, :]).then_inc(tops_y_done, 1)

            def key_places(n, c):
                if not n.real():
                    return
                wait_apart(dve, tops_y_done, 8 * n.t + 4 * (c - 1))
                wait_apart(dve, index_done, n.t)
                for h in range(4):
                    i = 4 * (c - 2) + h
                    last = nc.vector.max_index(key_y[:, i, :], best_y[:, i, :], sims_of(c)[:, h, :])
                last.then_inc(sims_read, 1)

            def route_1(n):
                if not n.real():
                    return
                dve.wait_ge(row_code_done, n.t + 1)
                nc.vector.tensor_scalar(row_base[:, :], row_code[:, :], -float(KEYS), float(XROWS * KEYS),
                                        ALU.mult, ALU.add).then_inc(row_base_done, 1)
                dve.wait_ge(tops_y_done, 8 * (n.t + 1))
                nc.vector.tensor_tensor(gate_sum[:, :], best_x[:, :], best_y[:, :, 0], ALU.add).then_inc(gate_sum_done, 1)

            def route_2(n):
                if not n.real():
                    return
                dve.wait_ge(sims_read, 4 * (n.t + 1))
                dve.wait_ge(row_base_done, n.t + 1)
                wait(dve, gathered[n.slot], 16 * FH * n.turn)
                nc.vector.tensor_tensor(index[n.slot][:, :], row_base[:, :], key_y[:, :, 0], ALU.add).then_inc(index_done, 1)
                dve.wait_ge(gate_sum_done, n.t + 1)
                wait(dve, gate_done, 3 * n.t)
                nc.vector.tensor_scalar(gate_all[:, :], gate_sum[:, :], 0.0, None, ALU.max).then_inc(gate_all_done, 1)

            def route_3(n):
                if not n.real():
                    return
                dve.wait_ge(index_done, n.t + 1)
                dve.wait_ge(gate_all_done, n.t + 1)
                wait(dve, lout_g_done, n.t - 1)
                nc.vector.scalar_tensor_tensor(gate[n.slot][:, 0:FH], index[n.slot][:, :], float(LAST) - 0.5,
                                               gate_all[:, :], ALU.is_le, ALU.mult).then_inc(gate_done, 1)

            def route_4(n):
                if not n.real():
                    return
                dve.wait_ge(gate_done, 3 * n.t + 1)
                nc.vector.tensor_tensor(gate_out[:, :], gate_all[:, :], gate[n.slot][:, 0:FH],
                                        ALU.subtract).then_inc(gate_done, 1)

            def route_5(n):
                if not n.real():
                    return
                dve.wait_ge(gate_done, 3 * n.t + 2)
                nc.vector.tensor_reduce(gate[n.slot][:, FH:EXP], gate_out[:, :], AX_X, ALU.add).then_inc(gate_done, 1)

            def lin_last(n):
                if not n.real():
                    return
                dve.wait_ge(hid_done, n.t + 1)
                wait(dve, lin_g_done, n.t)
                nc.vector.tensor_copy(lin[:, FH:EXP], hid_ps[:, FFN:FFN + 1]).then_inc(lin_done, 1)

            def lins(n, heads):
                if not n.real():
                    return
                if heads[0] == 0:
                    dve.wait_ge(gathered[n.slot], 16 * FH * (n.turn + 1))
                    dve.wait_ge(x_lin_done, n.t + 1)
                    wait(dve, lout_done, EXP * n.t)
                for h in heads:
                    nc.vector.tensor_tensor_reduce(prod[:, h, 0:DIM], x_lin[:, :], rows[n.slot][:, h, A_IN:A_IN + DIM],
                                                   1.0, 0.0, ALU.mult, ALU.add, lin[:, h:h + 1]).then_inc(lin_done, 1)

            def lin_gates(n):
                if not n.real():
                    return
                dve.wait_ge(lin_done, EXP * (n.t + 1))
                dve.wait_ge(gate_done, 3 * (n.t + 1))
                wait(dve, hidden_step, EXP * n.t)
                nc.vector.tensor_tensor(lin_g[:, :], lin[:, :], gate[n.slot][:, :], ALU.mult).then_inc(lin_g_done, 1)

            def hidden_sum(n, h):
                if not n.real():
                    return
                if h == 0:
                    dve.wait_ge(lin_g_done, n.t + 1)
                    wait(dve, gelu_done, n.t)
                else:
                    dve.wait_ge(hidden_step, EXP * n.t + h)
                weights = rows[n.slot][:, h, B_IN:B_IN + FFN] if h < FH else last_row[:, B_IN:B_IN + FFN]
                nc.vector.scalar_tensor_tensor(hidden[:, :], weights, lin_g[:, h:h + 1],
                                               hidden[:, :] if h else hid_ps[:, 0:FFN],
                                               ALU.mult, ALU.add).then_inc(hidden_step, 1)

            def louts(n, experts):
                if not n.real():
                    return
                if experts[0] == 0:
                    dve.wait_ge(gelu_done, n.t + 1)
                    wait(dve, lout_g_done, n.t)
                    wait(dve, lin_done, EXP * (n.t + 1))
                for h in experts:
                    nc.vector.tensor_tensor_reduce(prod[:, h, :], act_h[:, :], rows[n.slot][:, h, A_OUT:A_OUT + FFN],
                                                   1.0, 0.0, ALU.mult, ALU.add, lout[:, h:h + 1]).then_inc(lout_done, 1)

            def lout_last(n):
                if not n.real():
                    return
                dve.wait_ge(out_done, n.t + 1)
                wait(dve, lout_g_done, n.t)
                nc.vector.tensor_copy(lout[:, FH:EXP], out_ps[:, DIM:DIM + 1]).then_inc(lout_done, 1)

            def lout_gates(n):
                if not n.real():
                    return
                dve.wait_ge(lout_done, EXP * (n.t + 1))
                wait(dve, resid_step, (EXP + 1) * n.t)
                nc.vector.tensor_tensor(lout_g[:, :], lout[:, :], gate[n.slot][:, :], ALU.mult).then_inc(lout_g_done, 1)

            def resid_start(n):
                if not n.real():
                    return
                dve.wait_ge(out_done, n.t + 1)
                wait(dve, result_done, n.t - 1)
                nc.vector.tensor_tensor(e_resid[n.slot][:, :], x_lin[:, :], out_ps[:, 0:DIM], ALU.add).then_inc(resid_step, 1)

            def resid_sum(n, h):
                if not n.real():
                    return
                if h == 0:
                    dve.wait_ge(lout_g_done, n.t + 1)
                dve.wait_ge(resid_step, (EXP + 1) * n.t + 1 + h)
                weights = rows[n.slot][:, h, B_OUT:B_OUT + DIM] if h < FH else last_row[:, B_OUT:B_OUT + DIM]
                nc.vector.scalar_tensor_tensor(e_resid[n.slot][:, :], weights, lout_g[:, h:h + 1], e_resid[n.slot][:, :],
                                               ALU.mult, ALU.add).then_inc(resid_step, 1)

            def result_moments(n):
                if not n.real():
                    return
                dve.wait_ge(resid_step, (EXP + 1) * (n.t + 1))
                wait(dve, e_mv_done, n.t)
                nc.vector.bn_stats(e_stats[:, :], e_resid[n.slot][:, :]).then_inc(e_stats_done, 1)

            def result_aggregate(n):
                if not n.real():
                    return
                wait_apart(dve, e_stats_done, n.t + 1)
                wait_apart(dve, result_done, n.t)
                nc.vector.bn_aggr(e_mv[:, :], e_stats[:, :]).then_inc(e_mv_done, 1)

            def step(s):
                key_tops(s.at(-3), 2)
                result_moments(s.at(-6))
                kv_moments_end(s.at(1))
                invert(s.at(-1), 3)
                louts(s.at(-5), (0, 1))
                louts(s.at(-5), (2, 3))
                louts(s.at(-5), (4, 5))
                tops(s, 0)
                louts(s.at(-5), (6, 7))
                key_tops(s.at(-3), 3)
                key_places(s.at(-3), 2)
                route_4(s.at(-4))
                row_codes(s.at(-3))
                lout_last(s.at(-5))
                resid_start(s.at(-5))
                lout_gates(s.at(-5))
                invert(s, 0)
                route_5(s.at(-4))
                result_aggregate(s.at(-6))
                resid_sum(s.at(-5), 0)
                row_codes_end(s.at(-3))
                resid_sum(s.at(-5), 1)
                key_places(s.at(-3), 3)
                lins(s.at(-4), (0, 1, 2))
                lins(s.at(-4), (3, 4))
                tops(s, 1)
                lins(s.at(-4), (5, ))
                lins(s.at(-4), (6, ))
                lins(s.at(-4), (7, ))
                lin_last(s.at(-4))
                resid_sum(s.at(-5), 2)
                lin_gates(s.at(-4))
                route_1(s.at(-3))
                hidden_sum(s.at(-4), 0)
                route_2(s.at(-3))
                hidden_sum(s.at(-4), 1)
                tops(s, 2)
                invert(s, 1)
                resid_sum(s.at(-5), 3)
                out_moments(s.at(-1))
                hidden_sum(s.at(-4), 2)
                out_gain(s.at(-1))
                resid_sum(s.at(-5), 4)
                hidden_sum(s.at(-4), 3)
                resid_sum(s.at(-5), 5)
                tops(s, 3)
                hidden_sum(s.at(-4), 4)
                out_add(s.at(-1))
                route_3(s.at(-3))
                resid_sum(s.at(-5), 6)
                hidden_sum(s.at(-4), 5)
                kv_moments(s.at(2))
                resid_sum(s.at(-5), 7)
                hidden_sum(s.at(-4), 6)
                invert(s, 2)
                row_best(s.at(-2), 0)
                out_moments_2(s.at(-1))
                hidden_sum(s.at(-4), 7)
                out_aggregate_2(s.at(-1))
                row_hits(s.at(-2), 0)
                hidden_sum(s.at(-4), 8)
                row_best(s.at(-2), 1)
                resid_sum(s.at(-5), 8)
                row_hits(s.at(-2), 1)
            steps(dve, step, -3, PAIRS + 6, **LOOP)


def kernel(**inputs):
    import numpy as np
    import concourse.bacc as bacc
    from concourse.bass_utils import run_bass_kernel_spmd

    a = {k: np.asarray(v) for k, v in inputs.items()}

    def cat(*names, axis=-1):
        return np.concatenate([a[n] for n in names], axis=axis)

    def turned(m):
        return np.ascontiguousarray(m.T)

    def with_columns(m, v):
        return np.concatenate([m, v[:, None], v[:, None]], axis=1)

    wkv = a["L0_xattn_Wkv"]
    host = {
        "x": a["x"].reshape(BATCH * SEQ, DIM),
        "xT": turned(a["x"].reshape(BATCH * SEQ, DIM)),
        "ctx": a["ctx_1024"].reshape(BATCH * SEQ, DIM),
        "mask": a["mask_BxS2_bf1"].view(np.uint8),
        "w_attn": cat("L0_attn_W_qkv", "L0_attn_W_proj"),
        "u_attn": cat("L0_attn_u_qkv", "L0_attn_u_proj"),
        "sig_qkv": a["L0_attn_sigma_qkv"],
        "sig_proj": a["L0_attn_sigma_proj"],
        "gains": cat("L0_xattn_g_x", "L0_xattn_b_x", "L0_xattn_g_l", "L0_xattn_b_l", "L0_xattn_g_o", "L0_xattn_b_o"),
        "wq_t": turned(a["L0_xattn_Wq"]),
        "wk_t": turned(wkv[:, :INNER]),
        "wv_t": turned(wkv[:, INNER:]),
        "wout": a["L0_xattn_Wout"],
        "ffn_wq": a["L0_ffn_Wq"],
        "keys_t": a["L0_ffn_keys"].transpose(2, 0, 3, 1).reshape(2 * FH * XH, KEYS),
        "w_in_last": with_columns(turned(a["L0_ffn_W_in"]), a["L0_ffn_in_a"][LAST]),
        "w_out_last": with_columns(turned(a["L0_ffn_W_out"]), a["L0_ffn_out_a"][LAST]),
        "table": cat("L0_ffn_in_a", "L0_ffn_in_b", "L0_ffn_out_a", "L0_ffn_out_b"),
    }
    nc = bacc.Bacc("TRN2", target_bir_lowering=False, num_devices=1)
    arrays, args = {}, []
    for name, value in host.items():
        value = np.ascontiguousarray(value)
        arrays[f"in_{name}"] = value
        args.append(nc.dram_tensor(f"in_{name}", value.shape, mybir.dt.from_np(value.dtype), kind="ExternalInput").ap())
    out = nc.dram_tensor("result", (BATCH * SEQ, DIM), F32, kind="ExternalOutput").ap()
    decoder_layer(nc, *args, out)
    r = run_bass_kernel_spmd(nc, [arrays], core_ids=[0])
    return r.results[0]["result"].reshape(BATCH, SEQ, DIM)
```
